# Optimizing a Trainium2 kernel written in Bass

```python
import numpy as np
import jax
import jax.numpy as jnp

def _softmax(x, axis=-1):
    return jax.nn.softmax(x, axis=axis)

def _gelu(x):
    return jax.nn.gelu(x, approximate=True)

def _silu(x):
    return jax.nn.silu(x)

def _sigmoid(x):
    return jax.nn.sigmoid(x)

def _layernorm(x, axis=-1, eps=1e-05):
    m = jnp.mean(x, axis=axis, keepdims=True)
    v = jnp.var(x, axis=axis, keepdims=True)
    return (x - m) / jnp.sqrt(v + eps)

def _scatter_add(tgt, idx, src, axis=0):
    return tgt.at[idx].add(src)

def _segment_sum(src, seg, n):
    return jax.ops.segment_sum(src, seg, n)
kernel_name = 'mk_recurrent_d2_jaxref_r4_be57a7'

def setup_inputs(seed: int=0):
    np.random.seed(seed)
    _w = jnp.asarray

    def _L0_attn_setup():
        import math
        import jax, jax.numpy as jnp
        import numpy as np
        N_HEADS = 16
        CHUNK = 64

        def _chunked_causal_attention(q, k, v, chunk=CHUNK):
            B, H, S, D = q.shape
            scale = 1.0 / math.sqrt(D)
            nc = S // chunk
            qc = jnp.moveaxis(q.reshape(B, H, nc, chunk, D), 2, 0)
            kpos = jnp.arange(S)

            def body(_, inp):
                qi, ci = inp
                scores = jnp.einsum('bhcd,bhsd->bhcs', qi, k) * scale
                qpos = ci * chunk + jnp.arange(chunk)
                mask = kpos[None, :] <= qpos[:, None]
                scores = jnp.where(mask, scores, jnp.finfo(scores.dtype).min)
                p = jax.nn.softmax(scores, axis=-1)
                return (None, jnp.einsum('bhcs,bhsd->bhcd', p, v))
            _, outs = jax.lax.scan(body, None, (qc, jnp.arange(nc)))
            return jnp.moveaxis(outs, 0, 2).reshape(B, H, S, D)
        key = jax.random.key(seed)
        kx, kq, kk, kv, ko = jax.random.split(key, 5)
        d = 256
        x = jax.random.normal(kx, (1, 1024, d), dtype=jnp.float32)
        Wq = jax.random.normal(kq, (d, d), dtype=jnp.float32) * 0.02
        Wk = jax.random.normal(kk, (d, d), dtype=jnp.float32) * 0.02
        Wv = jax.random.normal(kv, (d, d), dtype=jnp.float32) * 0.02
        Wo = jax.random.normal(ko, (d, d), dtype=jnp.float32) * 0.02
        return {'x': x, 'Wq': Wq, 'Wk': Wk, 'Wv': Wv, 'Wo': Wo}
    _L0_attn_in = _L0_attn_setup()

    def _L0_ffn_setup():
        import jax, jax.numpy as jnp
        import numpy as np
        NUM_EXPERTS = 8
        CAPACITY_FACTOR = 1.0
        key = jax.random.key(seed)
        k1, k2, k3, k4 = jax.random.split(key, 4)
        B, S, D, E, F = (8, 512, 256, NUM_EXPERTS, 1024)
        x = jax.random.normal(k1, (B, S, D), dtype=jnp.float32)
        router_w = jax.random.normal(k2, (D, E), dtype=jnp.float32) * D ** (-0.5)
        w1 = jax.random.normal(k3, (E, D, F), dtype=jnp.float32) * D ** (-0.5)
        w2 = jax.random.normal(k4, (E, F, D), dtype=jnp.float32) * F ** (-0.5)
        return {'x': x, 'router_w': router_w, 'w1': w1, 'w2': w2}
    _L0_ffn_in = _L0_ffn_setup()

    def _L1_attn_setup():
        import jax, jax.numpy as jnp
        import numpy as np
        HEADS = 16
        DIM_HEAD = 64
        WINDOW = 128
        LOOK_BACKWARD = 1
        LOOK_FORWARD = 0
        THETA = 10000.0
        PAD_VALUE = -1

        def look_around(x, backward, forward, pad_value, axis):
            w = x.shape[axis]
            size = backward + forward + 1
            pads = [(0, 0)] * x.ndim
            pads[axis] = (backward, forward)
            p = jnp.pad(x, pads, constant_values=pad_value)
            segs = [jax.lax.slice_in_dim(p, s, s + w, axis=axis) for s in range(size)]
            return jnp.concatenate(segs, axis=axis + 1)

        def rotate_half(t):
            t1, t2 = jnp.split(t, 2, axis=-1)
            return jnp.concatenate([-t2, t1], axis=-1)
        key = jax.random.key(seed)
        k1, k2, k3 = jax.random.split(key, 3)
        dim = 256
        x = jax.random.normal(k1, (4, 1024, dim), dtype=jnp.float32)
        W_qkv = jax.random.normal(k2, (dim, 3 * HEADS * DIM_HEAD), dtype=jnp.float32) * dim ** (-0.5)
        W_out = jax.random.normal(k3, (HEADS * DIM_HEAD, dim), dtype=jnp.float32) * (HEADS * DIM_HEAD) ** (-0.5)
        return {'x': x, 'W_qkv': W_qkv, 'W_out': W_out}
    _L1_attn_in = _L1_attn_setup()

    def _L1_ffn_setup():
        import jax, jax.numpy as jnp
        import numpy as np
        B, T, D, E, TOP_K = (4, 1024, 256, 8, 2)
        CAPACITY_FACTOR = 1.5
        key = jax.random.key(seed)
        k1, k2, k3 = jax.random.split(key, 3)
        x = jax.random.normal(k1, (B, T, D), dtype=jnp.float32)
        Wr = jax.random.normal(k2, (E, D), dtype=jnp.float32) * 0.02
        We = jax.random.normal(k3, (E, D, D), dtype=jnp.float32) * 0.02
        return {'x': x, 'Wr': Wr, 'We': We}
    _L1_ffn_in = _L1_ffn_setup()
    _d = {'L0_attn_x': _L0_attn_in['x'], 'L0_attn_Wq': _L0_attn_in['Wq'], 'L0_attn_Wk': _L0_attn_in['Wk'], 'L0_attn_Wv': _L0_attn_in['Wv'], 'L0_attn_Wo': _L0_attn_in['Wo'], 'L0_ffn_router_w': _L0_ffn_in['router_w'], 'L0_ffn_w1': _L0_ffn_in['w1'], 'L0_ffn_w2': _L0_ffn_in['w2'], 'L1_attn_W_qkv': _L1_attn_in['W_qkv'], 'L1_attn_W_out': _L1_attn_in['W_out'], 'L1_ffn_Wr': _L1_ffn_in['Wr'], 'L1_ffn_We': _L1_ffn_in['We']}
    _x0 = _d['L0_attn_x']
    _d['L0_attn_x'] = jax.random.normal(jax.random.fold_in(jax.random.key(seed), 1), (2, 2048, 256), dtype=_x0.dtype)
    del _x0
    return _d

def reference(L0_attn_x, L0_attn_Wq, L0_attn_Wk, L0_attn_Wv, L0_attn_Wo, L0_ffn_router_w, L0_ffn_w1, L0_ffn_w2, L1_attn_W_qkv, L1_attn_W_out, L1_ffn_Wr, L1_ffn_We):

    def _L0_attn_ref(x, Wq, Wk, Wv, Wo):
        import math
        import jax, jax.numpy as jnp
        import numpy as np
        N_HEADS = 16
        CHUNK = 64

        def _chunked_causal_attention(q, k, v, chunk=CHUNK):
            B, H, S, D = q.shape
            scale = 1.0 / math.sqrt(D)
            nc = S // chunk
            qc = jnp.moveaxis(q.reshape(B, H, nc, chunk, D), 2, 0)
            kpos = jnp.arange(S)

            def body(_, inp):
                qi, ci = inp
                scores = jnp.einsum('bhcd,bhsd->bhcs', qi, k) * scale
                qpos = ci * chunk + jnp.arange(chunk)
                mask = kpos[None, :] <= qpos[:, None]
                scores = jnp.where(mask, scores, jnp.finfo(scores.dtype).min)
                p = jax.nn.softmax(scores, axis=-1)
                return (None, jnp.einsum('bhcs,bhsd->bhcd', p, v))
            _, outs = jax.lax.scan(body, None, (qc, jnp.arange(nc)))
            return jnp.moveaxis(outs, 0, 2).reshape(B, H, S, D)
        B, S, D = x.shape
        H = N_HEADS
        hd = D // H
        q = (x @ Wq.T).reshape(B, S, H, hd).transpose(0, 2, 1, 3)
        k = (x @ Wk.T).reshape(B, S, H, hd).transpose(0, 2, 1, 3)
        v = (x @ Wv.T).reshape(B, S, H, hd).transpose(0, 2, 1, 3)
        out = _chunked_causal_attention(q, k, v)
        out = out.transpose(0, 2, 1, 3).reshape(B, S, D)
        return out @ Wo.T

    def _L0_ffn_ref(x, router_w, w1, w2):
        import jax, jax.numpy as jnp
        import numpy as np
        NUM_EXPERTS = 8
        CAPACITY_FACTOR = 1.0
        B, S, D = x.shape
        E = router_w.shape[1]
        T = B * S
        C = int(CAPACITY_FACTOR * T / E)
        x_flat = x.reshape(T, D)
        logits = x_flat @ router_w
        probs = jax.nn.softmax(logits, axis=-1)
        expert_idx = jnp.argmax(probs, axis=-1)
        gate = jnp.take_along_axis(probs, expert_idx[:, None], axis=1)[:, 0]
        onehot = jax.nn.one_hot(expert_idx, E, dtype=jnp.float32)
        pos_all = jnp.cumsum(onehot, axis=0) - 1.0
        pos = jnp.take_along_axis(pos_all, expert_idx[:, None], axis=1)[:, 0]
        pos = pos.astype(jnp.int32)
        keep = (pos < C).astype(x_flat.dtype)
        pos_c = jnp.clip(pos, 0, C - 1)
        expert_in = jnp.zeros((E, C, D), dtype=x_flat.dtype)
        expert_in = expert_in.at[expert_idx, pos_c].add(x_flat * keep[:, None])
        hidden = jax.nn.gelu(jnp.einsum('ecd,edf->ecf', expert_in, w1))
        expert_out = jnp.einsum('ecf,efd->ecd', hidden, w2)
        y = expert_out[expert_idx, pos_c] * (gate * keep)[:, None]
        return y.reshape(B, S, D)

    def _L1_attn_ref(x, W_qkv, W_out):
        import jax, jax.numpy as jnp
        import numpy as np
        HEADS = 16
        DIM_HEAD = 64
        WINDOW = 128
        LOOK_BACKWARD = 1
        LOOK_FORWARD = 0
        THETA = 10000.0
        PAD_VALUE = -1

        def look_around(x, backward, forward, pad_value, axis):
            w = x.shape[axis]
            size = backward + forward + 1
            pads = [(0, 0)] * x.ndim
            pads[axis] = (backward, forward)
            p = jnp.pad(x, pads, constant_values=pad_value)
            segs = [jax.lax.slice_in_dim(p, s, s + w, axis=axis) for s in range(size)]
            return jnp.concatenate(segs, axis=axis + 1)

        def rotate_half(t):
            t1, t2 = jnp.split(t, 2, axis=-1)
            return jnp.concatenate([-t2, t1], axis=-1)
        b, n, dim = x.shape
        h, dh, ws = (HEADS, DIM_HEAD, WINDOW)
        w = n // ws
        j = ws * (LOOK_BACKWARD + LOOK_FORWARD + 1)
        qkv = x @ W_qkv
        q, k, v = jnp.split(qkv, 3, axis=-1)

        def to_bhwnd(t):
            return t.reshape(b, n, h, dh).transpose(0, 2, 1, 3).reshape(b, h, w, ws, dh)
        bq = to_bhwnd(q) * dh ** (-0.5)
        bk = look_around(to_bhwnd(k), LOOK_BACKWARD, LOOK_FORWARD, float(PAD_VALUE), axis=2)
        bv = look_around(to_bhwnd(v), LOOK_BACKWARD, LOOK_FORWARD, float(PAD_VALUE), axis=2)
        inv_freq = 1.0 / THETA ** (jnp.arange(0, dh, 2, dtype=jnp.float32) / dh)
        t_pos = jnp.arange(j, dtype=jnp.float32)
        freqs = t_pos[:, None] * inv_freq[None, :]
        freqs = jnp.concatenate([freqs, freqs], axis=-1)
        q_freqs = freqs[-ws:]
        bq = bq * jnp.cos(q_freqs) + rotate_half(bq) * jnp.sin(q_freqs)
        bk = bk * jnp.cos(freqs) + rotate_half(bk) * jnp.sin(freqs)
        sim = jnp.einsum('bhwid,bhwjd->bhwij', bq, bk)
        seq = jnp.arange(n).reshape(w, ws)
        bq_t = seq[:, :, None]
        bq_k = look_around(seq[None], LOOK_BACKWARD, LOOK_FORWARD, PAD_VALUE, axis=1)[0]
        bq_k = bq_k[:, None, :]
        pad_mask = bq_k == PAD_VALUE
        causal_mask = (bq_t < bq_k) | (bq_t > bq_k + ws * LOOK_BACKWARD)
        mask = causal_mask | pad_mask
        mask_value = -jnp.finfo(sim.dtype).max
        sim = jnp.where(mask, mask_value, sim)
        attn = jax.nn.softmax(sim, axis=-1)
        out = jnp.einsum('bhwij,bhwjd->bhwid', attn, bv)
        out = out.reshape(b, h, n, dh).transpose(0, 2, 1, 3).reshape(b, n, h * dh)
        return out @ W_out

    def _L1_ffn_ref(x, Wr, We):
        import jax, jax.numpy as jnp
        import numpy as np
        B, T, D, E, TOP_K = (4, 1024, 256, 8, 2)
        CAPACITY_FACTOR = 1.5
        Bb, Tt, Dd = x.shape
        Ee = Wr.shape[0]
        K = TOP_K
        C = int(Tt * K / Ee * CAPACITY_FACTOR) + 1
        logits = jnp.einsum('btd,ed->bte', x, Wr)
        top_vals, top_idx = jax.lax.top_k(logits, K)
        w = jax.nn.softmax(top_vals, axis=-1)
        flat_e = top_idx.reshape(Bb, Tt * K)
        oh = jax.nn.one_hot(flat_e, Ee, dtype=jnp.int32)
        pos_all = jnp.cumsum(oh, axis=1) - oh
        pos = jnp.take_along_axis(pos_all, flat_e[..., None], axis=-1)[..., 0]
        keep = pos < C
        b_idx = jnp.arange(Bb, dtype=jnp.int32)[:, None]
        dst = (b_idx * Ee + flat_e) * C + pos
        dst = jnp.where(keep, dst, Bb * Ee * C).reshape(-1)
        x_rep = jnp.repeat(x, K, axis=1).reshape(-1, Dd)
        buf = jnp.zeros((Bb * Ee * C, Dd), dtype=x.dtype).at[dst].add(x_rep, mode='drop')
        expert_in = buf.reshape(Bb, Ee, C, Dd)
        expert_out = jnp.einsum('becd,edf->becf', expert_in, We)
        gathered = jnp.take(expert_out.reshape(Bb * Ee * C, Dd), dst, axis=0, mode='fill', fill_value=0.0)
        gathered = gathered.reshape(Bb, Tt, K, Dd)
        out = jnp.einsum('btk,btkd->btd', w, gathered)
        return out
    x = L0_attn_x
    xn = _layernorm(x, axis=-1)
    s = _L0_attn_ref(xn, L0_attn_Wq, L0_attn_Wk, L0_attn_Wv, L0_attn_Wo)
    g = _silu(_L0_ffn_ref(xn, L0_ffn_router_w, L0_ffn_w1, L0_ffn_w2))
    x = x + s * g
    xn = _layernorm(x, axis=-1)
    s = _L1_attn_ref(xn, L1_attn_W_qkv, L1_attn_W_out)
    g = _silu(_L1_ffn_ref(xn, L1_ffn_Wr, L1_ffn_We))
    x = x + s * g
    return x

_drawn_inputs = setup_inputs


def setup_inputs(seed=0):
    import zlib

    import numpy as np

    out = dict(_drawn_inputs(seed))
    spreads = {}
    factors = {'L0_attn_Wq': 8.0,
     'L0_attn_Wk': 8.0,
     'L0_attn_Wv': 8.0,
     'L0_attn_Wo': 8.0,
     'L0_ffn_router_w': 8.0,
     'L0_ffn_w1': 8.0,
     'L0_ffn_w2': 8.0,
     'L1_attn_W_qkv': 3.024,
     'L1_attn_W_out': 3.018,
     'L1_ffn_Wr': 9.744,
     'L1_ffn_We': 3.036}
    for name, (base, spread) in spreads.items():
        noise = np.random.default_rng([zlib.crc32(name.encode()), seed]).standard_normal(out[name].shape)
        drawn = base * np.exp(spread * noise) if base else spread * noise
        out[name] = jnp.asarray(drawn.astype(out[name].dtype))
    for name, factor in factors.items():
        out[name] = (out[name] * factor).astype(out[name].dtype)
    return out
```

```python
from contextlib import ExitStack

import concourse.bass as bass
from concourse import mybir

F32 = mybir.dt.float32
BF16 = mybir.dt.bfloat16
U32 = mybir.dt.uint32
ALU = mybir.AluOpType
ACT = mybir.ActivationFunctionType
X = mybir.AxisListType.X

P = 128
B, S, D = 2, 2048, 256
T = B * S
NT = T // P
CH = 512
TC = CH // P
NC = T // CH
KD = D // P
E = 8
H = 16
EPS = 1e-5
NEG = -1e30

HD = D // H
F = 1024
FT = F // P
CAP0 = T // E
SKIP = 8192.0
GH = 4
HG = H // GH
KT = S // P
QC = S // CH
QR = 6 * HD
MR = QR + 3

DH = 64
J = H * DH
CAP1 = int(S * 2 / E * 1.5) + 1


def wait(eng, sem, value):
    if isinstance(value, int) and value <= 0:
        return
    eng.wait_ge(sem, value)


def rounds(eng, n):
    yield 0
    with eng.Fori(1, n) as i:
        yield i


def snap(eng, value):
    return value if isinstance(value, int) else eng.snap(value)


class Chain:

    def __init__(self, eng, sem, per_round=0):
        self.eng, self.sem, self.per, self.base, self.k = eng, sem, per_round, 0, 0

    def round(self, i):
        assert self.k in (0, self.per), self.k
        self.base, self.k = i * self.per, 0

    def after(self, n):
        assert self.k == self.per, self.k
        self.base, self.k = n * self.per, 0

    def link(self, ins):
        self.k += 1
        ins.then_inc(self.sem, 1)
        self.eng.wait_ge(self.sem, self.base + self.k)


class Stage:

    def __init__(self, nc, ctx, prefix=""):
        self.nc, self.ctx, self.prefix = nc, ctx, prefix

    def sb(self, name, shape, dt=F32):
        return self.ctx.enter_context(self.nc.sbuf_tensor(self.prefix + name, shape, dt))

    def ps(self, name, shape, dt=F32):
        return self.ctx.enter_context(self.nc.psum_tensor(self.prefix + name, shape, dt))

    def sem(self, name):
        return self.ctx.enter_context(self.nc.semaphore(self.prefix + name))


def build_constants(nc, keep):
    with ExitStack() as ctx:
        st = Stage(nc, ctx, "c_")
        pool_step = st.sem("const_step")
        block = ctx.enter_context(nc.Block())

        @block.gpsimd
        def _(pool):
            ch = Chain(pool, pool_step)
            ch.link(pool.memset(keep["identity"][:, :], 0.0))
            ch.link(pool.affine_select(out=keep["identity"][:, :], in_=keep["identity"][:, :], compare_op=ALU.not_equal,
                                       fill=1.0, base=0, pattern=[[-1, P]], channel_multiplier=1))
            ch.link(pool.tensor_copy(keep["identity16"][:, :], keep["identity"][:, :]))
            ch.link(pool.memset(keep["ones16"][:, :], 1.0))
            ch.link(pool.affine_select(out=keep["before16"][:, :], in_=keep["ones16"][:, :], compare_op=ALU.is_gt,
                                       fill=0.0, base=0, pattern=[[1, P]], channel_multiplier=-1))
            ch.link(pool.memset(keep["zero16"][:, :], 0.0))
            ch.link(pool.affine_select(out=keep["mask_qk"][:, :], in_=keep["zero16"][:, :], compare_op=ALU.is_ge,
                                       fill=NEG, base=0, pattern=[[-1, P]], channel_multiplier=1))
            ch.link(pool.affine_select(out=keep["mask_kq"][:, :], in_=keep["zero16"][:, :], compare_op=ALU.is_ge,
                                       fill=NEG, base=0, pattern=[[1, P]], channel_multiplier=-1))
            ch.link(pool.iota(keep["expert"][:, :, :], pattern=[[1, E], [0, NT]], base=0, channel_multiplier=0,
                              allow_small_or_imprecise_dtypes=True))
            ch.link(pool.iota(keep["expert8"][:, :, :], pattern=[[1, E], [0, NT]], base=E, channel_multiplier=0,
                              allow_small_or_imprecise_dtypes=True))
            for name, span in (("running0", NT), ("running1", NT // B)):
                ch.link(pool.memset(keep[name][:, :, :], 1.0))
                v = keep[name][:, :, :].rearrange("p e (b t) -> p (e b) t", t=span)
                ch.link(pool.memset(v[:, :, 0:1], 0.0))


def first_max(vec, ch, keep, logits, out_max, equal, first, onehot):
    ch.link(vec.tensor_reduce(out_max, logits.rearrange("p e t -> p t e"), X, ALU.max))
    ch.link(vec.tensor_tensor(equal, logits, out_max.unsqueeze(1).to_broadcast([P, E, NT]), ALU.is_equal))
    ch.link(vec.scalar_tensor_tensor(out=equal, in0=equal, scalar=-float(E), in1=keep["expert8"][:, :, :],
                                     op0=ALU.mult, op1=ALU.add))
    ch.link(vec.tensor_reduce(first, equal.rearrange("p e t -> p t e"), X, ALU.min))
    ch.link(vec.tensor_tensor(onehot, keep["expert"][:, :, :], first.unsqueeze(1).to_broadcast([P, E, NT]), ALU.is_equal))


def places(vec, ch, keep, running, tile_before, tile_total, total, scanned, place):
    flat = "p e t -> p (e t)"
    ch.link(vec.tensor_copy(total, tile_total.rearrange("p (e t) -> p e t", e=E)))
    ch.link(vec.tensor_tensor_scan(scanned.rearrange(flat), keep[running][:, :, :].rearrange(flat), total.rearrange(flat),
                                   0.0, ALU.mult, ALU.add))
    ch.link(vec.tensor_tensor(scanned, scanned, total, ALU.subtract))
    ch.link(vec.tensor_tensor(place, scanned, tile_before.rearrange("p (e t) -> p e t", e=E), ALU.add))


def stage_project(nc, io, keep, dram):
    with ExitStack() as ctx:
        st = Stage(nc, ctx, "p_")
        wqk = st.sb("wqk", [P, 2, KD, D])
        wvr = st.sb("wvr", [P, KD, D + E])
        xin = st.sb("xin", [P, 2, TC, D])
        stats = st.sb("stats", [P, 2, TC, 6])
        mv = st.sb("mv", [P, 2, TC, 2])
        std = st.sb("std", [P, 2, TC])
        rstd = st.sb("rstd", [P, 2, TC])
        xn = st.sb("xn", [P, 2, TC, D])
        xnt = st.sb("xnt", [P, 2, KD, CH])
        rest = st.sb("rest", [P, 4, CH])
        parts = st.sb("parts", [P, 4, 3, CH], BF16)
        vout = st.sb("vout", [P, 2, TC, D])
        eps = st.sb("eps", [P, 1])
        spare = st.sb("spare", [P, 1])
        logits = st.sb("logits", [P, E, NT])
        top = st.sb("top", [P, NT])
        equal = st.sb("equal", [P, E, NT])
        first = st.sb("first", [P, NT])
        onehot = st.sb("onehot", [P, E, NT])
        onehot16 = st.sb("onehot16", [P, E, NT], BF16)
        shifted = st.sb("shifted", [P, E, NT])
        expd = st.sb("expd", [P, E, NT])
        total = st.sb("total", [P, E, NT])
        scanned = st.sb("scanned", [P, E, NT])
        place = st.sb("place", [P, E, NT])
        small = st.sb("small", [P, 6, NT])
        pst = [st.ps(f"pst{k}", [P, CH]) for k in range(KD)]
        psq = [st.ps(f"psq{k}", [P, CH]) for k in range(4)]
        psv = [st.ps(f"psv{k}", [P, CH]) for k in range(2)]

        weights_landed = st.sem("weights_landed")
        x_landed = [st.sem(f"x_landed{u}") for u in range(2)]
        mv_ready, std_ready, xn_ready = st.sem("mv_ready"), st.sem("std_ready"), st.sem("xn_ready")
        turned, xnt_ready, xn_kept = st.sem("turned"), st.sem("xnt_ready"), st.sem("xn_kept")
        qk_ready, first_part, parts_ready = st.sem("qk_ready"), st.sem("first_part"), st.sem("parts_ready")
        parts_stored = [st.sem(f"parts_stored{k}") for k in range(4)]
        v_ready, v_copied = st.sem("v_ready"), st.sem("v_copied")
        v_stored = [st.sem(f"v_stored{u}") for u in range(2)]
        dve_step = st.sem("dve_step")
        zeroed = st.sem("zeroed")
        eps_set = st.sem("eps_set")
        onehot_ready, counted, shifted_ready, exp_ready = (st.sem("onehot_ready"), st.sem("counted"),
                                                           st.sem("shifted_ready"), st.sem("exp_ready"))
        block = ctx.enter_context(nc.Block())
        x_rows = io["x"].rearrange("b s d -> (b s) d")

        @block.gpsimd
        def _(pool):
            def load(u, c):
                pool.dma_start(xin[:, u, :, :], x_rows[bass.ds(c * CH, CH), :].rearrange("(t p) d -> p t d", p=P)
                               ).then_inc(x_landed[u], 16)

            for i in rounds(pool, NC // 2):
                for u in range(2):
                    wait(pool, xn_ready, 2 * i + u - 1)
                    load(u, 2 * i + u)

        @block.sync
        def _(sp):
            for n, name in enumerate(("wq", "wk")):
                sp.dma_start(wqk[:, n, :, :], io[name].rearrange("(k p) n -> p k n", p=P)).then_inc(weights_landed, 16)
            sp.dma_start(wvr[:, :, 0:D], io["wv"].rearrange("(k p) n -> p k n", p=P)).then_inc(weights_landed, 16)
            sp.dma_start(wvr[:, :, D:D + E], io["router0"].rearrange("(k p) n -> p k n", p=P)).then_inc(weights_landed, 16)
            for i in rounds(sp, NC // 2):
                for u in range(2):
                    c = 2 * i + u
                    for n in range(4):
                        sp.wait_ge(parts_ready, 4 * c + n + 1)
                        rows = dram["qk_parts"][n // 2, :, (n % 2) * P:(n % 2 + 1) * P, bass.ds(c * CH, CH)]
                        sp.dma_start(rows.rearrange("r p n -> p r n"), parts[:, n, :, :]).then_inc(parts_stored[n], 16)
                    sp.wait_ge(v_copied, TC * (c + 1))
                    sp.dma_start(dram["v"][bass.ds(c * CH, CH), :].rearrange("(t p) d -> p t d", p=P), vout[:, u, :, :]
                                 ).then_inc(v_stored[u], 16)
            for n in range(4):
                sp.wait_ge(parts_stored[n], 16 * NC)
            for u in range(2):
                sp.wait_ge(v_stored[u], 16 * (NC // 2))

        @block.vector
        def _(vec):
            vec.memset(eps[:, :], EPS).then_inc(eps_set, 1)
            vec.memset(keep["zero"][:, :], 0.0).then_inc(zeroed, 1)
            ch = Chain(vec, dve_step, per_round=2 * (2 + 2 * 4))
            for i in rounds(vec, NC // 2):
                ch.round(i)
                for u in range(2):
                    c = 2 * i + u
                    wait(vec, std_ready, c - 1)
                    vec.wait_ge(x_landed[u], 16 * (i + 1))
                    for t in range(TC):
                        ins = vec.bn_stats(stats[:, u, t, :], xin[:, u, t, :])
                    ch.link(ins)
                    vec.memset(spare[:, :], 0.0)
                    for t in range(TC):
                        ins = vec.bn_aggr(mv[:, u, t, :], stats[:, u, t, :])
                    ins.then_inc(mv_ready, 1)
                    vec.wait_ge(std_ready, c + 1)
                    vec.wait_ge(mv_ready, c + 1)
                    ch.link(vec.reciprocal(rstd[:, u, :], std[:, u, :]))
                    wait(vec, turned, c - 1)
                    wait(vec, xn_kept, c - 1)
                    for t in range(TC):
                        ins = vec.tensor_scalar(xn[:, u, t, :], xin[:, u, t, :], mv[:, u, t, 0:1], rstd[:, u, t:t + 1],
                                                ALU.subtract, ALU.mult)
                    ins.then_inc(xn_ready, 1)
                    for n in range(4):
                        scale = HD ** -0.5 if n < 2 else 1.0
                        vec.wait_ge(first_part, 4 * c + n + 1)
                        ch.link(vec.scalar_tensor_tensor(out=rest[:, n, :], in0=psq[n][:, :], scalar=scale,
                                                         in1=parts[:, n, 0, :], op0=ALU.mult, op1=ALU.subtract))
                        ch.link(vec.tensor_copy(parts[:, n, 1, :], rest[:, n, :]))
                        vec.tensor_tensor(parts[:, n, 2, :], rest[:, n, :], parts[:, n, 1, :], ALU.subtract
                                          ).then_inc(parts_ready, 1)
            ch.after(NC // 2)

            vec.wait_ge(v_copied, NT)
            L = logits[:, :, :]
            first_max(vec, ch, keep, L, top[:, :], equal[:, :, :], first[:, :], onehot[:, :, :])
            vec.tensor_copy(onehot16[:, :, :], onehot[:, :, :]).then_inc(onehot_ready, 1)
            vec.tensor_tensor(shifted[:, :, :], L, top[:, :].unsqueeze(1).to_broadcast([P, E, NT]), ALU.subtract
                              ).then_inc(shifted_ready, 1)
            vec.wait_ge(exp_ready, 1)
            den, kept, chosen, clipped, slot = (small[:, k, :] for k in range(5))
            ch.link(vec.tensor_reduce(den, expd[:, :, :].rearrange("p e t -> p t e"), X, ALU.add))
            ch.link(vec.reciprocal(keep["gate"][:, :], den))
            vec.wait_ge(counted, 1)
            places(vec, ch, keep, "running0", psq[0][:, 0:E * NT], psq[1][:, 0:E * NT], total[:, :, :], scanned[:, :, :],
                   place[:, :, :])
            ch.link(vec.tensor_tensor(place[:, :, :], place[:, :, :], onehot[:, :, :], ALU.mult))
            ch.link(vec.tensor_reduce(chosen, place[:, :, :].rearrange("p e t -> p t e"), X, ALU.add))
            ch.link(vec.tensor_scalar(kept, chosen, float(CAP0), None, ALU.is_lt))
            ch.link(vec.tensor_tensor(keep["gate"][:, :], keep["gate"][:, :], kept, ALU.mult))
            ch.link(vec.tensor_scalar(clipped, chosen, float(CAP0 - 1), None, ALU.min))
            ch.link(vec.scalar_tensor_tensor(out=slot, in0=first[:, :], scalar=float(CAP0), in1=clipped,
                                             op0=ALU.mult, op1=ALU.add))
            ch.link(vec.tensor_copy(keep["slot_get"][:, :], slot))
            ch.link(vec.scalar_tensor_tensor(out=clipped, in0=kept, scalar=-SKIP, in1=slot, op0=ALU.mult, op1=ALU.add))
            ch.link(vec.tensor_scalar(keep["slot_put"][:, :], clipped, SKIP, None, ALU.add))

        @block.scalar
        def _(act):
            act.wait_ge(eps_set, 1)
            for i in rounds(act, NC // 2):
                for u in range(2):
                    c = 2 * i + u
                    act.wait_ge(mv_ready, c + 1)
                    wait(act, xn_ready, c - 1)
                    act.activation(std[:, u, :], mv[:, u, :, 1], ACT.Sqrt, bias=eps[:, 0:1]).then_inc(std_ready, 1)
                    act.wait_ge(turned, c + 1)
                    wait(act, v_ready, TC * (c - 1))
                    act.copy(xnt[:, u, 0, :], pst[0][:, :])
                    act.copy(xnt[:, u, 1, :], pst[1][:, :]).then_inc(xnt_ready, 1)
                    act.copy(keep["xn_all"][:, bass.ds(c * TC, TC), :], xn[:, u, :, :]).then_inc(xn_kept, 1)
                    for n in range(4):
                        act.wait_ge(qk_ready, 4 * c + n + 1)
                        wait(act, parts_stored[n], 16 * c)
                        act.activation(parts[:, n, 0, :], psq[n][:, :], ACT.Copy, scale=HD ** -0.5 if n < 2 else 1.0
                                       ).then_inc(first_part, 1)
                    for t in range(TC):
                        act.wait_ge(v_ready, TC * c + t + 1)
                        if t == 0:
                            wait(act, v_stored[u], 16 * i)
                        act.copy(vout[:, u, t, :], psv[t % 2][:, 0:D])
                        act.copy(logits[:, :, bass.ds(c * TC + t, 1)].rearrange("p e t -> p (e t)"),
                                 psv[t % 2][:, D:D + E]).then_inc(v_copied, 1)
            act.wait_ge(shifted_ready, 1)
            act.activation(expd[:, :, :], shifted[:, :, :], ACT.Exp).then_inc(exp_ready, 1)

        @block.tensor
        def _(pe):
            pe.wait_ge(weights_landed, 64)
            for i in rounds(pe, NC // 2):
                for u in range(2):
                    c = 2 * i + u
                    pe.wait_ge(xn_ready, c + 1)
                    wait(pe, xnt_ready, c)
                    for t in range(TC):
                        for k in range(KD):
                            ins = pe.transpose(pst[k][:, t * P:(t + 1) * P], xn[:, u, t, k * P:(k + 1) * P],
                                               keep["identity"][:, :])
                    ins.then_inc(turned, 1)
                    pe.wait_ge(xnt_ready, c + 1)
                    for n in range(4):
                        wait(pe, parts_ready, 4 * (c - 1) + n + 1)
                        for k in range(KD):
                            ins = pe.matmul(psq[n][:, :], wqk[:, n // 2, k, (n % 2) * P:(n % 2 + 1) * P], xnt[:, u, k, :],
                                            start=(k == 0), stop=(k == KD - 1))
                        ins.then_inc(qk_ready, 1)
                    for t in range(TC):
                        wait(pe, v_copied, TC * c + t - 1)
                        for k in range(KD):
                            ins = pe.matmul(psv[t % 2][:, 0:D + E], xnt[:, u, k, t * P:(t + 1) * P], wvr[:, k, :],
                                            start=(k == 0), stop=(k == KD - 1))
                        ins.then_inc(v_ready, 1)
            pe.wait_ge(onehot_ready, 1)
            pe.wait_ge(parts_ready, 4 * NC)
            oh = onehot16[:, :, :].rearrange("p e t -> p (e t)")
            pe.matmul(psq[0][:, 0:E * NT], keep["before16"][:, :], oh, start=True, stop=True)
            pe.matmul(psq[1][:, 0:E * NT], keep["ones16"][:, :], oh, start=True, stop=True).then_inc(counted, 1)


def attention_steps():
    maxima, m_cost = [], []
    for c in range(QC):
        for h in range(GH):
            for i in range(TC * c, TC * c + TC):
                for k in range(c + 1):
                    maxima.append(("A", h, i, k))
        m_cost.append(len(maxima))

    def cost_a(u):
        return 90 + min(CH, (u[2] + 1) * P - u[3] * CH)

    whole = sum(cost_a(u) for u in maxima)
    lead, at = 0, 0
    while at < LEAD * whole:
        at += cost_a(maxima[lead])
        lead += 1

    def a_range(lo, hi, dg):
        for n in range(lo, hi):
            yield ("A", dg, *maxima[n][1:])
            if n + 1 in m_cost:
                c = m_cost.index(n + 1)
                yield ("M", dg, c)
                yield ("MT", dg, c)

    head = list(a_range(0, lead, 0))
    stream = list(a_range(lead, len(maxima), 0)) + list(a_range(0, lead, 1))
    tail = list(a_range(lead, len(maxima), 0))

    def width(c, j):
        return CH - max(0, j - TC * c) * P

    def weave(flow):
        pairs = [(c, j) for c in range(QC) for j in range(TC * (c + 1))]
        total = sum(width(*p) for p in pairs) * 2
        flow_total = sum(cost_a(("A", *u[2:])) for u in stream if u[0] == "A")
        flow, steps, done, flow_done, late = list(flow), [], 0, 0, []

        def advance():
            nonlocal flow_done
            while flow and flow_done * total < done * flow_total:
                u = flow.pop(0)
                if u[0] == "A":
                    flow_done += cost_a(("A", *u[2:]))
                if u[0] == "MT":
                    late.append([u, 3])
                else:
                    steps.append(u)

        for n, (c, j) in enumerate(pairs):
            for hp in range(2):
                steps.append(("S", c, j, hp))
                done += width(c, j)
                advance()
                for item in late:
                    item[1] -= 1
                while late and late[0][1] <= 0:
                    steps.append(late.pop(0)[0])
            if n:
                pc, pj = pairs[n - 1]
                steps.append(("PV", pc, pj))
                if pj == TC * (pc + 1) - 1:
                    steps.append(("COPY", pc))
                    late.append([("O", pc), 3])
        steps += flow + [u for u, _ in late]
        c, j = pairs[-1]
        return steps + [("PV", c, j), ("COPY", c), ("O", c)]

    return head, weave(stream), weave(tail)


LEAD = 0.47


def stage_attention(nc, io, keep, dram):
    head, steps, last_steps = attention_steps()
    n_a = sum(u[0] == "A" for u in steps)
    a_head = sum(u[0] == "A" for u in head)
    m_head = sum(u[0] == "M" for u in head)
    n_s = sum(u[0] == "S" for u in steps)
    n_pv = sum(u[0] == "PV" for u in steps)
    n_turn = sum(u[0] in ("O", "MT") for u in steps)
    parts_q, parts_k = (0, 0, 1, 1, 0, 2), (0, 1, 0, 1, 2, 0)
    n_loads = len(parts_q) * QC + len(parts_k) + GH
    with ExitStack() as ctx:
        st = Stage(nc, ctx, "a_")
        qa = [st.sb(f"qa{u}", [MR, QC, GH, CH], BF16) for u in range(2)]
        kb = [st.sb(f"kb{u}", [MR, GH, S], BF16) for u in range(2)]
        vg = [st.sb(f"vg{u}", [P, KT, GH, 32]) for u in range(2)]
        probs = st.sb("probs", [P, 4, 2, CH])
        best = st.sb("best", [P, QC, GH * TC, QC])
        neg = st.sb("neg", [P, GH * TC])
        neg_rest = st.sb("neg_rest", [P, GH * TC])
        neg_parts = st.sb("neg_parts", [P, P // (GH * TC), GH * TC], BF16)
        neg_rows = st.sb("neg_rows", [3 * GH * TC, 2, P], BF16)
        sums = st.sb("sums", [P, CH])
        inv = st.sb("inv", [P, TC, GH])
        oout = st.sb("oout", [P, 2, TC, GH, HD])
        psa = [st.ps(f"psa{k}", [P, CH]) for k in range(2)]
        pss = [st.ps(f"pss{k}", [P, 2, CH]) for k in range(2)]
        acc = st.ps("acc", [P, CH])
        turn = st.ps("turn", [P, CH])

        loaded = [st.sem(f"loaded{u}") for u in range(2)]
        set_up = st.sem("set_up")
        a_ready, a_taken = st.sem("a_ready"), st.sem("a_taken")
        s_ready, exp_done, pv_done = st.sem("s_ready"), st.sem("exp_done"), st.sem("pv_done")
        sums_copied = st.sem("sums_copied")
        m_split, turned, turn_taken = st.sem("m_split"), st.sem("turned"), st.sem("turn_taken")
        m_landed = [st.sem(f"m_landed{c}") for c in range(QC)]
        o_stored = [st.sem(f"o_stored{c}") for c in range(2)]
        dve_step = st.sem("dve_step")
        cleared, scattered = st.sem("cleared"), st.sem("scattered")
        block = ctx.enter_context(nc.Block())

        primed = 1

        def groups(eng):
            with eng.Fori(0, HG - 1) as i:
                for u in range(2):
                    yield 2 * i + u, i, u, steps
            for u in range(2):
                yield 2 * (HG - 1) + u, HG - 1, u, (steps, last_steps)[u]

        @block.gpsimd
        def _(pool):
            ch = Chain(pool, set_up)
            for u in range(2):
                ch.link(pool.memset(kb[u][QR:MR, :, :], 1.0))
                ch.link(pool.memset(vg[u][:, :, :, :], 0.0))
                ch.link(pool.memset(vg[u][:, :, :, HD:HD + 1], 1.0))
            table = dram["expert_in"].rearrange("(p a) d -> p (a d)", p=P)
            n = table.shape[1] // CH
            for k in range(n):
                pool.dma_start(table[:, k * CH:(k + 1) * CH], keep["zero"][:, :]).then_inc(cleared, 16)
            pool.wait_ge(cleared, 16 * n)
            for t in range(NT):
                pool.indirect_dma_start(dram["expert_in"], bass.IndirectOffsetOnAxis(ap=keep["slot_put"][:, t:t + 1], axis=0),
                                        keep["xn_all"][:, t, :], None, bounds_check=E * CAP0 - 1, oob_is_err=False
                                        ).then_inc(scattered, 16)
            pool.wait_ge(scattered, 16 * NT)

        @block.sync
        def _(sp):
            def load(first, u):
                tokens = slice(u * S, (u + 1) * S)
                rows = bass.ds(first, GH * HD)
                for r, part in enumerate(parts_q):
                    for c in range(QC):
                        sp.dma_start(qa[u][r * HD:(r + 1) * HD, c, :, :],
                                     dram["qk_parts"][0, part, rows, u * S + c * CH:u * S + (c + 1) * CH]
                                     .rearrange("(h d) n -> d h n", d=HD)).then_inc(loaded[u], 16)
                for r, part in enumerate(parts_k):
                    sp.dma_start(kb[u][r * HD:(r + 1) * HD, :, :],
                                 dram["qk_parts"][1, part, rows, tokens].rearrange("(h d) n -> d h n", d=HD)
                                 ).then_inc(loaded[u], 16)
                for h in range(GH):
                    sp.dma_start(vg[u][:, :, h, 0:HD],
                                 dram["v"][tokens, bass.ds(first + h * HD, HD)].rearrange("(j p) d -> p j d", p=P)
                                 ).then_inc(loaded[u], 16)

            def store_rows(g, u, c, k):
                sp.wait_ge(turn_taken, k + 1)
                for r in range(3):
                    sp.dma_start(qa[u][QR + r:QR + r + 1, c, :, :].rearrange("o h (i q) -> o (h i) q", q=P),
                                 neg_rows[r * GH * TC:(r + 1) * GH * TC, c % 2, :]
                                 ).then_inc(m_landed[c], 16)

            sp.wait_ge(set_up, 6)
            load(0, 0)
            k = 0
            for s in head:
                if s[0] == "MT":
                    store_rows(0, 0, s[2], k)
                    k += 1
            for g, i, u, order in groups(sp):
                if not (isinstance(g, int) and g == 2 * HG - 1):
                    first = snap(sp, (i + u) * GH * HD)
                    sp.wait_ge(pv_done, primed + g * n_pv)
                    load(first, 1 - u)
                k = 0
                for s in order:
                    if s[0] == "MT":
                        store_rows(g, (u + s[1]) % 2, s[2], m_head + g * n_turn + k)
                    k += s[0] in ("MT", "O")
            for c in range(2):
                sp.wait_ge(o_stored[c], 16 * (primed + QC * HG))

        @block.tensor
        def _(pe):
            def a_step(u, s, n, slot):
                _, dg, h, i, k = s
                keys = min(CH, (i + 1) * P - k * CH)
                diagonal = k == i // TC
                wait(pe, a_taken, n - 1)
                ins = pe.matmul(psa[slot][:, 0:keys], qa[u][0:QR, i // TC, h, (i % TC) * P:(i % TC + 1) * P], kb[u][0:QR, h, k * CH:k * CH + keys],
                                start=True, stop=not diagonal)
                if diagonal:
                    ins = pe.matmul(psa[slot][:, keys - P:keys], keep["identity16"][:, :], keep["mask_qk"][:, :],
                                    start=False, stop=True)
                ins.then_inc(a_ready, 1)

            def m_turn(n, k):
                pe.wait_ge(m_split, n + 1)
                wait(pe, turn_taken, k)
                pe.transpose(turn[:, 0:P // 2].bitcast(BF16), neg_parts[:, :, :].rearrange("p r n -> p (r n)"),
                             keep["identity16"][:, :]).then_inc(turned, 1)

            pe.nop().then_inc(pv_done, primed)
            pe.wait_ge(set_up, 6)
            pe.wait_ge(loaded[0], 16 * n_loads)
            n = m = 0
            for s in head:
                if s[0] == "A":
                    a_step(0, s, n, n % 2)
                    n += 1
                if s[0] == "MT":
                    m_turn(m, m)
                    m += 1
            for g, i, u, order in groups(pe):
                a = idx = pv = m = k = 0
                next_seen = False
                for s in order:
                    if s[0] == "A":
                        if s[1] == 1 and not next_seen:
                            next_seen = True
                            pe.wait_ge(loaded[1 - u], 16 * n_loads * (i + 1 + u))
                        a_step((u + s[1]) % 2, s, a_head + g * n_a + a, (a_head + a) % 2)
                        a += 1
                    elif s[0] == "MT":
                        m_turn(m_head + g * QC + m, m_head + g * n_turn + k)
                        m += 1
                        k += 1
                    elif s[0] == "S":
                        _, c, j, hp = s
                        lo = max(0, j - TC * c) * P
                        if j == 0 and hp == 0:
                            pe.wait_ge(m_landed[c], 48 * (g + 1))
                        pe.wait_ge(exp_done, primed + g * n_s + max(idx - 1, 0))
                        for e in range(2):
                            h = 2 * hp + e
                            ins = pe.matmul(pss[idx % 2][:, e, lo:CH], kb[u][0:MR, h, j * P:(j + 1) * P],
                                            qa[u][0:MR, c, h, lo:CH], start=True, stop=(j < TC * c))
                            if j >= TC * c:
                                ins = pe.matmul(pss[idx % 2][:, e, lo:lo + P], keep["identity16"][:, :],
                                                keep["mask_kq"][:, :], start=False, stop=True)
                        ins.then_inc(s_ready, 1)
                        idx += 1
                    elif s[0] == "PV":
                        _, c, j = s
                        lo = max(0, j - TC * c) * P
                        pe.wait_ge(exp_done, primed + g * n_s + 2 * pv + 2)
                        if j == 0:
                            pe.wait_ge(sums_copied, primed + g * QC + c)
                        for h in range(GH):
                            ins = pe.matmul(acc[32 * h:32 * h + 32, lo:CH], vg[u][:, j, h, :],
                                            probs[:, 2 * (pv % 2) + h // 2, h % 2, lo:CH],
                                            start=(j == 0), stop=(j == TC * (c + 1) - 1))
                        ins.then_inc(pv_done, 1)
                        pv += 1
                    elif s[0] == "O":
                        c = s[1]
                        pe.wait_ge(sums_copied, primed + g * QC + c + 1)
                        pe.wait_ge(turn_taken, m_head + g * n_turn + k)
                        for t in range(TC):
                            ins = pe.transpose(turn[:, t * P:(t + 1) * P], sums[:, t * P:(t + 1) * P], keep["identity"][:, :])
                        ins.then_inc(turned, 1)
                        k += 1

        @block.scalar
        def _(act):
            def store(g, i, u, c, k):
                act.wait_ge(turn_taken, m_head + g * n_turn + k + 1)
                act.dma_start(dram["attn0"][u * S + c * CH:u * S + (c + 1) * CH, bass.ds(i * GH * HD, GH * HD)]
                              .rearrange("(t p) d -> p t d", p=P),
                              oout[:, c % 2, :, :, :].rearrange("p t h d -> p t (h d)")).then_inc(o_stored[c % 2], 16)

            act.nop().then_inc(exp_done, primed)
            act.nop().then_inc(sums_copied, primed)
            for c in range(2):
                act.nop().then_inc(o_stored[c], 16 * primed)
            for g, i, u, order in groups(act):
                idx = k = pv = 0
                turned_at = None
                for s in order:
                    if turned_at and idx >= turned_at[0] + 3:
                        store(g, i, u, *turned_at[1:])
                        turned_at = None
                    if s[0] == "O":
                        turned_at = (idx, s[1], k)
                    if s[0] == "S":
                        _, c, j, hp = s
                        lo = max(0, j - TC * c) * P
                        act.wait_ge(s_ready, g * n_s + idx + 1)
                        act.wait_ge(pv_done, primed + g * n_pv + max(idx // 2 - 1, 0))
                        act.activation(probs[:, idx % 4, :, lo:CH], pss[idx % 2][:, :, lo:CH], ACT.Exp).then_inc(exp_done, 1)
                        idx += 1
                    elif s[0] == "PV":
                        pv += 1
                    elif s[0] == "COPY":
                        act.wait_ge(pv_done, primed + g * n_pv + pv)
                        act.wait_ge(turned, m_head + g * n_turn + (k if s[1] else 0))
                        act.copy(sums[:, :], acc[:, :]).then_inc(sums_copied, 1)
                    elif s[0] in ("O", "MT"):
                        k += 1
                store(g, i, u, *turned_at[1:])

        @block.vector
        def _(vec):
            ch = Chain(vec, dve_step)
            per_group = 4 * QC + QC
            ch_head = 4 * m_head + 1

            def take(s, n, slot):
                _, _, h, i, k = s
                keys = min(CH, (i + 1) * P - k * CH)
                vec.wait_ge(a_ready, n + 1)
                vec.tensor_reduce(best[:, i // TC, h * TC + i % TC, k:k + 1], psa[slot][:, 0:keys], X, ALU.max
                                  ).then_inc(a_taken, 1)

            def split(c, turns, taken):
                vec.wait_ge(a_taken, taken)
                wait(vec, turned, turns)
                ch.link(vec.tensor_reduce(neg[:, :], best[:, c, :, 0:c + 1], X, ALU.max, negate=True))
                ch.link(vec.tensor_copy(neg_parts[:, 0, :], neg[:, :]))
                ch.link(vec.tensor_tensor(neg_rest[:, :], neg[:, :], neg_parts[:, 0, :], ALU.subtract))
                ch.link(vec.tensor_copy(neg_parts[:, 1, :], neg_rest[:, :]))
                vec.tensor_tensor(neg_parts[:, 2, :], neg_rest[:, :], neg_parts[:, 1, :], ALU.subtract).then_inc(m_split, 1)

            def take_rows(c, k, landed):
                vec.wait_ge(turned, k + 1)
                wait(vec, m_landed[(c - 2) % QC], landed)
                vec.tensor_copy(neg_rows[:, c % 2, :], turn[0:3 * GH * TC, 0:P // 2].bitcast(BF16)).then_inc(turn_taken, 1)

            ch.link(vec.memset(neg_parts[:, :, :], 0.0))
            n = m = 0
            for s in head:
                if s[0] == "A":
                    take(s, n, n % 2)
                    n += 1
                elif s[0] == "M":
                    split(s[2], m, n)
                elif s[0] == "MT":
                    take_rows(s[2], m, 0)
                    m += 1
            for g, i, u, order in groups(vec):
                ch.base, ch.k = ch_head + g * per_group, 0
                a = k = m = 0
                for s in order:
                    if s[0] == "A":
                        take(s, a_head + g * n_a + a, (a_head + a) % 2)
                        a += 1
                    elif s[0] == "M":
                        split(s[2], m_head + g * n_turn + k, a_head + g * n_a + a)
                    elif s[0] == "MT":
                        _, dg, c = s
                        take_rows(c, m_head + g * n_turn + k, 48 * (g + dg + (c >= 2)))
                        k += 1
                    elif s[0] == "O":
                        c = s[1]
                        vec.wait_ge(turned, m_head + g * n_turn + k + 1)
                        t4 = turn[:, :].rearrange("p (t h x) -> p t h x", t=TC, h=GH)
                        ch.link(vec.reciprocal(inv[:, :, :], t4[:, :, :, HD:HD + 1].rearrange("p t h x -> p t (h x)")))
                        vec.wait_ge(o_stored[c % 2], 16 * (primed + 2 * g + c // 2))
                        vec.tensor_tensor(oout[:, c % 2, :, :, :], t4[:, :, :, 0:HD],
                                          inv[:, :, :].unsqueeze(3).to_broadcast([P, TC, GH, HD]), ALU.mult
                                          ).then_inc(turn_taken, 1)
                        k += 1


def stage_experts(nc, io, keep, dram):
    ST = CAP0 // P
    with ExitStack() as ctx:
        st = Stage(nc, ctx, "e_")
        w1 = [st.sb(f"w1_{u}", [P, KD, F]) for u in range(2)]
        w2 = [st.sb(f"w2_{u}", [P, FT, D]) for u in range(2)]
        rows = st.sb("rows", [P, 2, ST, D])
        rows_t = st.sb("rows_t", [P, 2, KD, CAP0])
        hidden = st.sb("hidden", [P, 2, FT, CAP0])
        yout = st.sb("yout", [P, 2, ST, D])
        pst = [st.ps(f"pst{k}", [P, CAP0]) for k in range(KD)]
        psh = [st.ps(f"psh{k}", [P, CAP0]) for k in range(4)]
        psy = [st.ps(f"psy{k}", [P, D]) for k in range(2)]
        landed = [st.sem(f"landed{u}") for u in range(2)]
        turned, turn_taken = st.sem("turned"), st.sem("turn_taken")
        h_ready, h_taken = st.sem("h_ready"), st.sem("h_taken")
        y_ready, y_taken = st.sem("y_ready"), st.sem("y_taken")
        stored = [st.sem(f"stored{u}") for u in range(2)]
        block = ctx.enter_context(nc.Block())
        w1_rows = io["w1"].rearrange("e d f -> (e d) f")
        w2_rows = io["w2"].rearrange("e f d -> (e f) d")

        @block.sync
        def _(sp):
            for i in rounds(sp, E // 2):
                for u in range(2):
                    e = 2 * i + u
                    slots, ins, outs = snap(sp, e * CAP0), snap(sp, e * D), snap(sp, e * F)
                    wait(sp, y_ready, ST * (e - 1))
                    sp.dma_start(rows[:, u, :, :], dram["expert_in"][bass.ds(slots, CAP0), :]
                                 .rearrange("(t p) d -> p t d", p=P)).then_inc(landed[u], 16)
                    sp.dma_start(w1[u][:, :, :], w1_rows[bass.ds(ins, D), :].rearrange("(k p) f -> p k f", p=P)
                                 ).then_inc(landed[u], 16)
                    sp.dma_start(w2[u][:, :, :], w2_rows[bass.ds(outs, F), :].rearrange("(k p) d -> p k d", p=P)
                                 ).then_inc(landed[u], 16)

        @block.gpsimd
        def _(pool):
            for i in rounds(pool, E // 2):
                for u in range(2):
                    e = 2 * i + u
                    pool.wait_ge(y_taken, ST * (e + 1))
                    pool.dma_start(dram["expert_out"][bass.ds(e * CAP0, CAP0), :].rearrange("(t p) d -> p t d", p=P),
                                   yout[:, u, :, :]).then_inc(stored[u], 16)
            for u in range(2):
                pool.wait_ge(stored[u], 16 * (E // 2))

        @block.tensor
        def _(pe):
            for i in rounds(pe, E // 2):
                for u in range(2):
                    e = 2 * i + u
                    pe.wait_ge(landed[u], 48 * (i + 1))
                    wait(pe, turn_taken, e)
                    for t in range(ST):
                        for k in range(KD):
                            ins = pe.transpose(pst[k][:, t * P:(t + 1) * P], rows[:, u, t, k * P:(k + 1) * P],
                                               keep["identity"][:, :])
                    ins.then_inc(turned, 1)
                    pe.wait_ge(turn_taken, e + 1)
                    for f in range(FT):
                        wait(pe, h_taken, FT * e + f - 3)
                        for k in range(KD):
                            ins = pe.matmul(psh[f % 4][:, :], w1[u][:, k, f * P:(f + 1) * P], rows_t[:, u, k, :],
                                            start=(k == 0), stop=(k == KD - 1))
                        ins.then_inc(h_ready, 1)
                    pe.wait_ge(h_taken, FT * (e + 1))
                    for t in range(ST):
                        wait(pe, y_taken, ST * e + t - 1)
                        for f in range(FT):
                            ins = pe.matmul(psy[t % 2][:, :], hidden[:, u, f, t * P:(t + 1) * P], w2[u][:, f, :],
                                            start=(f == 0), stop=(f == FT - 1))
                        ins.then_inc(y_ready, 1)

        @block.scalar
        def _(act):
            for i in rounds(act, E // 2):
                for u in range(2):
                    e = 2 * i + u
                    act.wait_ge(turned, e + 1)
                    wait(act, h_ready, FT * (e - 1))
                    act.copy(rows_t[:, u, 0, :], pst[0][:, :])
                    act.copy(rows_t[:, u, 1, :], pst[1][:, :]).then_inc(turn_taken, 1)
                    for f in range(FT):
                        act.wait_ge(h_ready, FT * e + f + 1)
                        if f == 0:
                            wait(act, y_ready, ST * (e - 1))
                        act.activation(hidden[:, u, f, :], psh[f % 4][:, :], ACT.Gelu_apprx_tanh).then_inc(h_taken, 1)

        @block.vector
        def _(vec):
            for i in rounds(vec, E // 2):
                for u in range(2):
                    e = 2 * i + u
                    for t in range(ST):
                        vec.wait_ge(y_ready, ST * e + t + 1)
                        if t == 0:
                            wait(vec, stored[u], 16 * i)
                        vec.tensor_copy(yout[:, u, t, :], psy[t % 2][:, :]).then_inc(y_taken, 1)


def ago(c):
    return c - 1


def chunks_skewed(eng, front, back):
    front(0, 0, 0)
    for i in rounds(eng, NC // 2 - 1):
        front(2 * i + 1, i, 1)
        back(2 * i, i, 0)
        front(2 * i + 2, i + 1, 0)
        back(2 * i + 1, i, 1)
    last = NC // 2 - 1
    front(NC - 1, last, 1)
    back(NC - 2, last, 0)
    back(NC - 1, last, 1)


def stage_join(nc, io, keep, dram):
    with ExitStack() as ctx:
        st = Stage(nc, ctx, "j_")
        wo = st.sb("wo", [P, KD, D])
        wr = st.sb("wr", [P, KD, E])
        oin = st.sb("oin", [P, 2, TC, D])
        xin = st.sb("xin", [P, 2, TC, D])
        yin = st.sb("yin", [P, 2, TC, D])
        ot = st.sb("ot", [P, 2, KD, CH])
        silu = st.sb("silu", [P, 2, TC, D])
        x1 = st.sb("x1", [P, 2, TC, D])
        xn = st.sb("xn", [P, 2, TC, D])
        xnt = st.sb("xnt", [P, 2, KD, CH])
        stats = st.sb("stats", [P, 2, TC, 6])
        mv = st.sb("mv", [P, 2, TC, 2])
        std = st.sb("std", [P, 2, TC])
        rstd = st.sb("rstd", [P, 2, TC])
        eps = st.sb("eps", [P, 1])
        spare = st.sb("spare", [P, 1])
        logits = st.sb("logits", [P, E, NT])
        names3 = ("equal", "onehot0", "onehot1", "both", "masked", "total", "scanned", "place", "fits")
        big = {n: st.sb("r_" + n, [P, E, NT]) for n in names3}
        both16 = st.sb("both16", [P, E, NT], BF16)
        small = {n: st.sb("s_" + n, [P, NT]) for n in ("top0", "top1", "first0", "first1", "gap", "ratio", "den", "w0", "w1")}
        pst = [st.ps(f"pst{k}", [P, CH]) for k in range(KD)]
        psx = [st.ps(f"psx{k}", [P, CH]) for k in range(KD)]
        pss = [st.ps(f"pss{k}", [P, 2, D]) for k in range(2)]
        psl = st.ps("psl", [P, TC, E])
        psc = st.ps("psc", [P, 2, E * NT])

        weights_landed = st.sem("weights_landed")
        in_landed = [st.sem(f"in_landed{u}") for u in range(2)]
        y_landed = [st.sem(f"y_landed{u}") for u in range(2)]
        o_turned, ot_ready, s_ready, silu_ready = (st.sem("o_turned"), st.sem("ot_ready"), st.sem("s_ready"),
                                                   st.sem("silu_ready"))
        s_taken = st.sem("s_taken")
        x1_ready = st.sem("x1_ready")
        mv_ready, std_ready, xn_ready = st.sem("mv_ready"), st.sem("std_ready"), st.sem("xn_ready")
        x_turned, xnt_ready, l_ready, l_taken = st.sem("x_turned"), st.sem("xnt_ready"), st.sem("l_ready"), st.sem("l_taken")
        x1_stored = [st.sem(f"x1_stored{u}") for u in range(2)]
        xnt_stored = [st.sem(f"xnt_stored{u}") for u in range(2)]
        eps_set, dve_step = st.sem("eps_set"), st.sem("dve_step")
        onehot_ready, counted, gap_ready, ratio_ready = (st.sem("onehot_ready"), st.sem("counted"), st.sem("gap_ready"),
                                                         st.sem("ratio_ready"))
        block = ctx.enter_context(nc.Block())
        x_rows = io["x"].rearrange("b s d -> (b s) d")

        def tiles(rows, c):
            return rows[bass.ds(c * CH, CH), :].rearrange("(t p) d -> p t d", p=P)

        @block.sync
        def _(sp):
            sp.dma_start(wo[:, :, :], io["wo"].rearrange("(k p) n -> p k n", p=P)).then_inc(weights_landed, 16)
            sp.dma_start(wr[:, :, :], io["router1"].rearrange("(k p) n -> p k n", p=P)).then_inc(weights_landed, 16)

            def load(c, u):
                sp.dma_start(oin[:, u, :, :], tiles(dram["attn0"], c)).then_inc(in_landed[u], 16)
                sp.dma_start(xin[:, u, :, :], tiles(x_rows, c)).then_inc(in_landed[u], 16)

            def store(c, u):
                sp.wait_ge(x1_ready, c + 1)
                sp.dma_start(tiles(dram["x1"], c), x1[:, u, :, :]).then_inc(x1_stored[u], 16)

            load(0, 0)
            load(1, 1)
            with sp.Fori(0, NC // 2 - 1) as i:
                for u in range(2):
                    store(2 * i + u, u)
                    load(2 * i + u + 2, u)
            store(NC - 2, 0)
            store(NC - 1, 1)
            for u in range(2):
                sp.wait_ge(x1_stored[u], 16 * (NC // 2))
                sp.wait_ge(xnt_stored[u], 16 * (NC // 2))

        @block.gpsimd
        def _(pool):
            for c in range(NC):
                u = c % 2
                if c >= 2:
                    pool.wait_ge(y_landed[u], 16 * TC * (c // 2))
                    pool.wait_ge(silu_ready, c - 1)
                for t in range(TC):
                    n = c * TC + t
                    pool.indirect_dma_start(yin[:, u, t, :], None, dram["expert_out"],
                                            bass.IndirectOffsetOnAxis(ap=keep["slot_get"][:, n:n + 1], axis=0)
                                            ).then_inc(y_landed[u], 16)

        @block.tensor
        def _(pe):
            pe.wait_ge(weights_landed, 32)

            def front(c, n, u):
                pe.wait_ge(in_landed[u], 32 * (n + 1))
                wait(pe, ot_ready, c)
                for t in range(TC):
                    for k in range(KD):
                        ins = pe.transpose(pst[k][:, t * P:(t + 1) * P], oin[:, u, t, k * P:(k + 1) * P],
                                           keep["identity"][:, :])
                ins.then_inc(o_turned, 1)
                pe.wait_ge(ot_ready, c + 1)
                wait(pe, s_taken, c)
                for t in range(TC):
                    for k in range(KD):
                        ins = pe.matmul(pss[t // 2][:, t % 2, :], ot[:, u, k, t * P:(t + 1) * P], wo[:, k, :],
                                        start=(k == 0), stop=(k == KD - 1))
                ins.then_inc(s_ready, 1)

            def back(c, n, u):
                pe.wait_ge(xn_ready, c + 1)
                wait(pe, xnt_ready, c)
                for t in range(TC):
                    for k in range(KD):
                        ins = pe.transpose(psx[k][:, t * P:(t + 1) * P], xn[:, u, t, k * P:(k + 1) * P],
                                           keep["identity"][:, :])
                ins.then_inc(x_turned, 1)
                pe.wait_ge(xnt_ready, c + 1)
                wait(pe, l_taken, c)
                for t in range(TC):
                    for k in range(KD):
                        ins = pe.matmul(psl[:, t, :], xnt[:, u, k, t * P:(t + 1) * P], wr[:, k, :],
                                        start=(k == 0), stop=(k == KD - 1))
                ins.then_inc(l_ready, 1)

            chunks_skewed(pe, front, back)
            pe.wait_ge(onehot_ready, 1)
            oh = both16[:, :, :].rearrange("p e t -> p (e t)")
            pe.matmul(psc[:, 0, :], keep["before16"][:, :], oh, start=True, stop=True)
            pe.matmul(psc[:, 1, :], keep["ones16"][:, :], oh, start=True, stop=True).then_inc(counted, 1)

        @block.scalar
        def _(act):
            act.wait_ge(eps_set, 1)

            def front(c, n, u):
                act.wait_ge(o_turned, c + 1)
                wait(act, s_ready, ago(c))
                act.copy(ot[:, u, 0, :], pst[0][:, :])
                act.copy(ot[:, u, 1, :], pst[1][:, :]).then_inc(ot_ready, 1)
                act.wait_ge(y_landed[u], 16 * TC * (n + 1))
                wait(act, x1_ready, ago(c))
                for t in range(TC):
                    ins = act.activation(silu[:, u, t, :], yin[:, u, t, :], ACT.Silu,
                                         scale=keep["gate"][:, bass.ds(c * TC + t, 1)])
                ins.then_inc(silu_ready, 1)
                act.wait_ge(mv_ready, c + 1)
                act.activation(std[:, u, :], mv[:, u, :, 1], ACT.Sqrt, bias=eps[:, 0:1]).then_inc(std_ready, 1)

            def back(c, n, u):
                act.wait_ge(x_turned, c + 1)
                wait(act, xnt_stored[u], 16 * n)
                act.copy(xnt[:, u, 0, :], psx[0][:, :])
                act.copy(xnt[:, u, 1, :], psx[1][:, :]).then_inc(xnt_ready, 1)
                act.wait_ge(l_ready, c + 1)
                act.copy(logits[:, :, bass.ds(c * TC, TC)].rearrange("p e t -> p t e"), psl[:, :, :]).then_inc(l_taken, 1)
                act.wait_ge(xnt_ready, c + 1)
                act.dma_start(dram["xnt1"][:, :, bass.ds(c * CH, CH)].rearrange("k p n -> p k n"), xnt[:, u, :, :]
                              ).then_inc(xnt_stored[u], 16)

            chunks_skewed(act, front, back)
            act.wait_ge(gap_ready, 1)
            act.activation(small["ratio"][:, :], small["gap"][:, :], ACT.Exp).then_inc(ratio_ready, 1)

        @block.vector
        def _(vec):
            vec.memset(eps[:, :], EPS).then_inc(eps_set, 1)
            ch = Chain(vec, dve_step)

            def front(c, n, u):
                ch.base, ch.k = 3 * c, 0
                vec.wait_ge(s_ready, c + 1)
                vec.wait_ge(silu_ready, c + 1)
                vec.wait_ge(in_landed[u], 32 * (n + 1))
                for k in range(2):
                    ins = vec.tensor_tensor(silu[:, u, 2 * k:2 * k + 2, :], pss[k][:, :, :], silu[:, u, 2 * k:2 * k + 2, :],
                                            ALU.mult)
                ins.then_inc(s_taken, 1)
                vec.wait_ge(s_taken, c + 1)
                wait(vec, x1_stored[u], 16 * n)
                vec.tensor_tensor(x1[:, u, :, :], xin[:, u, :, :], silu[:, u, :, :], ALU.add).then_inc(x1_ready, 1)
                vec.wait_ge(x1_ready, c + 1)
                for t in range(TC):
                    ins = vec.bn_stats(stats[:, u, t, :], x1[:, u, t, :])
                ch.link(ins)
                vec.memset(spare[:, :], 0.0)
                for t in range(TC):
                    ins = vec.bn_aggr(mv[:, u, t, :], stats[:, u, t, :])
                ins.then_inc(mv_ready, 1)
                vec.wait_ge(mv_ready, c + 1)
                vec.wait_ge(std_ready, c + 1)
                ch.link(vec.reciprocal(rstd[:, u, :], std[:, u, :]))
                wait(vec, x_turned, ago(c))
                for t in range(TC):
                    ins = vec.tensor_scalar(xn[:, u, t, :], x1[:, u, t, :], mv[:, u, t, 0:1], rstd[:, u, t:t + 1],
                                            ALU.subtract, ALU.mult)
                ins.then_inc(xn_ready, 1)
                ch.link(vec.memset(spare[:, :], 0.0))

            chunks_skewed(vec, front, lambda c, n, u: None)
            ch.base, ch.k = 3 * NC, 0

            vec.wait_ge(l_taken, NC)
            L, s = logits[:, :, :], {n: v[:, :] for n, v in small.items()}
            b = {n: v[:, :, :] for n, v in big.items()}
            first_max(vec, ch, keep, L, s["top0"], b["equal"], s["first0"], b["onehot0"])
            ch.link(vec.scalar_tensor_tensor(out=b["masked"], in0=b["onehot0"], scalar=-3.0e38, in1=L, op0=ALU.mult, op1=ALU.add))
            first_max(vec, ch, keep, b["masked"], s["top1"], b["equal"], s["first1"], b["onehot1"])
            ch.link(vec.tensor_tensor(b["both"], b["onehot0"], b["onehot1"], ALU.add))
            vec.tensor_copy(both16[:, :, :], b["both"]).then_inc(onehot_ready, 1)
            vec.tensor_tensor(s["gap"], s["top1"], s["top0"], ALU.subtract).then_inc(gap_ready, 1)
            vec.wait_ge(ratio_ready, 1)
            ch.link(vec.tensor_scalar(s["den"], s["ratio"], 1.0, None, ALU.add))
            ch.link(vec.reciprocal(s["w0"], s["den"]))
            ch.link(vec.tensor_tensor(s["w1"], s["ratio"], s["w0"], ALU.mult))
            vec.wait_ge(counted, 1)
            places(vec, ch, keep, "running1", psc[:, 0, :], psc[:, 1, :], b["total"], b["scanned"], b["place"])
            ch.link(vec.tensor_scalar(b["fits"], b["place"], float(CAP1), None, ALU.is_lt))
            for w, oh in (("w0", "onehot0"), ("w1", "onehot1")):
                ch.link(vec.tensor_tensor(b[oh], b[oh], s[w].unsqueeze(1).to_broadcast([P, E, NT]), ALU.mult))
            ch.link(vec.tensor_tensor(b["both"], b["onehot0"], b["onehot1"], ALU.add))
            ch.link(vec.tensor_tensor(keep["coef"][:, :, :].rearrange("p t e -> p e t"), b["both"], b["fits"], ALU.mult))


PAIRS = H // 2


def window_steps():
    fillers = {0: [("W", 0)], 1: [("W", 1)], 2: [("W", 2), ("QR", 0)], 3: [("W", 3), ("QR", 1), ("QR", 2)],
               4: [("W", 4), ("QR", 3), ("KR", 0), ("E", 0)], 5: [("W", 5), ("QR", 4), ("QR", 5), ("KR", 1), ("E", 1)],
               6: [("E", 2), ("QR", 6), ("KR", 2)], 7: [("E", 3), ("QR", 7), ("KR", 3)]}
    steps = []
    for p in range(PAIRS):
        steps.append(("S", p))
        if p >= 1:
            steps.append(("N", p - 1))
        steps += fillers[p]
        if p >= 2:
            steps.append(("T", p - 2))
        if p >= 3:
            steps.append(("PV", p - 3))
    steps += [("N", 7), ("T", 6), ("PV", 5), ("R", 0), ("R", 1), ("T", 7), ("PV", 6), ("R", 2), ("R", 3), ("PV", 7),
              ("R", 4), ("R", 5), ("OUT",)]
    return steps


def emptier(s):
    if s[0] == "W":
        return "act"
    if s[0] == "E":
        return "dve"
    if s[0] == "T":
        return ("dve", "act")[s[1] % 2]
    return "act" if s[1] < 4 else "dve"


class Uses:

    def __init__(self, kinds, ahead, steps):
        self.kinds = kinds
        self.ahead = ahead
        self.every = [s for s in steps if s[0] in kinds]
        assert len(ahead) % 2 == 0 and len(self.every) % 2 == 0

    def emptied(self, who, t):
        return sum(emptier(s) == who for s in self.ahead) + t * sum(emptier(s) == who for s in self.every)

    def filled(self, t):
        return len(self.ahead) + t * len(self.every)

    def within(self, order, n, who=None):
        mine = [s for s in order if s[0] in self.kinds][:n]
        return len([s for s in mine if who is None or emptier(s) == who])

    def index(self, order, step):
        return [s for s in order if s[0] in self.kinds].index(step)


def stage_windows(nc, io, keep, dram, out):
    steps = window_steps()
    first_steps = [("W", n) for n in range(6)] + [("QR", n) for n in range(8)] + [("KR", n) for n in range(4)] + [
        ("R", n) for n in range(6)]
    last_steps = [s for s in steps if s[0] not in ("W", "QR", "KR", "R")]
    work = Uses(("W", "E"), [("W", n) for n in range(6)], steps)
    turns = Uses(("T", "R"), [("R", n) for n in range(6)], steps)
    with ExitStack() as ctx:
        st = Stage(nc, ctx, "w_")
        wqkv = st.sb("wqkv", [P, KD, 3 * J])
        wout = st.sb("wout", [P, PAIRS, D])
        we = st.sb("we", [P, KD, E, D])
        rope_names = [f"{f}_{n}" for f in ("cos", "sin") for n in ("q0", "q1", "k")]
        rope = {n: st.sb("t_" + n, [P, DH // 2]) for n in rope_names}
        nsin = {n: st.sb("n_" + n, [P, DH // 2]) for n in ("q0", "q1", "k")}
        masks = st.sb("masks", [P, NT, 2 * P], BF16)
        xnt = st.sb("xnt", [P, 2, KD, P])
        x1 = st.sb("x1", [P, 2, D])
        raw = st.sb("raw", [P, 3, J])
        rot = st.sb("rot", [P, 3, J])
        crossed = st.sb("crossed", [P, 2, J])
        v = [st.sb(f"v{u}", [P, J]) for u in range(2)]
        kd = [st.sb(f"kd{u}", [P, PAIRS, 2, P]) for u in range(2)]
        qt = st.sb("qt", [P, 2, PAIRS, P])
        top = st.sb("top", [P, 2, PAIRS])
        rows = st.sb("rows", [P, 2, PAIRS])
        inv = st.sb("inv", [P, 2, PAIRS])
        probs = st.sb("probs", [P, 4, 2, 2 * P])
        pt = st.sb("pt", [P, 2, 4, P])
        ot = st.sb("ot", [P, PAIRS, P])
        y = st.sb("y", [P, D])
        sig = st.sb("sig", [P, D])
        res = st.sb("res", [P, 2, D])
        psw = [st.ps(f"psw{k}", [P, CH]) for k in range(2)]
        pss = [st.ps(f"pss{k}", [P, 2, 2 * P]) for k in range(2)]
        pst = [st.ps(f"pst{k}", [P, 4, P]) for k in range(2)]
        pso = st.ps("pso", [P, 4, P])
        psy = st.ps("psy", [P, D])

        weights_landed = st.sem("weights_landed")
        n_weights = 2 + KD + len(rope_names)
        pool_set = st.sem("pool_set")
        xt_landed = [st.sem(f"xt_landed{u}") for u in range(2)]
        x1_landed = [st.sem(f"x1_landed{u}") for u in range(2)]
        work_ready, s_ready, t_ready = st.sem("work_ready"), st.sem("s_ready"), st.sem("t_ready")
        work_taken = {w: st.sem("work_taken_" + w) for w in ("act", "dve")}
        turn_taken = {w: st.sem("turn_taken_" + w) for w in ("act", "dve")}
        top_ready, exp_ready, inv_ready, p_ready = (st.sem("top_ready"), st.sem("exp_ready"), st.sem("inv_ready"),
                                                    st.sem("p_ready"))
        pv_done, ot_ready, y_ready, out_ready = st.sem("pv_done"), st.sem("ot_ready"), st.sem("y_ready"), st.sem("out_ready")
        q_rotated, k_rotated, v_moved = st.sem("q_rotated"), st.sem("k_rotated"), st.sem("v_moved")
        sig_ready, res_step = st.sem("sig_ready"), st.sem("res_step")
        stored = [st.sem(f"stored{u}") for u in range(2)]
        dve_step, pool_step = st.sem("dve_step"), st.sem("pool_step")
        block = ctx.enter_context(nc.Block())
        out_rows = out.rearrange("b s d -> (b s) d")

        def tiles(eng):
            for i in rounds(eng, NT // 2 - 1):
                for u in range(2):
                    yield 2 * i + u, u, i, steps
            yield NT - 2, 0, NT // 2 - 1, steps
            yield NT - 1, 1, NT // 2 - 1, last_steps

        def heads(ap):
            return ap.rearrange("p (h s x) -> p h s x", s=2, x=DH // 2)

        wide = [P, H, DH // 2]

        def rotary(eng, r, c, name, n, src):
            if n < 2:
                sin = (nsin[name], rope["sin_" + name])[n]
                return eng.tensor_tensor(heads(crossed[:, c, :])[:, :, n, :], heads(src)[:, :, 1 - n, :],
                                         sin[:, :].unsqueeze(1).to_broadcast(wide), ALU.mult)
            if n == 2:
                halves = [P, 2 * H, DH // 2]
                return eng.tensor_tensor(rot[:, r, :].rearrange("p (h x) -> p h x", x=DH // 2),
                                         src.rearrange("p (h x) -> p h x", x=DH // 2),
                                         rope["cos_" + name][:, :].unsqueeze(1).to_broadcast(halves), ALU.mult)
            return eng.tensor_tensor(rot[:, r, :], rot[:, r, :], crossed[:, c, :], ALU.add)

        @block.sync
        def _(sp):
            sp.dma_start(wqkv[:, :, :], io["w_qkv"].rearrange("(k p) n -> p k n", p=P)).then_inc(weights_landed, 16)
            sp.dma_start(wout[:, :, :], io["w_out"].rearrange("(k p) n -> p k n", p=P)).then_inc(weights_landed, 16)
            for k in range(KD):
                sp.dma_start(we[:, k, :, :], io["we"][:, k * P:(k + 1) * P, :].rearrange("e p d -> p e d")
                             ).then_inc(weights_landed, 16)
            for f in ("cos", "sin"):
                for n, at in (("q0", 0), ("q1", P), ("k", 0)):
                    sp.dma_start(rope[f"{f}_{n}"][:, :], io[f"{f}_{n[0]}"][at:at + P, :]).then_inc(weights_landed, 16)

            def load_t(at, u):
                sp.dma_start(xnt[:, u, :, :], dram["xnt1"][:, :, bass.ds(at, P)].rearrange("k p n -> p k n")
                             ).then_inc(xt_landed[u], 16)

            load_t(0, 0)
            load_t(P, 1)
            for t, u, i, order in tiles(sp):
                if not (isinstance(t, int) and t >= NT - 2):
                    sp.wait_ge(work_ready, work.filled(t + 1))
                    load_t((t + 2) * P, u)


        @block.gpsimd
        def _(pool):
            ch = Chain(pool, pool_step)
            ch.link(pool.memset(masks[:, :, :], 0.0))
            ch.link(pool.affine_select(out=masks[:, :, 0:P], in_=masks[:, :, 0:P], compare_op=ALU.is_ge, fill=NEG, base=0,
                                       pattern=[[0, NT], [1, P]], channel_multiplier=-1))
            ch.link(pool.affine_select(out=masks[:, :, P:2 * P], in_=masks[:, :, P:2 * P], compare_op=ALU.is_ge, fill=NEG,
                                       base=0, pattern=[[0, NT], [-1, P]], channel_multiplier=1))
            for b in range(B):
                ins = pool.memset(masks[:, b * NT // B, 0:P], NEG)
                ch.link(ins)
            pool.wait_ge(weights_landed, 16 * n_weights)
            for n in ("q0", "q1", "k"):
                ch.link(pool.tensor_scalar(nsin[n][:, :], rope["sin_" + n][:, :], -1.0, 0.0, ALU.mult, ALU.add))
            pool.memset(v[1][:, :], 0.0).then_inc(pool_set, 1)

            def rotate(n, t, taken):
                if n == 0:
                    wait(pool, work_taken["act"], taken)
                    wait(pool, t_ready, turns.filled(t))
                    wait(pool, k_rotated, t + 1)
                ins = rotary(pool, 2, 1, "k", n, raw[:, 1, :])
                if n < 3:
                    ch.link(ins)
                else:
                    ins.then_inc(k_rotated, 1)

            pool.wait_ge(pool_set, 1)
            for n in range(4):
                rotate(n, -1, 4)
            start = ch.k
            for t, u, i, order in tiles(pool):
                ch.base, ch.k = start + t * 3, 0
                for s in order:
                    if s[0] == "N":
                        p = s[1]
                        wait(pool, inv_ready, PAIRS * t + p + 1)
                        pool.tensor_tensor(probs[:, p % 4, :, :], probs[:, p % 4, :, :],
                                           inv[:, :, p:p + 1].to_broadcast([P, 2, 2 * P]), ALU.mult).then_inc(p_ready, 1)
                    elif s[0] == "KR":
                        rotate(s[1], t, work.emptied("act", t) + 4)
                wait(pool, out_ready, t + 1)
                pool.dma_start(out_rows[bass.ds(t * P, P), :], res[:, u, :]).then_inc(stored[u], 16)
            for u in range(2):
                wait(pool, stored[u], 16 * (NT // 2))

        @block.tensor
        def _(pe):
            def bank_free(use, taken, order, t, n):
                if n < 2:
                    for who in ("act", "dve"):
                        wait(pe, taken[who], use.emptied(who, t))
                else:
                    before = [s for s in order if s[0] in use.kinds][n - 2]
                    who = emptier(before)
                    wait(pe, taken[who], use.emptied(who, t) + use.within(order, n - 1, who))

            def project(n, bank, src):
                for k in range(KD):
                    ins = pe.matmul(psw[bank][:, :], xnt[:, src, k, :], wqkv[:, k, n * CH:(n + 1) * CH],
                                    start=(k == 0), stop=(k == KD - 1))
                ins.then_inc(work_ready, 1)

            def turn(n, bank, tile):
                pe.wait_ge(q_rotated if n < 4 else k_rotated, tile + 1)
                for j in range(4):
                    pair = 4 * (n % 2) + j
                    ins = pe.transpose(pst[bank][:, j, :], rot[:, n // 2, pair * P:(pair + 1) * P], keep["identity"][:, :])
                ins.then_inc(t_ready, 1)

            pe.wait_ge(weights_landed, 16 * n_weights)
            pe.wait_ge(xt_landed[0], 16)
            for n in range(6):
                wait(pe, work_taken["act"], n - 1)
                project(n, n % 2, 0)
            for n in range(6):
                if n >= 2:
                    pe.wait_ge(turn_taken["act"], n - 1)
                turn(n, n % 2, 0)
            pe.wait_ge(pool_set, 1)
            for t, u, i, order in tiles(pe):
                w = r = 0
                for s in order:
                    if s[0] == "S":
                        p = s[1]
                        if p == 0:
                            for who in ("act", "dve"):
                                wait(pe, turn_taken[who], turns.emptied(who, t))
                        wait(pe, exp_ready, PAIRS * t + max(p - 1, 0))
                        pe.matmul(pss[p % 2][:, :, :], keep["identity16"][:, :],
                                  masks[:, bass.ds(t, 1), :].to_broadcast([P, 2, 2 * P]), start=True, stop=False)
                        pe.matmul(pss[p % 2][:, :, 0:P], qt[:, 1, p, :], kd[1 - u][:, p, :, :], start=False, stop=False)
                        pe.matmul(pss[p % 2][:, :, P:2 * P], qt[:, 0, p, :], kd[u][:, p, :, :], start=False, stop=True
                                  ).then_inc(s_ready, 1)
                    elif s[0] == "W":
                        bank_free(work, work_taken, order, t, w)
                        if s[1] == 0:
                            pe.wait_ge(xt_landed[1 - u], 16 * (i + 1 + u))
                        project(s[1], w % 2, 1 - u)
                        w += 1
                    elif s[0] == "E":
                        bank_free(work, work_taken, order, t, w)
                        for k in range(KD):
                            ins = pe.matmul(psw[w % 2][:, :], xnt[:, u, k, :], we[:, k, 2 * s[1]:2 * s[1] + 2, :],
                                            start=(k == 0), stop=(k == KD - 1))
                        ins.then_inc(work_ready, 1)
                        w += 1
                    elif s[0] == "T":
                        p = s[1]
                        wait(pe, p_ready, PAIRS * t + p + 1)
                        bank_free(turns, turn_taken, order, t, r)
                        for e in range(2):
                            for role in range(2):
                                ins = pe.transpose(pst[r % 2][:, 2 * e + role, :], probs[:, p % 4, e, role * P:(role + 1) * P],
                                                   keep["identity"][:, :])
                        ins.then_inc(t_ready, 1)
                        r += 1
                    elif s[0] == "R":
                        bank_free(turns, turn_taken, order, t, r)
                        turn(s[1], r % 2, t + 1)
                        r += 1
                    elif s[0] == "PV":
                        p = s[1]
                        n = turns.index(order, ("T", p))
                        who = emptier(("T", p))
                        wait(pe, turn_taken[who], turns.emptied(who, t) + turns.within(order, n + 1, who))
                        if p == 0:
                            pe.wait_ge(v_moved, t + 1)
                            wait(pe, ot_ready, 2 * t)
                        if p == 4:
                            wait(pe, ot_ready, 2 * t + 1)
                        for role in range(2):
                            for e in range(2):
                                h = 2 * p + e
                                ins = pe.matmul(pso[e * DH:(e + 1) * DH, p % 4, :], v[(u + 1 + role) % 2][:, h * DH:(h + 1) * DH],
                                                pt[:, p % 2, 2 * e + role, :], start=(role == 0), stop=(role == 1))
                        ins.then_inc(pv_done, 1)
                    elif s[0] == "OUT":
                        wait(pe, ot_ready, 2 * t + 2)
                        wait(pe, out_ready, t)
                        for p in range(PAIRS):
                            ins = pe.matmul(psy[:, :], ot[:, p, :], wout[:, p, :], start=(p == 0), stop=(p == PAIRS - 1))
                        ins.then_inc(y_ready, 1)

        @block.scalar
        def _(act):
            def take_work(n, t, filled, bank):
                act.wait_ge(work_ready, filled)
                wait(act, (q_rotated, k_rotated, v_moved)[n // 2], t + 1)
                act.copy(raw[:, n // 2, (n % 2) * CH:(n % 2 + 1) * CH], psw[bank][:, :]).then_inc(work_taken["act"], 1)

            def take_q(n, t, filled, bank):
                wait(act, t_ready, filled)
                wait(act, s_ready, PAIRS * (t + 1))
                act.copy(qt[:, n // 2, 4 * (n % 2):4 * (n % 2) + 4, :], pst[bank][:, :, :]).then_inc(turn_taken["act"], 1)

            for n in range(6):
                take_work(n, -1, n + 1, n % 2)
            for n in range(4):
                take_q(n, -1, n + 1, n % 2)
            for t, u, i, order in tiles(act):
                wait(act, out_ready, t)
                act.dma_start(x1[:, u, :], dram["x1"][bass.ds(t * P, P), :]).then_inc(x1_landed[u], 16)
                wait(act, pv_done, PAIRS * t)
                wait(act, work_taken["act"], work.emptied("act", t))
                act.copy(v[u][:, :], raw[:, 2, :]).then_inc(v_moved, 1)
                w = r = 0
                for s in order:
                    if s[0] == "S":
                        p = s[1]
                        if p == 0:
                            wait(act, inv_ready, PAIRS * t)
                        act.wait_ge(top_ready, PAIRS * t + p + 1)
                        wait(act, t_ready, turns.filled(t) + (turns.index(order, ("T", p - 4)) + 1 if p >= 4 else 0))
                        for e in range(2):
                            ins = act.activation(probs[:, p % 4, e, :], pss[p % 2][:, e, :], ACT.Exp, bias=top[:, e, p:p + 1],
                                                 accum_out=rows[:, e, p:p + 1])
                        ins.then_inc(exp_ready, 1)
                    elif s[0] == "W":
                        take_work(s[1], t, work.filled(t) + w + 1, w % 2)
                        w += 1
                    elif s[0] == "E":
                        w += 1
                    elif s[0] in ("T", "R"):
                        if s[0] == "T" and emptier(s) == "act":
                            wait(act, t_ready, turns.filled(t) + r + 1)
                            wait(act, pv_done, PAIRS * t + max(s[1] - 1, 0))
                            act.copy(pt[:, s[1] % 2, :, :], pst[r % 2][:, :, :]).then_inc(turn_taken["act"], 1)
                        elif s[0] == "R" and emptier(s) == "act":
                            take_q(s[1], t, turns.filled(t) + r + 1, r % 2)
                        r += 1
                    elif s[0] == "PV" and s[1] % 4 == 3:
                        half = s[1] // 4
                        wait(act, pv_done, PAIRS * t + s[1] + 1)
                        if half == 0:
                            wait(act, y_ready, t)
                        act.copy(ot[:, 4 * half:4 * half + 4, :], pso[:, :, :]).then_inc(ot_ready, 1)
                    if s == ("T", 6):
                        act.wait_ge(work_taken["dve"], work.emptied("dve", t + 1))
                        wait(act, out_ready, t)
                        act.activation(sig[:, :], y[:, :], ACT.Exp, scale=-1.0).then_inc(sig_ready, 1)

        @block.vector
        def _(vec):
            ch = Chain(vec, dve_step)
            for u in range(2):
                ins = vec.memset(kd[u][:, :, :, :], 0.0)
            ch.link(ins)

            def rotate(n, t, taken):
                if n == 0:
                    wait(vec, work_taken["act"], taken)
                    wait(vec, t_ready, turns.filled(t))
                    wait(vec, q_rotated, t + 1)
                ins = rotary(vec, n // 4, 0, f"q{n // 4}", n % 4, raw[:, 0, :])
                if n < 7:
                    ch.link(ins)
                else:
                    ins.then_inc(q_rotated, 1)

            def take_k(n, t, filled, bank, into):
                wait(vec, t_ready, filled)
                wait(vec, s_ready, PAIRS * (t + 1))
                for e in range(2):
                    ins = vec.tensor_copy(kd[into][e * DH:(e + 1) * DH, 4 * (n % 2):4 * (n % 2) + 4, e, :],
                                          pst[bank][e * DH:(e + 1) * DH, :, :])
                ins.then_inc(turn_taken["dve"], 1)

            vec.wait_ge(pool_set, 1)
            for n in range(8):
                rotate(n, -1, 2)
            for n in (4, 5):
                take_k(n, -1, n + 1, n % 2, 0)
            start = ch.k
            per_tile = 7 + 4 + 3
            for t, u, i, order in tiles(vec):
                ch.base, ch.k = start + t * per_tile, 0
                w = r = 0
                for s in order:
                    if s[0] == "S":
                        p = s[1]
                        vec.wait_ge(s_ready, PAIRS * t + p + 1)
                        vec.tensor_reduce(top[:, :, p], pss[p % 2][:, :, :], X, ALU.max, negate=True).then_inc(top_ready, 1)
                    elif s[0] == "N":
                        p = s[1]
                        if p == 0:
                            wait(vec, p_ready, PAIRS * t)
                        wait(vec, exp_ready, PAIRS * t + p + 1)
                        vec.reciprocal(inv[:, :, p], rows[:, :, p]).then_inc(inv_ready, 1)
                    elif s[0] == "QR":
                        rotate(s[1], t, work.emptied("act", t) + 2)
                    elif s[0] == "W":
                        w += 1
                    elif s[0] == "E":
                        n = s[1]
                        vec.wait_ge(work_ready, work.filled(t) + w + 1)
                        if n == 0:
                            wait(vec, out_ready, t)
                        for e in range(2):
                            weight = keep["coef"][:, bass.ds(t, 1), 2 * n + e:2 * n + e + 1].rearrange("p t e -> p (t e)")
                            part = psw[w % 2][:, e * D:(e + 1) * D]
                            if n == 0 and e == 0:
                                ins = vec.tensor_scalar(y[:, :], part, weight, None, ALU.mult)
                            else:
                                ins = vec.scalar_tensor_tensor(out=y[:, :], in0=part, scalar=weight, in1=y[:, :],
                                                               op0=ALU.mult, op1=ALU.add)
                            if e == 0:
                                ch.link(ins)
                        ins.then_inc(work_taken["dve"], 1)
                        w += 1
                        vec.wait_ge(work_taken["dve"], work.emptied("dve", t) + n + 1)
                    elif s[0] in ("T", "R"):
                        if s[0] == "T" and emptier(s) == "dve":
                            wait(vec, t_ready, turns.filled(t) + r + 1)
                            wait(vec, pv_done, PAIRS * t + max(s[1] - 1, 0))
                            vec.tensor_copy(pt[:, s[1] % 2, :, :], pst[r % 2][:, :, :]).then_inc(turn_taken["dve"], 1)
                        elif s[0] == "R" and emptier(s) == "dve":
                            take_k(s[1], t, turns.filled(t) + r + 1, r % 2, 1 - u)
                        r += 1
                    elif s[0] == "OUT":
                        vec.wait_ge(sig_ready, t + 1)
                        ch.link(vec.tensor_scalar(sig[:, :], sig[:, :], 1.0, None, ALU.add))
                        ch.link(vec.reciprocal(sig[:, :], sig[:, :]))
                        ch.link(vec.tensor_tensor(sig[:, :], sig[:, :], y[:, :], ALU.mult))
                        wait(vec, y_ready, t + 1)
                        wait(vec, stored[u], 16 * i)
                        ins = vec.tensor_tensor(res[:, u, :], psy[:, :], sig[:, :], ALU.mult)
                        ins.then_inc(res_step, 1)
                        vec.wait_ge(res_step, t + 1)
                        vec.wait_ge(x1_landed[u], 16 * (i + 1))
                        vec.tensor_tensor(res[:, u, :], res[:, u, :], x1[:, u, :], ALU.add).then_inc(out_ready, 1)


def make_program(nc, io, out, upto=7):
    dram = {
        "qk_parts": nc.dram_tensor("qk_parts", [2, 3, D, T], BF16).ap(),
        "v": nc.dram_tensor("v_rows", [T, D], F32).ap(),
        "expert_in": nc.dram_tensor("expert_in", [E * CAP0, D], F32).ap(),
        "expert_out": nc.dram_tensor("expert_out", [E * CAP0, D], F32).ap(),
        "attn0": nc.dram_tensor("attn0", [T, D], F32).ap(),
        "xnt1": nc.dram_tensor("xnt1", [KD, P, T], F32).ap(),
        "x1": nc.dram_tensor("x1", [T, D], F32).ap(),
    }
    with ExitStack() as ctx:
        st = Stage(nc, ctx)
        keep = {
            "identity": st.sb("identity", [P, P]),
            "identity16": st.sb("identity16", [P, P], BF16),
            "ones16": st.sb("ones16", [P, P], BF16),
            "zero16": st.sb("zero16", [P, P], BF16),
            "before16": st.sb("before16", [P, P], BF16),
            "mask_qk": st.sb("mask_qk", [P, P], BF16),
            "mask_kq": st.sb("mask_kq", [P, P], BF16),
            "expert": st.sb("expert", [P, E, NT]),
            "expert8": st.sb("expert8", [P, E, NT]),
            "running0": st.sb("running0", [P, E, NT]),
            "running1": st.sb("running1", [P, E, NT]),
            "gate": st.sb("gate", [P, NT]),
            "slot_get": st.sb("slot_get", [P, NT], U32),
            "slot_put": st.sb("slot_put", [P, NT], U32),
            "zero": st.sb("zero", [P, CH]),
            "coef": st.sb("coef", [P, NT, E]),
        }
        build_constants(nc, keep)
        with ExitStack() as front:
            keep["xn_all"] = Stage(nc, front).sb("xn_all", [P, NT, D])
            stage_project(nc, io, keep, dram)
            if upto >= 3:
                stage_attention(nc, io, keep, dram)
        if upto >= 4:
            stage_experts(nc, io, keep, dram)
        if upto >= 5:
            stage_join(nc, io, keep, dram)
        if upto >= 7:
            stage_windows(nc, io, keep, dram, out)
    return dram


def declare(nc, inputs):
    import numpy as np

    def turned(a):
        return np.ascontiguousarray(np.asarray(a).T)

    arrays = {
        "x": np.ascontiguousarray(inputs["L0_attn_x"]),
        "wq": turned(inputs["L0_attn_Wq"]), "wk": turned(inputs["L0_attn_Wk"]), "wv": turned(inputs["L0_attn_Wv"]),
        "wo": turned(inputs["L0_attn_Wo"]), "router0": np.ascontiguousarray(inputs["L0_ffn_router_w"]),
        "w1": np.ascontiguousarray(inputs["L0_ffn_w1"]), "w2": np.ascontiguousarray(inputs["L0_ffn_w2"]),
        "w_qkv": np.ascontiguousarray(inputs["L1_attn_W_qkv"]), "w_out": np.ascontiguousarray(inputs["L1_attn_W_out"]),
        "router1": turned(inputs["L1_ffn_Wr"]), "we": np.ascontiguousarray(inputs["L1_ffn_We"]),
    }
    arrays.update(tables())
    named = {f"in_{k}": v for k, v in arrays.items()}
    io = {k: nc.dram_tensor(f"in_{k}", list(v.shape), mybir.dt.from_np(v.dtype), kind="ExternalInput").ap()
          for k, v in arrays.items()}
    out = nc.dram_tensor("out_0", [B, S, D], F32, kind="ExternalOutput").ap()
    return named, io, out


def tables():
    import numpy as np

    inv_freq = (1.0 / np.power(np.float32(10000.0), np.arange(0, DH, 2, dtype=np.float32) / np.float32(DH))).astype(np.float32)
    angles = np.arange(2 * P, dtype=np.float32)[:, None] * inv_freq[None, :]
    cos, sin = np.cos(angles).astype(np.float32), np.sin(angles).astype(np.float32)
    scale = np.float32(DH ** -0.5)
    return {"cos_q": cos * scale, "sin_q": sin * scale, "cos_k": cos, "sin_k": sin}


def kernel(**inputs):
    import concourse.bacc as bacc
    from concourse.bass_utils import run_bass_kernel_spmd

    nc = bacc.Bacc("TRN2", target_bir_lowering=False, num_devices=1)
    arrays, io, out = declare(nc, inputs)
    make_program(nc, io, out)
    r = run_bass_kernel_spmd(nc, [arrays], core_ids=[0])
    return r.results[0]["out_0"]
```

```python
from contextlib import ExitStack

import concourse.bass as bass
from concourse import mybir

F32 = mybir.dt.float32
BF16 = mybir.dt.bfloat16
F32R = mybir.dt.float32r
U32 = mybir.dt.uint32
I32 = mybir.dt.int32
ALU = mybir.AluOpType
ACT = mybir.ActivationFunctionType
X = mybir.AxisListType.X

P = 128
B, S, D = 2, 2048, 256
T = B * S
NT = T // P
CH = 512
TC = CH // P
NC = T // CH
KD = D // P
E = 8
H = 16
EPS = 1e-5
NEG = -1e30

HD = D // H
F = 1024
FT = F // P
CAP0 = T // E
SKIP = 8192.0
GH = 4
HG = H // GH
KT = S // P
QC = S // CH
QR = 6 * HD
MR = QR + 3

DH = 64
J = H * DH
CAP1 = int(S * 2 / E * 1.5) + 1


def wait(eng, sem, value):
    if isinstance(value, int) and value <= 0:
        return
    eng.wait_ge(sem, value)


def rounds(eng, n):
    yield 0
    with eng.Fori(1, n) as i:
        yield i


def snap(eng, value):
    return value if isinstance(value, int) else eng.snap(value)


class Chain:

    def __init__(self, eng, sem, per_round=0):
        self.eng, self.sem, self.per, self.base, self.k = eng, sem, per_round, 0, 0

    def round(self, i):
        assert self.k in (0, self.per), self.k
        self.base, self.k = i * self.per, 0

    def after(self, n):
        assert self.k == self.per, self.k
        self.base, self.k = n * self.per, 0

    def link(self, ins):
        self.k += 1
        ins.then_inc(self.sem, 1)
        self.eng.wait_ge(self.sem, self.base + self.k)


class Stage:

    def __init__(self, nc, ctx, prefix=""):
        self.nc, self.ctx, self.prefix = nc, ctx, prefix

    def sb(self, name, shape, dt=F32):
        return self.ctx.enter_context(self.nc.sbuf_tensor(self.prefix + name, shape, dt))

    def ps(self, name, shape, dt=F32):
        return self.ctx.enter_context(self.nc.psum_tensor(self.prefix + name, shape, dt))

    def sem(self, name):
        return self.ctx.enter_context(self.nc.semaphore(self.prefix + name))


def build_constants(nc, keep):
    with ExitStack() as ctx:
        st = Stage(nc, ctx, "c_")
        pool_step = st.sem("const_step")
        block = ctx.enter_context(nc.Block())

        @block.gpsimd
        def _(pool):
            ch = Chain(pool, pool_step)
            ch.link(pool.memset(keep["identity"][:, :], 0.0))
            ch.link(pool.affine_select(out=keep["identity"][:, :], in_=keep["identity"][:, :], compare_op=ALU.not_equal,
                                       fill=1.0, base=0, pattern=[[-1, P]], channel_multiplier=1))
            ch.link(pool.tensor_copy(keep["identity16"][:, :], keep["identity"][:, :]))
            ch.link(pool.memset(keep["ones16"][:, :], 1.0))
            ch.link(pool.affine_select(out=keep["before16"][:, :], in_=keep["ones16"][:, :], compare_op=ALU.is_gt,
                                       fill=0.0, base=0, pattern=[[1, P]], channel_multiplier=-1))
            ch.link(pool.memset(keep["zero16"][:, :], 0.0))
            ch.link(pool.affine_select(out=keep["mask_qk"][:, :], in_=keep["zero16"][:, :], compare_op=ALU.is_ge,
                                       fill=NEG, base=0, pattern=[[-1, P]], channel_multiplier=1))
            ch.link(pool.affine_select(out=keep["mask_kq"][:, :], in_=keep["zero16"][:, :], compare_op=ALU.is_ge,
                                       fill=NEG, base=0, pattern=[[1, P]], channel_multiplier=-1))
            ch.link(pool.iota(keep["expert"][:, :, :], pattern=[[1, E], [0, NT]], base=0, channel_multiplier=0,
                              allow_small_or_imprecise_dtypes=True))
            ch.link(pool.iota(keep["expert8"][:, :, :], pattern=[[1, E], [0, NT]], base=E, channel_multiplier=0,
                              allow_small_or_imprecise_dtypes=True))
            for name, span in (("running0", NT), ("running1", NT // B)):
                ch.link(pool.memset(keep[name][:, :, :], 1.0))
                v = keep[name][:, :, :].rearrange("p e (b t) -> p (e b) t", t=span)
                ch.link(pool.memset(v[:, :, 0:1], 0.0))


def first_max(vec, ch, keep, logits, out_max, equal, first, onehot):
    ch.link(vec.tensor_reduce(out_max, logits.rearrange("p e t -> p t e"), X, ALU.max))
    ch.link(vec.tensor_tensor(equal, logits, out_max.unsqueeze(1).to_broadcast([P, E, NT]), ALU.is_equal))
    ch.link(vec.scalar_tensor_tensor(out=equal, in0=equal, scalar=-float(E), in1=keep["expert8"][:, :, :],
                                     op0=ALU.mult, op1=ALU.add))
    ch.link(vec.tensor_reduce(first, equal.rearrange("p e t -> p t e"), X, ALU.min))
    ch.link(vec.tensor_tensor(onehot, keep["expert"][:, :, :], first.unsqueeze(1).to_broadcast([P, E, NT]), ALU.is_equal))


def places(vec, ch, keep, running, tile_before, tile_total, total, scanned, place):
    flat = "p e t -> p (e t)"
    ch.link(vec.tensor_copy(total, tile_total.rearrange("p (e t) -> p e t", e=E)))
    ch.link(vec.tensor_tensor_scan(scanned.rearrange(flat), keep[running][:, :, :].rearrange(flat), total.rearrange(flat),
                                   0.0, ALU.mult, ALU.add))
    ch.link(vec.tensor_tensor(scanned, scanned, total, ALU.subtract))
    ch.link(vec.tensor_tensor(place, scanned, tile_before.rearrange("p (e t) -> p e t", e=E), ALU.add))


def ago(c):
    return c - 1


def chunks_skewed(eng, front, back):
    front(0, 0, 0)
    for i in rounds(eng, NC // 2 - 1):
        front(2 * i + 1, i, 1)
        back(2 * i, i, 0)
        front(2 * i + 2, i + 1, 0)
        back(2 * i + 1, i, 1)
    last = NC // 2 - 1
    front(NC - 1, last, 1)
    back(NC - 2, last, 0)
    back(NC - 1, last, 1)


def split_r(eng, hi, lo, src):
    return (lambda: eng.tensor_copy(hi, src)), (lambda: eng.tensor_tensor(lo, src, hi.bitcast(F32), ALU.subtract))


def inverse_root(vec, ch, out, value, half):
    ch.link(vec.tensor_scalar(value, value, EPS, None, ALU.add))
    ch.link(vec.tensor_scalar(half.bitcast(I32), value.bitcast(I32), 1, None, ALU.logical_shift_right))
    ch.link(vec.tensor_scalar(out.bitcast(I32), half.bitcast(I32), -1.0, float(0x5F3759DF), ALU.mult, ALU.add))
    for _ in range(3):
        ch.link(vec.scalar_tensor_tensor(out=half, in0=out, scalar=-0.5, in1=out, op0=ALU.mult, op1=ALU.mult))
        ch.link(vec.tensor_tensor(half, half, value, ALU.mult))
        ch.link(vec.scalar_tensor_tensor(out=out, in0=half, scalar=1.5, in1=out, op0=ALU.add, op1=ALU.mult))


ROOT_STEPS = 12
NORM_STEPS = ROOT_STEPS + 3


def layer_norm(vec, ch, src, dst, stats, mv, var, half, rstd, spare, before_write):
    for t in range(TC):
        ins = vec.bn_stats(stats[:, t, :], src[:, t, :])
    ch.link(ins)
    vec.memset(spare, 0.0)
    for t in range(TC):
        ins = vec.bn_aggr(mv[:, t, :], stats[:, t, :])
    ch.link(ins)
    ch.link(vec.tensor_copy(var, mv[:, :, 1]))
    inverse_root(vec, ch, rstd, var, half)
    before_write()
    for t in range(TC):
        ins = vec.tensor_scalar(dst[:, t, :], src[:, t, :], mv[:, t, 0:1], rstd[:, t:t + 1], ALU.subtract, ALU.mult)
    return ins


def stage_project(nc, io, keep, dram):
    with ExitStack() as ctx:
        st = Stage(nc, ctx, "p_")
        wqk = st.sb("wqk", [P, 2, KD, D])
        wvr = st.sb("wvr", [P, KD, D + E])
        wqk_r = [st.sb(f"wqk_r{r}", [P, 2, KD, D], F32R) for r in range(2)]
        wvr_r = [st.sb(f"wvr_r{r}", [P, KD, D + E], F32R) for r in range(2)]
        xin = st.sb("xin", [P, 2, TC, D])
        stats = st.sb("stats", [P, 2, TC, 6])
        mv = st.sb("mv", [P, 2, TC, 2])
        var = st.sb("var", [P, 2, TC])
        half = st.sb("half", [P, 2, TC])
        rstd = st.sb("rstd", [P, 2, TC])
        xn = st.sb("xn", [P, 2, TC, D])
        xnt = [[st.sb(f"xnt{r}_{u}", [P, KD, CH], F32R) for r in range(2)] for u in range(2)]
        rest = st.sb("rest", [P, 4, CH])
        parts = st.sb("parts", [P, 4, 3, CH], BF16)
        vout = st.sb("vout", [P, 2, TC, D])
        spare = st.sb("spare", [P, 1])
        logits = st.sb("logits", [P, E, NT])
        top = st.sb("top", [P, NT])
        equal = st.sb("equal", [P, E, NT])
        first = st.sb("first", [P, NT])
        onehot = st.sb("onehot", [P, E, NT])
        onehot16 = st.sb("onehot16", [P, E, NT], BF16)
        shifted = st.sb("shifted", [P, E, NT])
        expd = st.sb("expd", [P, E, NT])
        total = st.sb("total", [P, E, NT])
        scanned = st.sb("scanned", [P, E, NT])
        place = st.sb("place", [P, E, NT])
        small = st.sb("small", [P, 6, NT])
        pst = [st.ps(f"pst{k}", [P, CH]) for k in range(KD)]
        psq = [st.ps(f"psq{k}", [P, CH]) for k in range(4)]
        psv = [st.ps(f"psv{k}", [P, CH]) for k in range(2)]

        weights_landed = st.sem("weights_landed")
        x_landed = [st.sem(f"x_landed{u}") for u in range(2)]
        weights_split, xn_ready = st.sem("weights_split"), st.sem("xn_ready")
        turned, high_ready, xnt_ready, xn_kept = (st.sem("turned"), st.sem("high_ready"), st.sem("xnt_ready"),
                                                  st.sem("xn_kept"))
        qk_ready, first_part, rest_ready = st.sem("qk_ready"), st.sem("first_part"), st.sem("rest_ready")
        second_part, parts_ready = st.sem("second_part"), st.sem("parts_ready")
        parts_stored = [st.sem(f"parts_stored{k}") for k in range(4)]
        v_ready, v_copied = st.sem("v_ready"), st.sem("v_copied")
        v_stored = [st.sem(f"v_stored{u}") for u in range(2)]
        dve_step = st.sem("dve_step")
        zeroed = st.sem("zeroed")
        onehot_ready, counted, shifted_ready, exp_ready = (st.sem("onehot_ready"), st.sem("counted"),
                                                           st.sem("shifted_ready"), st.sem("exp_ready"))
        block = ctx.enter_context(nc.Block())
        x_rows = io["x"].rearrange("b s d -> (b s) d")

        @block.gpsimd
        def _(pool):
            def keep_copy(c, n, u):
                pool.wait_ge(xn_ready, c + 1)
                pool.tensor_copy(keep["xn_all"][:, bass.ds(c * TC, TC), :], xn[:, u, :, :]).then_inc(xn_kept, 1)

            chunks_skewed(pool, keep_copy, lambda c, n, u: None)

        @block.sync
        def _(sp):
            def load(u, c):
                sp.dma_start(xin[:, u, :, :], x_rows[bass.ds(c * CH, CH), :].rearrange("(t p) d -> p t d", p=P)
                             ).then_inc(x_landed[u], 16)

            load(0, 0)
            load(1, 1)
            for n, name in enumerate(("wq", "wk")):
                sp.dma_start(wqk[:, n, :, :], io[name].rearrange("(k p) n -> p k n", p=P)).then_inc(weights_landed, 16)
            sp.dma_start(wvr[:, :, 0:D], io["wv"].rearrange("(k p) n -> p k n", p=P)).then_inc(weights_landed, 16)
            sp.dma_start(wvr[:, :, D:D + E], io["router0"].rearrange("(k p) n -> p k n", p=P)).then_inc(weights_landed, 16)
            with sp.Fori(1, NC // 2) as i:
                for u in range(2):
                    at = snap(sp, (2 * i + u) * CH)
                    sp.wait_ge(xn_ready, 2 * i + u - 1)
                    sp.dma_start(xin[:, u, :, :], x_rows[bass.ds(at, CH), :].rearrange("(t p) d -> p t d", p=P)
                                 ).then_inc(x_landed[u], 16)

        @block.vector
        def _(vec):
            vec.memset(keep["zero"][:, :], 0.0).then_inc(zeroed, 1)
            ch = Chain(vec, dve_step)

            def split_weights():
                vec.wait_ge(weights_landed, 64)
                for hi, lo, src in ((wqk_r[0][:, :, :, :], wqk_r[1][:, :, :, :], wqk[:, :, :, :]),
                                    (wvr_r[0][:, :, :], wvr_r[1][:, :, :], wvr[:, :, :])):
                    high, low = split_r(vec, hi, lo, src)
                    ch.link(high())
                    low().then_inc(weights_split, 1)

            def front(c, n, u):
                vec.wait_ge(x_landed[u], 16 * (n + 1))

                def before_write():
                    wait(vec, turned, ago(c))
                    wait(vec, xn_kept, ago(c))

                ch.base, ch.k = start + NORM_STEPS * c, 0
                layer_norm(vec, ch, xin[:, u, :, :], xn[:, u, :, :], stats[:, u, :, :], mv[:, u, :, :], var[:, u, :],
                           half[:, u, :], rstd[:, u, :], spare[:, :], before_write).then_inc(xn_ready, 1)
                vec.wait_ge(high_ready, c + 1)
                wait(vec, v_ready, TC * ago(c))
                for k in range(KD):
                    ins = vec.tensor_tensor(xnt[u][1][:, k, :], pst[k][:, :], xnt[u][0][:, k, :].bitcast(F32), ALU.subtract)
                ins.then_inc(xnt_ready, 1)

            def back(c, n, u):
                def rest_of(m):
                    vec.wait_ge(first_part, 4 * c + m + 1)
                    vec.scalar_tensor_tensor(out=rest[:, m, :], in0=psq[m][:, :], scalar=HD ** -0.5 if m < 2 else 1.0,
                                             in1=parts[:, m, 0, :], op0=ALU.mult, op1=ALU.subtract).then_inc(rest_ready, 1)

                def third(m):
                    vec.wait_ge(second_part, 4 * c + m + 1)
                    vec.tensor_tensor(parts[:, m, 2, :], rest[:, m, :], parts[:, m, 1, :], ALU.subtract
                                      ).then_inc(parts_ready, 1)

                for m in range(5):
                    if m < 4:
                        rest_of(m)
                    if m:
                        third(m - 1)

            split_weights()
            start = ch.k
            chunks_skewed(vec, front, back)
            ch.base, ch.k = start + NORM_STEPS * NC, 0

            vec.wait_ge(v_copied, NT)
            L = logits[:, :, :]
            first_max(vec, ch, keep, L, top[:, :], equal[:, :, :], first[:, :], onehot[:, :, :])
            vec.tensor_copy(onehot16[:, :, :], onehot[:, :, :]).then_inc(onehot_ready, 1)
            vec.tensor_tensor(shifted[:, :, :], L, top[:, :].unsqueeze(1).to_broadcast([P, E, NT]), ALU.subtract
                              ).then_inc(shifted_ready, 1)
            vec.wait_ge(exp_ready, 1)
            den, kept, chosen, clipped, slot = (small[:, k, :] for k in range(5))
            ch.link(vec.tensor_reduce(den, expd[:, :, :].rearrange("p e t -> p t e"), X, ALU.add))
            ch.link(vec.reciprocal(keep["gate"][:, :], den))
            vec.wait_ge(counted, 1)
            places(vec, ch, keep, "running0", psq[0][:, 0:E * NT], psq[1][:, 0:E * NT], total[:, :, :], scanned[:, :, :],
                   place[:, :, :])
            ch.link(vec.tensor_tensor(place[:, :, :], place[:, :, :], onehot[:, :, :], ALU.mult))
            ch.link(vec.tensor_reduce(chosen, place[:, :, :].rearrange("p e t -> p t e"), X, ALU.add))
            ch.link(vec.tensor_scalar(kept, chosen, float(CAP0), None, ALU.is_lt))
            ch.link(vec.tensor_tensor(keep["gate"][:, :], keep["gate"][:, :], kept, ALU.mult))
            ch.link(vec.tensor_scalar(clipped, chosen, float(CAP0 - 1), None, ALU.min))
            ch.link(vec.scalar_tensor_tensor(out=slot, in0=first[:, :], scalar=float(CAP0), in1=clipped,
                                             op0=ALU.mult, op1=ALU.add))
            ch.link(vec.tensor_copy(keep["slot_get"][:, :], slot))
            ch.link(vec.scalar_tensor_tensor(out=clipped, in0=kept, scalar=-SKIP, in1=slot, op0=ALU.mult, op1=ALU.add))
            ch.link(vec.tensor_scalar(keep["slot_put"][:, :], clipped, SKIP, None, ALU.add))

        @block.scalar
        def _(act):
            def front(c, n, u):
                act.wait_ge(turned, c + 1)
                wait(act, v_ready, TC * ago(c))
                act.copy(xnt[u][0][:, 0, :], pst[0][:, :])
                act.copy(xnt[u][0][:, 1, :], pst[1][:, :]).then_inc(high_ready, 1)

            def back(c, n, u):
                def first(m):
                    act.wait_ge(qk_ready, 4 * c + m + 1)
                    wait(act, parts_stored[m], 16 * c)
                    act.activation(parts[:, m, 0, :], psq[m][:, :], ACT.Copy, scale=HD ** -0.5 if m < 2 else 1.0
                                   ).then_inc(first_part, 1)

                def second(m):
                    act.wait_ge(rest_ready, 4 * c + m + 1)
                    act.copy(parts[:, m, 1, :], rest[:, m, :]).then_inc(second_part, 1)

                def store(m):
                    act.wait_ge(parts_ready, 4 * c + m + 1)
                    rows = dram["qk_parts"][m // 2, :, (m % 2) * P:(m % 2 + 1) * P, bass.ds(c * CH, CH)]
                    act.dma_start(rows.rearrange("r p n -> p r n"), parts[:, m, :, :]).then_inc(parts_stored[m], 16)

                for m in range(5):
                    if m < 4:
                        first(m)
                    if m:
                        second(m - 1)
                for t in range(TC):
                    act.wait_ge(v_ready, TC * c + t + 1)
                    if t == 0:
                        wait(act, v_stored[u], 16 * n)
                    act.copy(vout[:, u, t, :], psv[t % 2][:, 0:D])
                    act.copy(logits[:, :, bass.ds(c * TC + t, 1)].rearrange("p e t -> p (e t)"),
                             psv[t % 2][:, D:D + E]).then_inc(v_copied, 1)
                for m in range(4):
                    store(m)
                act.wait_ge(v_copied, TC * (c + 1))
                act.dma_start(dram["v"][bass.ds(c * CH, CH), :].rearrange("(t p) d -> p t d", p=P), vout[:, u, :, :]
                              ).then_inc(v_stored[u], 16)

            chunks_skewed(act, front, back)
            for m in range(4):
                act.wait_ge(parts_stored[m], 16 * NC)
            for u in range(2):
                act.wait_ge(v_stored[u], 16 * (NC // 2))
            act.wait_ge(shifted_ready, 1)
            act.activation(expd[:, :, :], shifted[:, :, :], ACT.Exp).then_inc(exp_ready, 1)

        @block.tensor
        def _(pe):
            def product(bank, stationary, moving):
                pairs = [(k, a, b) for k in range(KD) for a, b in ((0, 0), (1, 0), (0, 1))]
                for n, (k, a, b) in enumerate(pairs):
                    ins = pe.matmul(bank, stationary(a, k), moving(b, k), start=(n == 0), stop=(n == len(pairs) - 1))
                return ins

            def front(c, n, u):
                pe.wait_ge(xn_ready, c + 1)
                wait(pe, xnt_ready, c)
                for t in range(TC):
                    for k in range(KD):
                        ins = pe.transpose(pst[k][:, t * P:(t + 1) * P], xn[:, u, t, k * P:(k + 1) * P],
                                           keep["identity"][:, :])
                ins.then_inc(turned, 1)

            def back(c, n, u):
                pe.wait_ge(xnt_ready, c + 1)
                for m in range(4):
                    wait(pe, rest_ready, 4 * (c - 1) + m + 1)
                    product(psq[m][:, :], lambda r, k: wqk_r[r][:, m // 2, k, (m % 2) * P:(m % 2 + 1) * P],
                            lambda r, k: xnt[u][r][:, k, :]).then_inc(qk_ready, 1)
                for t in range(TC):
                    wait(pe, v_copied, TC * c + t - 1)
                    product(psv[t % 2][:, 0:D + E], lambda r, k: xnt[u][r][:, k, t * P:(t + 1) * P],
                            lambda r, k: wvr_r[r][:, k, :]).then_inc(v_ready, 1)

            pe.wait_ge(weights_split, 2)
            chunks_skewed(pe, front, back)
            pe.wait_ge(onehot_ready, 1)
            pe.wait_ge(parts_ready, 4 * NC)
            oh = onehot16[:, :, :].rearrange("p e t -> p (e t)")
            pe.matmul(psq[0][:, 0:E * NT], keep["before16"][:, :], oh, start=True, stop=True)
            pe.matmul(psq[1][:, 0:E * NT], keep["ones16"][:, :], oh, start=True, stop=True).then_inc(counted, 1)


def attention_steps():
    maxima, ends = [], []
    for c in range(QC):
        for h in range(GH):
            for i in range(TC * c, TC * c + TC):
                for k in range(c + 1):
                    maxima.append((h, i, k))
        ends.append(len(maxima))

    def cost(u):
        return 90 + min(CH, (u[1] + 1) * P - u[2] * CH)

    def width(c, j):
        return CH - max(0, j - TC * c) * P

    whole = sum(cost(u) for u in maxima)
    lead, at = 0, 0
    while at < LEAD * whole:
        at += cost(maxima[lead])
        lead += 1

    def flow(lo, hi, dg):
        for n in range(lo, hi):
            yield ("A", dg, *maxima[n])
            if n + 1 in ends:
                c = ends.index(n + 1)
                yield ("M", dg, c)
                yield ("MT", dg, c)

    def weave(ahead):
        pairs = [(c, j) for c in range(QC) for j in range(TC * (c + 1))]
        total = sum(width(*p) for p in pairs) * GH
        ahead, steps, done, ahead_done, late = list(ahead), [], 0, 0, []

        def advance():
            nonlocal ahead_done
            while ahead and ahead_done * total < done * whole:
                u = ahead.pop(0)
                if u[0] == "A":
                    ahead_done += cost(u[2:])
                if u[0] == "MT":
                    late.append([u, 6])
                else:
                    steps.append(u)

        for n, (c, j) in enumerate(pairs):
            for h in range(GH):
                steps.append(("S", c, j, h))
                done += width(c, j)
                advance()
                for item in late:
                    item[1] -= 1
                while late and late[0][1] <= 0:
                    steps.append(late.pop(0)[0])
            if n:
                pc, pj = pairs[n - 1]
                steps.append(("PV", pc, pj))
                if pj == TC * (pc + 1) - 1:
                    steps.append(("COPY", pc))
                    late.append([("O", pc), 6])
        c, j = pairs[-1]
        steps += ahead + [u for u, _ in late] + [("PV", c, j), ("COPY", c), ("O", c)]
        return steps

    head = list(flow(0, lead, 0))
    stream = list(flow(lead, len(maxima), 0)) + list(flow(0, lead, 1))
    return head, weave(stream), weave(flow(lead, len(maxima), 0))


RING = 3


LEAD = 0.5


def stage_attention(nc, io, keep, dram):
    head, steps, last_steps = attention_steps()
    in_ring = ("A", "MT", "O")
    r_head, n_ring = (sum(u[0] in in_ring for u in order) for order in (head, steps))
    m_head = sum(u[0] == "M" for u in head)
    n_s = sum(u[0] == "S" for u in steps) // 2
    n_pv = sum(u[0] == "PV" for u in steps)
    parts_q, parts_k = (0, 0, 1, 1, 0, 2), (0, 1, 0, 1, 2, 0)
    n_loads = len(parts_q) * QC + len(parts_k)
    with ExitStack() as ctx:
        st = Stage(nc, ctx, "a_")
        qa = [st.sb(f"qa{u}", [MR, QC, GH, CH], BF16) for u in range(2)]
        kb = [st.sb(f"kb{u}", [MR, GH, S], BF16) for u in range(2)]
        vg = [st.sb(f"vg{u}", [P, KT, GH, 32]) for u in range(2)]
        probs = st.sb("probs", [P, 4, 2, CH])
        best = st.sb("best", [P, QC, GH * TC, QC])
        neg = st.sb("neg", [P, GH * TC])
        neg_rest = st.sb("neg_rest", [P, GH * TC])
        neg_parts = st.sb("neg_parts", [P, P // (GH * TC), GH * TC], BF16)
        neg_rows = st.sb("neg_rows", [3 * GH * TC, 2, P], BF16)
        sums = st.sb("sums", [P, CH])
        inv = st.sb("inv", [P, TC, GH])
        oout = st.sb("oout", [P, 2, TC, GH, HD])
        ring = [st.ps(f"ring{k}", [P, CH]) for k in range(RING)]
        pss = [st.ps(f"pss{k}", [P, 2, CH]) for k in range(2)]
        acc = st.ps("acc", [P, CH])

        loaded = [st.sem(f"loaded{u}") for u in range(2)]
        v_loaded = [st.sem(f"v_loaded{u}") for u in range(2)]
        set_up, ones_set = st.sem("set_up"), st.sem("ones_set")
        ring_full, ring_taken = st.sem("ring_full"), st.sem("ring_taken")
        s_ready, exp_done, pv_done = st.sem("s_ready"), st.sem("exp_done"), st.sem("pv_done")
        sums_copied = st.sem("sums_copied")
        m_split = st.sem("m_split")
        m_landed = [st.sem(f"m_landed{c}") for c in range(QC)]
        o_stored = [st.sem(f"o_stored{c}") for c in range(2)]
        dve_step = st.sem("dve_step")
        cleared, scattered = st.sem("cleared"), st.sem("scattered")
        block = ctx.enter_context(nc.Block())

        def bank_of(u, r):
            assert 2 * n_ring % RING == 0
            return ring[(r_head + u * n_ring + r) % RING]

        primed = 1

        def groups(eng):
            with eng.Fori(0, HG - 1) as i:
                for u in range(2):
                    yield 2 * i + u, i, u, steps
            for u in range(2):
                yield 2 * (HG - 1) + u, HG - 1, u, (steps, last_steps)[u]

        def load_q(eng, first, u):
            for c in range(QC):
                for r, part in enumerate(parts_q):
                    eng.dma_start(qa[u][r * HD:(r + 1) * HD, c, :, :],
                                  dram["qk_parts"][0, part, bass.ds(first, GH * HD), u * S + c * CH:u * S + (c + 1) * CH]
                                  .rearrange("(h d) n -> d h n", d=HD)).then_inc(loaded[u], 16)

        def load_k(eng, first, u):
            for r, part in enumerate(parts_k):
                eng.dma_start(kb[u][r * HD:(r + 1) * HD, :, :],
                              dram["qk_parts"][1, part, bass.ds(first, GH * HD), u * S:(u + 1) * S]
                              .rearrange("(h d) n -> d h n", d=HD)).then_inc(loaded[u], 16)

        @block.gpsimd
        def _(pool):
            ch = Chain(pool, set_up)
            for u in range(2):
                ch.link(pool.memset(vg[u][:, :, :, :], 0.0))
                ch.link(pool.memset(vg[u][:, :, :, HD:HD + 1], 1.0))
            table = dram["expert_in"].rearrange("(p a) d -> p (a d)", p=P)
            n = table.shape[1] // CH
            for k in range(n):
                pool.dma_start(table[:, k * CH:(k + 1) * CH], keep["zero"][:, :]).then_inc(cleared, 16)
            pool.wait_ge(cleared, 16 * n)
            for t in range(NT):
                pool.indirect_dma_start(dram["expert_in"], bass.IndirectOffsetOnAxis(ap=keep["slot_put"][:, t:t + 1], axis=0),
                                        keep["xn_all"][:, t, :], None, bounds_check=E * CAP0 - 1, oob_is_err=False
                                        ).then_inc(scattered, 16)
            pool.wait_ge(scattered, 16 * NT)

        @block.sync
        def _(sp):
            def load(first, u):
                load_q(sp, first, u)
                load_k(sp, first, u)
                load_v(first, u)

            def load_v(first, u):
                for h in range(GH):
                    sp.dma_start(vg[u][:, :, h, 0:HD],
                                 dram["v"][u * S:(u + 1) * S, bass.ds(first + h * HD, HD)]
                                 .rearrange("(j p) d -> p j d", p=P)).then_inc(v_loaded[u], 16)

            def store_rows(u, c, r):
                sp.wait_ge(ring_taken, r + 1)
                for part in range(3):
                    sp.dma_start(qa[u][QR + part:QR + part + 1, c, :, :].rearrange("o h (i q) -> o (h i) q", q=P),
                                 neg_rows[part * GH * TC:(part + 1) * GH * TC, c % 2, :]
                                 ).then_inc(m_landed[c], 16)

            load_q(sp, 0, 0)
            sp.wait_ge(set_up, 4)
            load_v(0, 0)
            for r, s in enumerate(s for s in head if s[0] in in_ring):
                if s[0] == "MT":
                    store_rows(0, s[2], r)
            for g, i, u, order in groups(sp):
                if not (isinstance(g, int) and g == 2 * HG - 1):
                    first = snap(sp, (i + u) * GH * HD)
                    sp.wait_ge(pv_done, primed + g * n_pv)
                    load(first, 1 - u)
                for r, s in enumerate(s for s in order if s[0] in in_ring):
                    if s[0] == "MT":
                        store_rows((u + s[1]) % 2, s[2], r_head + g * n_ring + r)
            for c in range(2):
                sp.wait_ge(o_stored[c], 16 * (primed + QC * HG))

        @block.tensor
        def _(pe):
            def a_step(u, s, r, bank):
                _, dg, h, i, k = s
                keys = min(CH, (i + 1) * P - k * CH)
                diagonal = k == i // TC
                wait(pe, ring_taken, r + 1 - RING)
                ins = pe.matmul(bank[:, 0:keys], qa[u][0:QR, i // TC, h, (i % TC) * P:(i % TC + 1) * P], kb[u][0:QR, h, k * CH:k * CH + keys],
                                start=True, stop=not diagonal)
                if diagonal:
                    ins = pe.matmul(bank[:, keys - P:keys], keep["identity16"][:, :], keep["mask_qk"][:, :],
                                    start=False, stop=True)
                ins.then_inc(ring_full, 1)

            def m_turn(n, r, bank):
                pe.wait_ge(m_split, n + 1)
                wait(pe, ring_taken, r + 1 - RING)
                pe.transpose(bank[:, 0:P // 2].bitcast(BF16), neg_parts[:, :, :].rearrange("p r n -> p (r n)"),
                             keep["identity16"][:, :]).then_inc(ring_full, 1)

            pe.nop().then_inc(pv_done, primed)
            pe.wait_ge(loaded[0], 16 * n_loads)
            m = 0
            for r, s in enumerate(s for s in head if s[0] in in_ring):
                if s[0] == "A":
                    a_step(0, s, r, ring[r % RING])
                if s[0] == "MT":
                    m_turn(m, r, ring[r % RING])
                    m += 1
            pe.wait_ge(set_up, 4)
            pe.wait_ge(ones_set, 1)
            for g, i, u, order in groups(pe):
                idx = pv = m = r = 0
                next_seen = False
                for s in order:
                    if s[0] == "A":
                        if s[1] == 1 and not next_seen:
                            next_seen = True
                            pe.wait_ge(loaded[1 - u], 16 * n_loads * (i + 1 + u))
                        a_step((u + s[1]) % 2, s, r_head + g * n_ring + r, bank_of(u, r))
                        r += 1
                    elif s[0] == "MT":
                        m_turn(m_head + g * QC + m, r_head + g * n_ring + r, bank_of(u, r))
                        m += 1
                        r += 1
                    elif s[0] == "S":
                        _, c, j, h = s
                        e = h % 2
                        lo = max(0, j - TC * c) * P
                        if j == 0 and h == 0:
                            pe.wait_ge(m_landed[c], 48 * (g + 1))
                        if e == 0:
                            pe.wait_ge(exp_done, primed + g * n_s + max(idx - 1, 0))
                        ins = pe.matmul(pss[idx % 2][:, e, lo:CH], kb[u][0:MR, h, j * P:(j + 1) * P],
                                        qa[u][0:MR, c, h, lo:CH], start=True, stop=(j < TC * c))
                        if j >= TC * c:
                            ins = pe.matmul(pss[idx % 2][:, e, lo:lo + P], keep["identity16"][:, :],
                                            keep["mask_kq"][:, :], start=False, stop=True)
                        if e == 1:
                            ins.then_inc(s_ready, 1)
                            idx += 1
                    elif s[0] == "PV":
                        _, c, j = s
                        lo = max(0, j - TC * c) * P
                        pe.wait_ge(exp_done, primed + g * n_s + 2 * pv + 2)
                        if c == 0 and j == 0:
                            pe.wait_ge(v_loaded[u], 16 * GH * (i + 1))
                        if j == 0:
                            pe.wait_ge(sums_copied, primed + g * QC + c)
                        for h in range(GH):
                            ins = pe.matmul(acc[32 * h:32 * h + 32, lo:CH], vg[u][:, j, h, :],
                                            probs[:, 2 * (pv % 2) + h // 2, h % 2, lo:CH],
                                            start=(j == 0), stop=(j == TC * (c + 1) - 1))
                        ins.then_inc(pv_done, 1)
                        pv += 1
                    elif s[0] == "O":
                        c = s[1]
                        pe.wait_ge(sums_copied, primed + g * QC + c + 1)
                        pe.wait_ge(ring_taken, r_head + g * n_ring + r + 1 - RING)
                        for t in range(TC):
                            ins = pe.transpose(bank_of(u, r)[:, t * P:(t + 1) * P], sums[:, t * P:(t + 1) * P],
                                               keep["identity"][:, :])
                        ins.then_inc(ring_full, 1)
                        r += 1

        @block.scalar
        def _(act):
            def store(g, i, u, c, r):
                act.wait_ge(ring_taken, r_head + g * n_ring + r + 1)
                act.dma_start(dram["attn0"][u * S + c * CH:u * S + (c + 1) * CH, bass.ds(i * GH * HD, GH * HD)]
                              .rearrange("(t p) d -> p t d", p=P),
                              oout[:, c % 2, :, :, :].rearrange("p t h d -> p t (h d)")).then_inc(o_stored[c % 2], 16)

            load_k(act, 0, 0)
            act.nop().then_inc(exp_done, primed)
            act.nop().then_inc(sums_copied, primed)
            for c in range(2):
                act.nop().then_inc(o_stored[c], 16 * primed)
            for g, i, u, order in groups(act):
                idx = r = pv = r_turn = 0
                turned_at = None
                for s in order:
                    if turned_at and idx >= turned_at[0] + 3:
                        store(g, i, u, *turned_at[1:])
                        turned_at = None
                    if s[0] == "O":
                        turned_at, r_turn = (idx, s[1], r), r + 1
                    if s[0] == "S" and s[3] % 2 == 1:
                        _, c, j, h = s
                        lo = max(0, j - TC * c) * P
                        act.wait_ge(s_ready, g * n_s + idx + 1)
                        act.wait_ge(pv_done, primed + g * n_pv + max(idx // 2 - 1, 0))
                        act.activation(probs[:, idx % 4, :, lo:CH], pss[idx % 2][:, :, lo:CH], ACT.Exp).then_inc(exp_done, 1)
                        idx += 1
                    elif s[0] == "PV":
                        pv += 1
                    elif s[0] == "COPY":
                        act.wait_ge(pv_done, primed + g * n_pv + pv)
                        act.wait_ge(ring_full, r_head + g * n_ring + r_turn)
                        act.copy(sums[:, :], acc[:, :]).then_inc(sums_copied, 1)
                    elif s[0] in in_ring:
                        r += 1
                store(g, i, u, *turned_at[1:])

        @block.vector
        def _(vec):
            ch = Chain(vec, dve_step)
            per_group = 4 * QC + QC
            ch_head = 4 * m_head + 1

            def take(s, r, bank):
                _, _, h, i, k = s
                keys = min(CH, (i + 1) * P - k * CH)
                vec.wait_ge(ring_full, r + 1)
                vec.tensor_reduce(best[:, i // TC, h * TC + i % TC, k:k + 1], bank[:, 0:keys], X, ALU.max
                                  ).then_inc(ring_taken, 1)

            def split(c, r):
                vec.wait_ge(ring_taken, r)
                ch.link(vec.tensor_reduce(neg[:, :], best[:, c, :, 0:c + 1], X, ALU.max, negate=True))
                ch.link(vec.tensor_copy(neg_parts[:, 0, :], neg[:, :]))
                ch.link(vec.tensor_tensor(neg_rest[:, :], neg[:, :], neg_parts[:, 0, :], ALU.subtract))
                ch.link(vec.tensor_copy(neg_parts[:, 1, :], neg_rest[:, :]))
                vec.tensor_tensor(neg_parts[:, 2, :], neg_rest[:, :], neg_parts[:, 1, :], ALU.subtract).then_inc(m_split, 1)

            def take_rows(c, r, bank, landed):
                vec.wait_ge(ring_full, r + 1)
                wait(vec, m_landed[(c - 2) % QC], landed)
                vec.tensor_copy(neg_rows[:, c % 2, :], bank[0:3 * GH * TC, 0:P // 2].bitcast(BF16)).then_inc(ring_taken, 1)

            for u in range(2):
                ins = vec.memset(kb[u][QR:MR, :, :], 1.0)
            ins.then_inc(ones_set, 1)
            ch.link(vec.memset(neg_parts[:, :, :], 0.0))
            r = 0
            for s in head:
                if s[0] == "A":
                    take(s, r, ring[r % RING])
                elif s[0] == "M":
                    split(s[2], r)
                elif s[0] == "MT":
                    take_rows(s[2], r, ring[r % RING], 0)
                r += s[0] in in_ring
            for g, i, u, order in groups(vec):
                ch.base, ch.k = ch_head + g * per_group, 0
                r = 0
                for s in order:
                    at, bank = r_head + g * n_ring + r, bank_of(u, r)
                    if s[0] == "A":
                        take(s, at, bank)
                    elif s[0] == "M":
                        split(s[2], at)
                    elif s[0] == "MT":
                        _, dg, c = s
                        take_rows(c, at, bank, 48 * (g + dg + (c >= 2)))
                    elif s[0] == "O":
                        c = s[1]
                        vec.wait_ge(ring_full, at + 1)
                        t4 = bank[:, :].rearrange("p (t h x) -> p t h x", t=TC, h=GH)
                        ch.link(vec.reciprocal(inv[:, :, :], t4[:, :, :, HD:HD + 1].rearrange("p t h x -> p t (h x)")))
                        vec.wait_ge(o_stored[c % 2], 16 * (primed + 2 * g + c // 2))
                        vec.tensor_tensor(oout[:, c % 2, :, :, :], t4[:, :, :, 0:HD],
                                          inv[:, :, :].unsqueeze(3).to_broadcast([P, TC, GH, HD]), ALU.mult
                                          ).then_inc(ring_taken, 1)
                    r += s[0] in in_ring


def stage_experts(nc, io, keep, dram):
    ST = CAP0 // P
    with ExitStack() as ctx:
        st = Stage(nc, ctx, "e_")
        w1 = [st.sb(f"w1_{u}", [P, KD, F]) for u in range(2)]
        w2 = [st.sb(f"w2_{u}", [P, FT, D]) for u in range(2)]
        rows = st.sb("rows", [P, 2, ST, D])
        rows_t = st.sb("rows_t", [P, 2, KD, CAP0])
        hidden = st.sb("hidden", [P, 2, FT, CAP0])
        yout = st.sb("yout", [P, 2, ST, D])
        pst = [st.ps(f"pst{k}", [P, CAP0]) for k in range(KD)]
        psh = [st.ps(f"psh{k}", [P, CAP0]) for k in range(4)]
        psy = [st.ps(f"psy{k}", [P, D]) for k in range(2)]
        landed = [st.sem(f"landed{u}") for u in range(2)]
        turned, turn_taken = st.sem("turned"), st.sem("turn_taken")
        h_ready, h_taken = st.sem("h_ready"), st.sem("h_taken")
        y_ready, y_taken = st.sem("y_ready"), st.sem("y_taken")
        stored = [st.sem(f"stored{u}") for u in range(2)]
        block = ctx.enter_context(nc.Block())
        w1_rows = io["w1"].rearrange("e d f -> (e d) f")
        w2_rows = io["w2"].rearrange("e f d -> (e f) d")

        @block.sync
        def _(sp):
            for i in rounds(sp, E // 2):
                for u in range(2):
                    e = 2 * i + u
                    slots, ins, outs = snap(sp, e * CAP0), snap(sp, e * D), snap(sp, e * F)
                    wait(sp, y_ready, ST * (e - 1))
                    sp.dma_start(rows[:, u, :, :], dram["expert_in"][bass.ds(slots, CAP0), :]
                                 .rearrange("(t p) d -> p t d", p=P)).then_inc(landed[u], 16)
                    sp.dma_start(w1[u][:, :, :], w1_rows[bass.ds(ins, D), :].rearrange("(k p) f -> p k f", p=P)
                                 ).then_inc(landed[u], 16)
                    sp.dma_start(w2[u][:, :, :], w2_rows[bass.ds(outs, F), :].rearrange("(k p) d -> p k d", p=P)
                                 ).then_inc(landed[u], 16)

        @block.gpsimd
        def _(pool):
            for i in rounds(pool, E // 2):
                for u in range(2):
                    e = 2 * i + u
                    pool.wait_ge(y_taken, ST * (e + 1))
                    pool.dma_start(dram["expert_out"][bass.ds(e * CAP0, CAP0), :].rearrange("(t p) d -> p t d", p=P),
                                   yout[:, u, :, :]).then_inc(stored[u], 16)
            for u in range(2):
                pool.wait_ge(stored[u], 16 * (E // 2))

        @block.tensor
        def _(pe):
            for i in rounds(pe, E // 2):
                for u in range(2):
                    e = 2 * i + u
                    pe.wait_ge(landed[u], 48 * (i + 1))
                    wait(pe, turn_taken, e)
                    for t in range(ST):
                        for k in range(KD):
                            ins = pe.transpose(pst[k][:, t * P:(t + 1) * P], rows[:, u, t, k * P:(k + 1) * P],
                                               keep["identity"][:, :])
                    ins.then_inc(turned, 1)
                    pe.wait_ge(turn_taken, e + 1)
                    for f in range(FT):
                        wait(pe, h_taken, FT * e + f - 3)
                        for k in range(KD):
                            ins = pe.matmul(psh[f % 4][:, :], w1[u][:, k, f * P:(f + 1) * P], rows_t[:, u, k, :],
                                            start=(k == 0), stop=(k == KD - 1))
                        ins.then_inc(h_ready, 1)
                    pe.wait_ge(h_taken, FT * (e + 1))
                    for t in range(ST):
                        wait(pe, y_taken, ST * e + t - 1)
                        for f in range(FT):
                            ins = pe.matmul(psy[t % 2][:, :], hidden[:, u, f, t * P:(t + 1) * P], w2[u][:, f, :],
                                            start=(f == 0), stop=(f == FT - 1))
                        ins.then_inc(y_ready, 1)

        @block.scalar
        def _(act):
            for i in rounds(act, E // 2):
                for u in range(2):
                    e = 2 * i + u
                    act.wait_ge(turned, e + 1)
                    wait(act, h_ready, FT * (e - 1))
                    act.copy(rows_t[:, u, 0, :], pst[0][:, :])
                    act.copy(rows_t[:, u, 1, :], pst[1][:, :]).then_inc(turn_taken, 1)
                    for f in range(FT):
                        act.wait_ge(h_ready, FT * e + f + 1)
                        if f == 0:
                            wait(act, y_ready, ST * (e - 1))
                        act.activation(hidden[:, u, f, :], psh[f % 4][:, :], ACT.Gelu_apprx_tanh).then_inc(h_taken, 1)

        @block.vector
        def _(vec):
            for i in rounds(vec, E // 2):
                for u in range(2):
                    e = 2 * i + u
                    for t in range(ST):
                        vec.wait_ge(y_ready, ST * e + t + 1)
                        if t == 0:
                            wait(vec, stored[u], 16 * i)
                        vec.tensor_copy(yout[:, u, t, :], psy[t % 2][:, :]).then_inc(y_taken, 1)


def stage_join(nc, io, keep, dram):
    with ExitStack() as ctx:
        st = Stage(nc, ctx, "j_")
        wo = st.sb("wo", [P, KD, D])
        wr = st.sb("wr", [P, KD, E])
        oin = st.sb("oin", [P, 2, TC, D])
        xin = st.sb("xin", [P, 2, TC, D])
        yin = st.sb("yin", [P, 2, TC, D])
        ot = st.sb("ot", [P, 2, KD, CH])
        silu = st.sb("silu", [P, 2, TC, D])
        x1 = st.sb("x1", [P, 2, TC, D])
        xn = st.sb("xn", [P, 2, TC, D])
        xnt = st.sb("xnt", [P, 2, KD, CH])
        stats = st.sb("stats", [P, 2, TC, 6])
        mv = st.sb("mv", [P, 2, TC, 2])
        std = st.sb("std", [P, 2, TC])
        rstd = st.sb("rstd", [P, 2, TC])
        eps = st.sb("eps", [P, 1])
        spare = st.sb("spare", [P, 1])
        logits = st.sb("logits", [P, E, NT])
        names3 = ("equal", "onehot0", "onehot1", "both", "masked", "total", "scanned", "place", "fits")
        big = {n: st.sb("r_" + n, [P, E, NT]) for n in names3}
        both16 = st.sb("both16", [P, E, NT], BF16)
        small = {n: st.sb("s_" + n, [P, NT]) for n in ("top0", "top1", "first0", "first1", "gap", "ratio", "den", "w0", "w1")}
        pst = [st.ps(f"pst{k}", [P, CH]) for k in range(KD)]
        psx = [st.ps(f"psx{k}", [P, CH]) for k in range(KD)]
        pss = [st.ps(f"pss{k}", [P, 2, D]) for k in range(2)]
        psl = st.ps("psl", [P, TC, E])
        psc = st.ps("psc", [P, 2, E * NT])

        weights_landed = st.sem("weights_landed")
        in_landed = [st.sem(f"in_landed{u}") for u in range(2)]
        y_landed = [st.sem(f"y_landed{u}") for u in range(2)]
        o_turned, ot_ready, s_ready, silu_ready = (st.sem("o_turned"), st.sem("ot_ready"), st.sem("s_ready"),
                                                   st.sem("silu_ready"))
        s_taken = st.sem("s_taken")
        x1_ready = st.sem("x1_ready")
        mv_ready, std_ready, xn_ready = st.sem("mv_ready"), st.sem("std_ready"), st.sem("xn_ready")
        x_turned, xnt_ready, l_ready, l_taken = st.sem("x_turned"), st.sem("xnt_ready"), st.sem("l_ready"), st.sem("l_taken")
        x1_stored = [st.sem(f"x1_stored{u}") for u in range(2)]
        xnt_stored = [st.sem(f"xnt_stored{u}") for u in range(2)]
        eps_set, dve_step = st.sem("eps_set"), st.sem("dve_step")
        onehot_ready, counted, gap_ready, ratio_ready = (st.sem("onehot_ready"), st.sem("counted"), st.sem("gap_ready"),
                                                         st.sem("ratio_ready"))
        block = ctx.enter_context(nc.Block())
        x_rows = io["x"].rearrange("b s d -> (b s) d")

        def tiles(rows, c):
            return rows[bass.ds(c * CH, CH), :].rearrange("(t p) d -> p t d", p=P)

        @block.sync
        def _(sp):
            sp.dma_start(wo[:, :, :], io["wo"].rearrange("(k p) n -> p k n", p=P)).then_inc(weights_landed, 16)
            sp.dma_start(wr[:, :, :], io["router1"].rearrange("(k p) n -> p k n", p=P)).then_inc(weights_landed, 16)

            def load(c, u):
                sp.dma_start(oin[:, u, :, :], tiles(dram["attn0"], c)).then_inc(in_landed[u], 16)
                sp.dma_start(xin[:, u, :, :], tiles(x_rows, c)).then_inc(in_landed[u], 16)

            def store(c, u):
                sp.wait_ge(x1_ready, c + 1)
                sp.dma_start(tiles(dram["x1"], c), x1[:, u, :, :]).then_inc(x1_stored[u], 16)

            load(0, 0)
            load(1, 1)
            with sp.Fori(0, NC // 2 - 1) as i:
                for u in range(2):
                    store(2 * i + u, u)
                    load(2 * i + u + 2, u)
            store(NC - 2, 0)
            store(NC - 1, 1)
            for u in range(2):
                sp.wait_ge(x1_stored[u], 16 * (NC // 2))
                sp.wait_ge(xnt_stored[u], 16 * (NC // 2))

        @block.gpsimd
        def _(pool):
            for c in range(NC):
                u = c % 2
                if c >= 2:
                    pool.wait_ge(y_landed[u], 16 * TC * (c // 2))
                    pool.wait_ge(silu_ready, c - 1)
                for t in range(TC):
                    n = c * TC + t
                    pool.indirect_dma_start(yin[:, u, t, :], None, dram["expert_out"],
                                            bass.IndirectOffsetOnAxis(ap=keep["slot_get"][:, n:n + 1], axis=0)
                                            ).then_inc(y_landed[u], 16)

        @block.tensor
        def _(pe):
            pe.wait_ge(weights_landed, 32)

            def front(c, n, u):
                pe.wait_ge(in_landed[u], 32 * (n + 1))
                wait(pe, ot_ready, c)
                for t in range(TC):
                    for k in range(KD):
                        ins = pe.transpose(pst[k][:, t * P:(t + 1) * P], oin[:, u, t, k * P:(k + 1) * P],
                                           keep["identity"][:, :])
                ins.then_inc(o_turned, 1)
                pe.wait_ge(ot_ready, c + 1)
                wait(pe, s_taken, c)
                for t in range(TC):
                    for k in range(KD):
                        ins = pe.matmul(pss[t // 2][:, t % 2, :], ot[:, u, k, t * P:(t + 1) * P], wo[:, k, :],
                                        start=(k == 0), stop=(k == KD - 1))
                ins.then_inc(s_ready, 1)

            def back(c, n, u):
                pe.wait_ge(xn_ready, c + 1)
                wait(pe, xnt_ready, c)
                for t in range(TC):
                    for k in range(KD):
                        ins = pe.transpose(psx[k][:, t * P:(t + 1) * P], xn[:, u, t, k * P:(k + 1) * P],
                                           keep["identity"][:, :])
                ins.then_inc(x_turned, 1)
                pe.wait_ge(xnt_ready, c + 1)
                wait(pe, l_taken, c)
                for t in range(TC):
                    for k in range(KD):
                        ins = pe.matmul(psl[:, t, :], xnt[:, u, k, t * P:(t + 1) * P], wr[:, k, :],
                                        start=(k == 0), stop=(k == KD - 1))
                ins.then_inc(l_ready, 1)

            chunks_skewed(pe, front, back)
            pe.wait_ge(onehot_ready, 1)
            oh = both16[:, :, :].rearrange("p e t -> p (e t)")
            pe.matmul(psc[:, 0, :], keep["before16"][:, :], oh, start=True, stop=True)
            pe.matmul(psc[:, 1, :], keep["ones16"][:, :], oh, start=True, stop=True).then_inc(counted, 1)

        @block.scalar
        def _(act):
            act.wait_ge(eps_set, 1)

            def front(c, n, u):
                act.wait_ge(o_turned, c + 1)
                wait(act, s_ready, ago(c))
                act.copy(ot[:, u, 0, :], pst[0][:, :])
                act.copy(ot[:, u, 1, :], pst[1][:, :]).then_inc(ot_ready, 1)
                act.wait_ge(y_landed[u], 16 * TC * (n + 1))
                wait(act, x1_ready, ago(c))
                for t in range(TC):
                    ins = act.activation(silu[:, u, t, :], yin[:, u, t, :], ACT.Silu,
                                         scale=keep["gate"][:, bass.ds(c * TC + t, 1)])
                ins.then_inc(silu_ready, 1)
                act.wait_ge(mv_ready, c + 1)
                act.activation(std[:, u, :], mv[:, u, :, 1], ACT.Sqrt, bias=eps[:, 0:1]).then_inc(std_ready, 1)

            def back(c, n, u):
                act.wait_ge(x_turned, c + 1)
                wait(act, xnt_stored[u], 16 * n)
                act.copy(xnt[:, u, 0, :], psx[0][:, :])
                act.copy(xnt[:, u, 1, :], psx[1][:, :]).then_inc(xnt_ready, 1)
                act.wait_ge(l_ready, c + 1)
                act.copy(logits[:, :, bass.ds(c * TC, TC)].rearrange("p e t -> p t e"), psl[:, :, :]).then_inc(l_taken, 1)
                act.wait_ge(xnt_ready, c + 1)
                act.dma_start(dram["xnt1"][:, :, bass.ds(c * CH, CH)].rearrange("k p n -> p k n"), xnt[:, u, :, :]
                              ).then_inc(xnt_stored[u], 16)

            chunks_skewed(act, front, back)
            act.wait_ge(gap_ready, 1)
            act.activation(small["ratio"][:, :], small["gap"][:, :], ACT.Exp).then_inc(ratio_ready, 1)

        @block.vector
        def _(vec):
            vec.memset(eps[:, :], EPS).then_inc(eps_set, 1)
            ch = Chain(vec, dve_step)

            def front(c, n, u):
                ch.base, ch.k = 3 * c, 0
                vec.wait_ge(s_ready, c + 1)
                vec.wait_ge(silu_ready, c + 1)
                vec.wait_ge(in_landed[u], 32 * (n + 1))
                for k in range(2):
                    ins = vec.tensor_tensor(silu[:, u, 2 * k:2 * k + 2, :], pss[k][:, :, :], silu[:, u, 2 * k:2 * k + 2, :],
                                            ALU.mult)
                ins.then_inc(s_taken, 1)
                vec.wait_ge(s_taken, c + 1)
                wait(vec, x1_stored[u], 16 * n)
                vec.tensor_tensor(x1[:, u, :, :], xin[:, u, :, :], silu[:, u, :, :], ALU.add).then_inc(x1_ready, 1)
                vec.wait_ge(x1_ready, c + 1)
                for t in range(TC):
                    ins = vec.bn_stats(stats[:, u, t, :], x1[:, u, t, :])
                ch.link(ins)
                vec.memset(spare[:, :], 0.0)
                for t in range(TC):
                    ins = vec.bn_aggr(mv[:, u, t, :], stats[:, u, t, :])
                ins.then_inc(mv_ready, 1)
                vec.wait_ge(mv_ready, c + 1)
                vec.wait_ge(std_ready, c + 1)
                ch.link(vec.reciprocal(rstd[:, u, :], std[:, u, :]))
                wait(vec, x_turned, ago(c))
                for t in range(TC):
                    ins = vec.tensor_scalar(xn[:, u, t, :], x1[:, u, t, :], mv[:, u, t, 0:1], rstd[:, u, t:t + 1],
                                            ALU.subtract, ALU.mult)
                ins.then_inc(xn_ready, 1)
                ch.link(vec.memset(spare[:, :], 0.0))

            chunks_skewed(vec, front, lambda c, n, u: None)
            ch.base, ch.k = 3 * NC, 0

            vec.wait_ge(l_taken, NC)
            L, s = logits[:, :, :], {n: v[:, :] for n, v in small.items()}
            b = {n: v[:, :, :] for n, v in big.items()}
            first_max(vec, ch, keep, L, s["top0"], b["equal"], s["first0"], b["onehot0"])
            ch.link(vec.scalar_tensor_tensor(out=b["masked"], in0=b["onehot0"], scalar=-3.0e38, in1=L, op0=ALU.mult, op1=ALU.add))
            first_max(vec, ch, keep, b["masked"], s["top1"], b["equal"], s["first1"], b["onehot1"])
            ch.link(vec.tensor_tensor(b["both"], b["onehot0"], b["onehot1"], ALU.add))
            vec.tensor_copy(both16[:, :, :], b["both"]).then_inc(onehot_ready, 1)
            vec.tensor_tensor(s["gap"], s["top1"], s["top0"], ALU.subtract).then_inc(gap_ready, 1)
            vec.wait_ge(ratio_ready, 1)
            ch.link(vec.tensor_scalar(s["den"], s["ratio"], 1.0, None, ALU.add))
            ch.link(vec.reciprocal(s["w0"], s["den"]))
            ch.link(vec.tensor_tensor(s["w1"], s["ratio"], s["w0"], ALU.mult))
            vec.wait_ge(counted, 1)
            places(vec, ch, keep, "running1", psc[:, 0, :], psc[:, 1, :], b["total"], b["scanned"], b["place"])
            ch.link(vec.tensor_scalar(b["fits"], b["place"], float(CAP1), None, ALU.is_lt))
            for w, oh in (("w0", "onehot0"), ("w1", "onehot1")):
                ch.link(vec.tensor_tensor(b[oh], b[oh], s[w].unsqueeze(1).to_broadcast([P, E, NT]), ALU.mult))
            ch.link(vec.tensor_tensor(b["both"], b["onehot0"], b["onehot1"], ALU.add))
            ch.link(vec.tensor_tensor(keep["coef"][:, :, :].rearrange("p t e -> p e t"), b["both"], b["fits"], ALU.mult))


PAIRS = H // 2


def window_steps():
    fillers = {0: [("W", 0)], 1: [("W", 1)], 2: [("W", 2), ("QR", 0)], 3: [("W", 3), ("QR", 1), ("QR", 2)],
               4: [("W", 4), ("QR", 3), ("KR", 0), ("E", 0)], 5: [("W", 5), ("QR", 4), ("QR", 5), ("KR", 1), ("E", 1)],
               6: [("E", 2), ("QR", 6), ("KR", 2)], 7: [("E", 3), ("QR", 7), ("KR", 3)]}
    steps = []
    for p in range(PAIRS):
        steps.append(("S", p))
        if p >= 1:
            steps.append(("N", p - 1))
        steps += fillers[p]
        if p >= 2:
            steps.append(("T", p - 2))
        if p >= 3:
            steps.append(("PV", p - 3))
    steps += [("N", 7), ("T", 6), ("PV", 5), ("R", 0), ("R", 1), ("T", 7), ("PV", 6), ("R", 2), ("R", 3), ("PV", 7),
              ("R", 4), ("R", 5), ("OUT",)]
    return steps


def emptier(s):
    if s[0] == "W":
        return "act"
    if s[0] == "E":
        return "dve"
    if s[0] == "T":
        return ("dve", "act")[s[1] % 2]
    return "act" if s[1] < 4 else "dve"


class Uses:

    def __init__(self, kinds, ahead, steps):
        self.kinds = kinds
        self.ahead = ahead
        self.every = [s for s in steps if s[0] in kinds]
        assert len(ahead) % 2 == 0 and len(self.every) % 2 == 0

    def emptied(self, who, t):
        return sum(emptier(s) == who for s in self.ahead) + t * sum(emptier(s) == who for s in self.every)

    def filled(self, t):
        return len(self.ahead) + t * len(self.every)

    def within(self, order, n, who=None):
        mine = [s for s in order if s[0] in self.kinds][:n]
        return len([s for s in mine if who is None or emptier(s) == who])

    def index(self, order, step):
        return [s for s in order if s[0] in self.kinds].index(step)


def stage_windows(nc, io, keep, dram, out):
    steps = window_steps()
    first_steps = [("W", n) for n in range(6)] + [("QR", n) for n in range(8)] + [("KR", n) for n in range(4)] + [
        ("R", n) for n in range(6)]
    last_steps = [s for s in steps if s[0] not in ("W", "QR", "KR", "R")]
    work = Uses(("W", "E"), [("W", n) for n in range(6)], steps)
    turns = Uses(("T", "R"), [("R", n) for n in range(6)], steps)
    with ExitStack() as ctx:
        st = Stage(nc, ctx, "w_")
        wqkv = st.sb("wqkv", [P, KD, 3 * J])
        wout = st.sb("wout", [P, PAIRS, D])
        we = st.sb("we", [P, KD, E, D])
        rope_names = [f"{f}_{n}" for f in ("cos", "sin") for n in ("q0", "q1", "k")]
        rope = {n: st.sb("t_" + n, [P, DH // 2]) for n in rope_names}
        nsin = {n: st.sb("n_" + n, [P, DH // 2]) for n in ("q0", "q1", "k")}
        masks = st.sb("masks", [P, NT, 2 * P], BF16)
        xnt = st.sb("xnt", [P, 2, KD, P])
        x1 = st.sb("x1", [P, 2, D])
        raw = st.sb("raw", [P, 3, J])
        rot = st.sb("rot", [P, 3, J])
        crossed = st.sb("crossed", [P, 2, J])
        v = [st.sb(f"v{u}", [P, J]) for u in range(2)]
        kd = [st.sb(f"kd{u}", [P, PAIRS, 2, P]) for u in range(2)]
        qt = st.sb("qt", [P, 2, PAIRS, P])
        top = st.sb("top", [P, 2, PAIRS])
        rows = st.sb("rows", [P, 2, PAIRS])
        inv = st.sb("inv", [P, 2, PAIRS])
        probs = st.sb("probs", [P, 4, 2, 2 * P])
        pt = st.sb("pt", [P, 2, 4, P])
        ot = st.sb("ot", [P, PAIRS, P])
        y = st.sb("y", [P, D])
        sig = st.sb("sig", [P, D])
        res = st.sb("res", [P, 2, D])
        psw = [st.ps(f"psw{k}", [P, CH]) for k in range(2)]
        pss = [st.ps(f"pss{k}", [P, 2, 2 * P]) for k in range(2)]
        pst = [st.ps(f"pst{k}", [P, 4, P]) for k in range(2)]
        pso = st.ps("pso", [P, 4, P])
        psy = st.ps("psy", [P, D])

        weights_landed = st.sem("weights_landed")
        n_weights = 2 + KD + len(rope_names)
        pool_set = st.sem("pool_set")
        xt_landed = [st.sem(f"xt_landed{u}") for u in range(2)]
        x1_landed = [st.sem(f"x1_landed{u}") for u in range(2)]
        work_ready, s_ready, t_ready = st.sem("work_ready"), st.sem("s_ready"), st.sem("t_ready")
        work_taken = {w: st.sem("work_taken_" + w) for w in ("act", "dve")}
        turn_taken = {w: st.sem("turn_taken_" + w) for w in ("act", "dve")}
        top_ready, exp_ready, inv_ready, p_ready = (st.sem("top_ready"), st.sem("exp_ready"), st.sem("inv_ready"),
                                                    st.sem("p_ready"))
        pv_done, ot_ready, y_ready, out_ready = st.sem("pv_done"), st.sem("ot_ready"), st.sem("y_ready"), st.sem("out_ready")
        q_rotated, k_rotated, v_moved = st.sem("q_rotated"), st.sem("k_rotated"), st.sem("v_moved")
        sig_ready, res_step = st.sem("sig_ready"), st.sem("res_step")
        stored = [st.sem(f"stored{u}") for u in range(2)]
        dve_step, pool_step = st.sem("dve_step"), st.sem("pool_step")
        block = ctx.enter_context(nc.Block())
        out_rows = out.rearrange("b s d -> (b s) d")

        def tiles(eng):
            for i in rounds(eng, NT // 2 - 1):
                for u in range(2):
                    yield 2 * i + u, u, i, steps
            yield NT - 2, 0, NT // 2 - 1, steps
            yield NT - 1, 1, NT // 2 - 1, last_steps

        def heads(ap):
            return ap.rearrange("p (h s x) -> p h s x", s=2, x=DH // 2)

        wide = [P, H, DH // 2]

        def rotary(eng, r, c, name, n, src):
            if n < 2:
                sin = (nsin[name], rope["sin_" + name])[n]
                return eng.tensor_tensor(heads(crossed[:, c, :])[:, :, n, :], heads(src)[:, :, 1 - n, :],
                                         sin[:, :].unsqueeze(1).to_broadcast(wide), ALU.mult)
            if n == 2:
                halves = [P, 2 * H, DH // 2]
                return eng.tensor_tensor(rot[:, r, :].rearrange("p (h x) -> p h x", x=DH // 2),
                                         src.rearrange("p (h x) -> p h x", x=DH // 2),
                                         rope["cos_" + name][:, :].unsqueeze(1).to_broadcast(halves), ALU.mult)
            return eng.tensor_tensor(rot[:, r, :], rot[:, r, :], crossed[:, c, :], ALU.add)

        @block.sync
        def _(sp):
            sp.dma_start(wqkv[:, :, :], io["w_qkv"].rearrange("(k p) n -> p k n", p=P)).then_inc(weights_landed, 16)
            sp.dma_start(wout[:, :, :], io["w_out"].rearrange("(k p) n -> p k n", p=P)).then_inc(weights_landed, 16)
            for k in range(KD):
                sp.dma_start(we[:, k, :, :], io["we"][:, k * P:(k + 1) * P, :].rearrange("e p d -> p e d")
                             ).then_inc(weights_landed, 16)
            for f in ("cos", "sin"):
                for n, at in (("q0", 0), ("q1", P), ("k", 0)):
                    sp.dma_start(rope[f"{f}_{n}"][:, :], io[f"{f}_{n[0]}"][at:at + P, :]).then_inc(weights_landed, 16)

            def load_t(at, u):
                sp.dma_start(xnt[:, u, :, :], dram["xnt1"][:, :, bass.ds(at, P)].rearrange("k p n -> p k n")
                             ).then_inc(xt_landed[u], 16)

            load_t(0, 0)
            load_t(P, 1)
            for t, u, i, order in tiles(sp):
                if not (isinstance(t, int) and t >= NT - 2):
                    sp.wait_ge(work_ready, work.filled(t + 1))
                    load_t((t + 2) * P, u)


        @block.gpsimd
        def _(pool):
            ch = Chain(pool, pool_step)
            ch.link(pool.memset(masks[:, :, :], 0.0))
            ch.link(pool.affine_select(out=masks[:, :, 0:P], in_=masks[:, :, 0:P], compare_op=ALU.is_ge, fill=NEG, base=0,
                                       pattern=[[0, NT], [1, P]], channel_multiplier=-1))
            ch.link(pool.affine_select(out=masks[:, :, P:2 * P], in_=masks[:, :, P:2 * P], compare_op=ALU.is_ge, fill=NEG,
                                       base=0, pattern=[[0, NT], [-1, P]], channel_multiplier=1))
            for b in range(B):
                ins = pool.memset(masks[:, b * NT // B, 0:P], NEG)
                ch.link(ins)
            pool.wait_ge(weights_landed, 16 * n_weights)
            for n in ("q0", "q1", "k"):
                ch.link(pool.tensor_scalar(nsin[n][:, :], rope["sin_" + n][:, :], -1.0, 0.0, ALU.mult, ALU.add))
            pool.memset(v[1][:, :], 0.0).then_inc(pool_set, 1)

            def rotate(n, t, taken):
                if n == 0:
                    wait(pool, work_taken["act"], taken)
                    wait(pool, t_ready, turns.filled(t))
                    wait(pool, k_rotated, t + 1)
                ins = rotary(pool, 2, 1, "k", n, raw[:, 1, :])
                if n < 3:
                    ch.link(ins)
                else:
                    ins.then_inc(k_rotated, 1)

            pool.wait_ge(pool_set, 1)
            for n in range(4):
                rotate(n, -1, 4)
            start = ch.k
            for t, u, i, order in tiles(pool):
                ch.base, ch.k = start + t * 3, 0
                for s in order:
                    if s[0] == "N":
                        p = s[1]
                        wait(pool, inv_ready, PAIRS * t + p + 1)
                        pool.tensor_tensor(probs[:, p % 4, :, :], probs[:, p % 4, :, :],
                                           inv[:, :, p:p + 1].to_broadcast([P, 2, 2 * P]), ALU.mult).then_inc(p_ready, 1)
                    elif s[0] == "KR":
                        rotate(s[1], t, work.emptied("act", t) + 4)
                wait(pool, out_ready, t + 1)
                pool.dma_start(out_rows[bass.ds(t * P, P), :], res[:, u, :]).then_inc(stored[u], 16)
            for u in range(2):
                wait(pool, stored[u], 16 * (NT // 2))

        @block.tensor
        def _(pe):
            def bank_free(use, taken, order, t, n):
                if n < 2:
                    for who in ("act", "dve"):
                        wait(pe, taken[who], use.emptied(who, t))
                else:
                    before = [s for s in order if s[0] in use.kinds][n - 2]
                    who = emptier(before)
                    wait(pe, taken[who], use.emptied(who, t) + use.within(order, n - 1, who))

            def project(n, bank, src):
                for k in range(KD):
                    ins = pe.matmul(psw[bank][:, :], xnt[:, src, k, :], wqkv[:, k, n * CH:(n + 1) * CH],
                                    start=(k == 0), stop=(k == KD - 1))
                ins.then_inc(work_ready, 1)

            def turn(n, bank, tile):
                pe.wait_ge(q_rotated if n < 4 else k_rotated, tile + 1)
                for j in range(4):
                    pair = 4 * (n % 2) + j
                    ins = pe.transpose(pst[bank][:, j, :], rot[:, n // 2, pair * P:(pair + 1) * P], keep["identity"][:, :])
                ins.then_inc(t_ready, 1)

            pe.wait_ge(weights_landed, 16 * n_weights)
            pe.wait_ge(xt_landed[0], 16)
            for n in range(6):
                wait(pe, work_taken["act"], n - 1)
                project(n, n % 2, 0)
            for n in range(6):
                if n >= 2:
                    pe.wait_ge(turn_taken["act"], n - 1)
                turn(n, n % 2, 0)
            pe.wait_ge(pool_set, 1)
            for t, u, i, order in tiles(pe):
                w = r = 0
                for s in order:
                    if s[0] == "S":
                        p = s[1]
                        if p == 0:
                            for who in ("act", "dve"):
                                wait(pe, turn_taken[who], turns.emptied(who, t))
                        wait(pe, exp_ready, PAIRS * t + max(p - 1, 0))
                        pe.matmul(pss[p % 2][:, :, :], keep["identity16"][:, :],
                                  masks[:, bass.ds(t, 1), :].to_broadcast([P, 2, 2 * P]), start=True, stop=False)
                        pe.matmul(pss[p % 2][:, :, 0:P], qt[:, 1, p, :], kd[1 - u][:, p, :, :], start=False, stop=False)
                        pe.matmul(pss[p % 2][:, :, P:2 * P], qt[:, 0, p, :], kd[u][:, p, :, :], start=False, stop=True
                                  ).then_inc(s_ready, 1)
                    elif s[0] == "W":
                        bank_free(work, work_taken, order, t, w)
                        if s[1] == 0:
                            pe.wait_ge(xt_landed[1 - u], 16 * (i + 1 + u))
                        project(s[1], w % 2, 1 - u)
                        w += 1
                    elif s[0] == "E":
                        bank_free(work, work_taken, order, t, w)
                        for k in range(KD):
                            ins = pe.matmul(psw[w % 2][:, :], xnt[:, u, k, :], we[:, k, 2 * s[1]:2 * s[1] + 2, :],
                                            start=(k == 0), stop=(k == KD - 1))
                        ins.then_inc(work_ready, 1)
                        w += 1
                    elif s[0] == "T":
                        p = s[1]
                        wait(pe, p_ready, PAIRS * t + p + 1)
                        bank_free(turns, turn_taken, order, t, r)
                        for e in range(2):
                            for role in range(2):
                                ins = pe.transpose(pst[r % 2][:, 2 * e + role, :], probs[:, p % 4, e, role * P:(role + 1) * P],
                                                   keep["identity"][:, :])
                        ins.then_inc(t_ready, 1)
                        r += 1
                    elif s[0] == "R":
                        bank_free(turns, turn_taken, order, t, r)
                        turn(s[1], r % 2, t + 1)
                        r += 1
                    elif s[0] == "PV":
                        p = s[1]
                        n = turns.index(order, ("T", p))
                        who = emptier(("T", p))
                        wait(pe, turn_taken[who], turns.emptied(who, t) + turns.within(order, n + 1, who))
                        if p == 0:
                            pe.wait_ge(v_moved, t + 1)
                            wait(pe, ot_ready, 2 * t)
                        if p == 4:
                            wait(pe, ot_ready, 2 * t + 1)
                        for role in range(2):
                            for e in range(2):
                                h = 2 * p + e
                                ins = pe.matmul(pso[e * DH:(e + 1) * DH, p % 4, :], v[(u + 1 + role) % 2][:, h * DH:(h + 1) * DH],
                                                pt[:, p % 2, 2 * e + role, :], start=(role == 0), stop=(role == 1))
                        ins.then_inc(pv_done, 1)
                    elif s[0] == "OUT":
                        wait(pe, ot_ready, 2 * t + 2)
                        wait(pe, out_ready, t)
                        for p in range(PAIRS):
                            ins = pe.matmul(psy[:, :], ot[:, p, :], wout[:, p, :], start=(p == 0), stop=(p == PAIRS - 1))
                        ins.then_inc(y_ready, 1)

        @block.scalar
        def _(act):
            def take_work(n, t, filled, bank):
                act.wait_ge(work_ready, filled)
                wait(act, (q_rotated, k_rotated, v_moved)[n // 2], t + 1)
                act.copy(raw[:, n // 2, (n % 2) * CH:(n % 2 + 1) * CH], psw[bank][:, :]).then_inc(work_taken["act"], 1)

            def take_q(n, t, filled, bank):
                wait(act, t_ready, filled)
                wait(act, s_ready, PAIRS * (t + 1))
                act.copy(qt[:, n // 2, 4 * (n % 2):4 * (n % 2) + 4, :], pst[bank][:, :, :]).then_inc(turn_taken["act"], 1)

            for n in range(6):
                take_work(n, -1, n + 1, n % 2)
            for n in range(4):
                take_q(n, -1, n + 1, n % 2)
            for t, u, i, order in tiles(act):
                wait(act, out_ready, t)
                act.dma_start(x1[:, u, :], dram["x1"][bass.ds(t * P, P), :]).then_inc(x1_landed[u], 16)
                wait(act, pv_done, PAIRS * t)
                wait(act, work_taken["act"], work.emptied("act", t))
                act.copy(v[u][:, :], raw[:, 2, :]).then_inc(v_moved, 1)
                w = r = 0
                for s in order:
                    if s[0] == "S":
                        p = s[1]
                        if p == 0:
                            wait(act, inv_ready, PAIRS * t)
                        act.wait_ge(top_ready, PAIRS * t + p + 1)
                        wait(act, t_ready, turns.filled(t) + (turns.index(order, ("T", p - 4)) + 1 if p >= 4 else 0))
                        for e in range(2):
                            ins = act.activation(probs[:, p % 4, e, :], pss[p % 2][:, e, :], ACT.Exp, bias=top[:, e, p:p + 1],
                                                 accum_out=rows[:, e, p:p + 1])
                        ins.then_inc(exp_ready, 1)
                    elif s[0] == "W":
                        take_work(s[1], t, work.filled(t) + w + 1, w % 2)
                        w += 1
                    elif s[0] == "E":
                        w += 1
                    elif s[0] in ("T", "R"):
                        if s[0] == "T" and emptier(s) == "act":
                            wait(act, t_ready, turns.filled(t) + r + 1)
                            wait(act, pv_done, PAIRS * t + max(s[1] - 1, 0))
                            act.copy(pt[:, s[1] % 2, :, :], pst[r % 2][:, :, :]).then_inc(turn_taken["act"], 1)
                        elif s[0] == "R" and emptier(s) == "act":
                            take_q(s[1], t, turns.filled(t) + r + 1, r % 2)
                        r += 1
                    elif s[0] == "PV" and s[1] % 4 == 3:
                        half = s[1] // 4
                        wait(act, pv_done, PAIRS * t + s[1] + 1)
                        if half == 0:
                            wait(act, y_ready, t)
                        act.copy(ot[:, 4 * half:4 * half + 4, :], pso[:, :, :]).then_inc(ot_ready, 1)
                    if s == ("T", 6):
                        act.wait_ge(work_taken["dve"], work.emptied("dve", t + 1))
                        wait(act, out_ready, t)
                        act.activation(sig[:, :], y[:, :], ACT.Exp, scale=-1.0).then_inc(sig_ready, 1)

        @block.vector
        def _(vec):
            ch = Chain(vec, dve_step)
            for u in range(2):
                ins = vec.memset(kd[u][:, :, :, :], 0.0)
            ch.link(ins)

            def rotate(n, t, taken):
                if n == 0:
                    wait(vec, work_taken["act"], taken)
                    wait(vec, t_ready, turns.filled(t))
                    wait(vec, q_rotated, t + 1)
                ins = rotary(vec, n // 4, 0, f"q{n // 4}", n % 4, raw[:, 0, :])
                if n < 7:
                    ch.link(ins)
                else:
                    ins.then_inc(q_rotated, 1)

            def take_k(n, t, filled, bank, into):
                wait(vec, t_ready, filled)
                wait(vec, s_ready, PAIRS * (t + 1))
                for e in range(2):
                    ins = vec.tensor_copy(kd[into][e * DH:(e + 1) * DH, 4 * (n % 2):4 * (n % 2) + 4, e, :],
                                          pst[bank][e * DH:(e + 1) * DH, :, :])
                ins.then_inc(turn_taken["dve"], 1)

            vec.wait_ge(pool_set, 1)
            for n in range(8):
                rotate(n, -1, 2)
            for n in (4, 5):
                take_k(n, -1, n + 1, n % 2, 0)
            start = ch.k
            per_tile = 7 + 4 + 3
            for t, u, i, order in tiles(vec):
                ch.base, ch.k = start + t * per_tile, 0
                w = r = 0
                for s in order:
                    if s[0] == "S":
                        p = s[1]
                        vec.wait_ge(s_ready, PAIRS * t + p + 1)
                        vec.tensor_reduce(top[:, :, p], pss[p % 2][:, :, :], X, ALU.max, negate=True).then_inc(top_ready, 1)
                    elif s[0] == "N":
                        p = s[1]
                        if p == 0:
                            wait(vec, p_ready, PAIRS * t)
                        wait(vec, exp_ready, PAIRS * t + p + 1)
                        vec.reciprocal(inv[:, :, p], rows[:, :, p]).then_inc(inv_ready, 1)
                    elif s[0] == "QR":
                        rotate(s[1], t, work.emptied("act", t) + 2)
                    elif s[0] == "W":
                        w += 1
                    elif s[0] == "E":
                        n = s[1]
                        vec.wait_ge(work_ready, work.filled(t) + w + 1)
                        if n == 0:
                            wait(vec, out_ready, t)
                        for e in range(2):
                            weight = keep["coef"][:, bass.ds(t, 1), 2 * n + e:2 * n + e + 1].rearrange("p t e -> p (t e)")
                            part = psw[w % 2][:, e * D:(e + 1) * D]
                            if n == 0 and e == 0:
                                ins = vec.tensor_scalar(y[:, :], part, weight, None, ALU.mult)
                            else:
                                ins = vec.scalar_tensor_tensor(out=y[:, :], in0=part, scalar=weight, in1=y[:, :],
                                                               op0=ALU.mult, op1=ALU.add)
                            if e == 0:
                                ch.link(ins)
                        ins.then_inc(work_taken["dve"], 1)
                        w += 1
                        vec.wait_ge(work_taken["dve"], work.emptied("dve", t) + n + 1)
                    elif s[0] in ("T", "R"):
                        if s[0] == "T" and emptier(s) == "dve":
                            wait(vec, t_ready, turns.filled(t) + r + 1)
                            wait(vec, pv_done, PAIRS * t + max(s[1] - 1, 0))
                            vec.tensor_copy(pt[:, s[1] % 2, :, :], pst[r % 2][:, :, :]).then_inc(turn_taken["dve"], 1)
                        elif s[0] == "R" and emptier(s) == "dve":
                            take_k(s[1], t, turns.filled(t) + r + 1, r % 2, 1 - u)
                        r += 1
                    elif s[0] == "OUT":
                        vec.wait_ge(sig_ready, t + 1)
                        ch.link(vec.tensor_scalar(sig[:, :], sig[:, :], 1.0, None, ALU.add))
                        ch.link(vec.reciprocal(sig[:, :], sig[:, :]))
                        ch.link(vec.tensor_tensor(sig[:, :], sig[:, :], y[:, :], ALU.mult))
                        wait(vec, y_ready, t + 1)
                        wait(vec, stored[u], 16 * i)
                        ins = vec.tensor_tensor(res[:, u, :], psy[:, :], sig[:, :], ALU.mult)
                        ins.then_inc(res_step, 1)
                        vec.wait_ge(res_step, t + 1)
                        vec.wait_ge(x1_landed[u], 16 * (i + 1))
                        vec.tensor_tensor(res[:, u, :], res[:, u, :], x1[:, u, :], ALU.add).then_inc(out_ready, 1)


def make_program(nc, io, out, upto=7):
    dram = {
        "qk_parts": nc.dram_tensor("qk_parts", [2, 3, D, T], BF16).ap(),
        "v": nc.dram_tensor("v_rows", [T, D], F32).ap(),
        "expert_in": nc.dram_tensor("expert_in", [E * CAP0, D], F32).ap(),
        "expert_out": nc.dram_tensor("expert_out", [E * CAP0, D], F32).ap(),
        "attn0": nc.dram_tensor("attn0", [T, D], F32).ap(),
        "xnt1": nc.dram_tensor("xnt1", [KD, P, T], F32).ap(),
        "x1": nc.dram_tensor("x1", [T, D], F32).ap(),
    }
    with ExitStack() as ctx:
        st = Stage(nc, ctx)
        keep = {
            "identity": st.sb("identity", [P, P]),
            "identity16": st.sb("identity16", [P, P], BF16),
            "ones16": st.sb("ones16", [P, P], BF16),
            "zero16": st.sb("zero16", [P, P], BF16),
            "before16": st.sb("before16", [P, P], BF16),
            "mask_qk": st.sb("mask_qk", [P, P], BF16),
            "mask_kq": st.sb("mask_kq", [P, P], BF16),
            "expert": st.sb("expert", [P, E, NT]),
            "expert8": st.sb("expert8", [P, E, NT]),
            "running0": st.sb("running0", [P, E, NT]),
            "running1": st.sb("running1", [P, E, NT]),
            "gate": st.sb("gate", [P, NT]),
            "slot_get": st.sb("slot_get", [P, NT], U32),
            "slot_put": st.sb("slot_put", [P, NT], U32),
            "zero": st.sb("zero", [P, CH]),
            "coef": st.sb("coef", [P, NT, E]),
        }
        build_constants(nc, keep)
        with ExitStack() as front:
            keep["xn_all"] = Stage(nc, front).sb("xn_all", [P, NT, D])
            stage_project(nc, io, keep, dram)
            if upto >= 3:
                stage_attention(nc, io, keep, dram)
        if upto >= 4:
            stage_experts(nc, io, keep, dram)
        if upto >= 5:
            stage_join(nc, io, keep, dram)
        if upto >= 7:
            stage_windows(nc, io, keep, dram, out)
    return dram


def declare(nc, inputs):
    import numpy as np

    def turned(a):
        return np.ascontiguousarray(np.asarray(a).T)

    arrays = {
        "x": np.ascontiguousarray(inputs["L0_attn_x"]),
        "wq": turned(inputs["L0_attn_Wq"]), "wk": turned(inputs["L0_attn_Wk"]), "wv": turned(inputs["L0_attn_Wv"]),
        "wo": turned(inputs["L0_attn_Wo"]), "router0": np.ascontiguousarray(inputs["L0_ffn_router_w"]),
        "w1": np.ascontiguousarray(inputs["L0_ffn_w1"]), "w2": np.ascontiguousarray(inputs["L0_ffn_w2"]),
        "w_qkv": np.ascontiguousarray(inputs["L1_attn_W_qkv"]), "w_out": np.ascontiguousarray(inputs["L1_attn_W_out"]),
        "router1": turned(inputs["L1_ffn_Wr"]), "we": np.ascontiguousarray(inputs["L1_ffn_We"]),
    }
    arrays.update(tables())
    named = {f"in_{k}": v for k, v in arrays.items()}
    io = {k: nc.dram_tensor(f"in_{k}", list(v.shape), mybir.dt.from_np(v.dtype), kind="ExternalInput").ap()
          for k, v in arrays.items()}
    out = nc.dram_tensor("out_0", [B, S, D], F32, kind="ExternalOutput").ap()
    return named, io, out


def tables():
    import numpy as np

    inv_freq = (1.0 / np.power(np.float32(10000.0), np.arange(0, DH, 2, dtype=np.float32) / np.float32(DH))).astype(np.float32)
    angles = np.arange(2 * P, dtype=np.float32)[:, None] * inv_freq[None, :]
    cos, sin = np.cos(angles).astype(np.float32), np.sin(angles).astype(np.float32)
    scale = np.float32(DH ** -0.5)
    return {"cos_q": cos * scale, "sin_q": sin * scale, "cos_k": cos, "sin_k": sin}


def kernel(**inputs):
    import concourse.bacc as bacc
    from concourse.bass_utils import run_bass_kernel_spmd

    nc = bacc.Bacc("TRN2", target_bir_lowering=False, num_devices=1)
    arrays, io, out = declare(nc, inputs)
    make_program(nc, io, out)
    r = run_bass_kernel_spmd(nc, [arrays], core_ids=[0])
    return r.results[0]["out_0"]
```

```python
from contextlib import ExitStack

import concourse.bass as bass
from concourse import mybir

F32 = mybir.dt.float32
BF16 = mybir.dt.bfloat16
F32R = mybir.dt.float32r
U32 = mybir.dt.uint32
I32 = mybir.dt.int32
ALU = mybir.AluOpType
ACT = mybir.ActivationFunctionType
X = mybir.AxisListType.X

P = 128
B, S, D = 2, 2048, 256
T = B * S
NT = T // P
CH = 512
TC = CH // P
NC = T // CH
KD = D // P
E = 8
H = 16
EPS = 1e-5
NEG = -1e30

HD = D // H
F = 1024
FT = F // P
CAP0 = T // E
SKIP = 8192.0
GH = 4
HG = H // GH
KT = S // P
QC = S // CH
QR = 6 * HD
MR = QR + 3

PARTS = ((0, 0), (0, 1), (1, 0))

DH = 64
J = H * DH
CAP1 = int(S * 2 / E * 1.5) + 1


def wait(eng, sem, value):
    if isinstance(value, int) and value <= 0:
        return
    eng.wait_ge(sem, value)


def rounds(eng, n):
    yield 0
    with eng.Fori(1, n) as i:
        yield i


def snap(eng, value):
    return value if isinstance(value, int) else eng.snap(value)


class Chain:

    def __init__(self, eng, sem):
        self.eng, self.sem, self.base, self.k = eng, sem, 0, 0

    def link(self, ins):
        self.k += 1
        ins.then_inc(self.sem, 1)
        self.eng.wait_ge(self.sem, self.base + self.k)


class Stage:

    def __init__(self, nc, ctx, prefix=""):
        self.nc, self.ctx, self.prefix = nc, ctx, prefix

    def sb(self, name, shape, dt=F32):
        return self.ctx.enter_context(self.nc.sbuf_tensor(self.prefix + name, shape, dt))

    def ps(self, name, shape, dt=F32):
        return self.ctx.enter_context(self.nc.psum_tensor(self.prefix + name, shape, dt))

    def sem(self, name):
        return self.ctx.enter_context(self.nc.semaphore(self.prefix + name))


def build_constants(nc, keep):
    with ExitStack() as ctx:
        st = Stage(nc, ctx, "c_")
        pool_step = st.sem("const_step")
        block = ctx.enter_context(nc.Block())

        @block.gpsimd
        def _(pool):
            ch = Chain(pool, pool_step)
            ch.link(pool.memset(keep["identity"][:, :], 0.0))
            ch.link(pool.affine_select(out=keep["identity"][:, :], in_=keep["identity"][:, :], compare_op=ALU.not_equal,
                                       fill=1.0, base=0, pattern=[[-1, P]], channel_multiplier=1))
            ch.link(pool.tensor_copy(keep["identity16"][:, :], keep["identity"][:, :]))
            ch.link(pool.memset(keep["ones16"][:, :], 1.0))
            ch.link(pool.affine_select(out=keep["before16"][:, :], in_=keep["ones16"][:, :], compare_op=ALU.is_gt,
                                       fill=0.0, base=0, pattern=[[1, P]], channel_multiplier=-1))
            ch.link(pool.memset(keep["zero16"][:, :], 0.0))
            ch.link(pool.affine_select(out=keep["mask_qk"][:, :], in_=keep["zero16"][:, :], compare_op=ALU.is_ge,
                                       fill=NEG, base=0, pattern=[[-1, P]], channel_multiplier=1))
            ch.link(pool.affine_select(out=keep["mask_kq"][:, :], in_=keep["zero16"][:, :], compare_op=ALU.is_ge,
                                       fill=NEG, base=0, pattern=[[1, P]], channel_multiplier=-1))
            ch.link(pool.iota(keep["expert"][:, :, :], pattern=[[1, E], [0, NT]], base=0, channel_multiplier=0,
                              allow_small_or_imprecise_dtypes=True))
            ch.link(pool.iota(keep["expert8"][:, :, :], pattern=[[1, E], [0, NT]], base=E, channel_multiplier=0,
                              allow_small_or_imprecise_dtypes=True))
            for name, span in (("running0", NT), ("running1", NT // B)):
                ch.link(pool.memset(keep[name][:, :, :], 1.0))
                v = keep[name][:, :, :].rearrange("p e (b t) -> p (e b) t", t=span)
                ch.link(pool.memset(v[:, :, 0:1], 0.0))


def first_max(vec, ch, keep, logits, out_max, equal, first, onehot):
    ch.link(vec.tensor_reduce(out_max, logits.rearrange("p e t -> p t e"), X, ALU.max))
    ch.link(vec.tensor_tensor(equal, logits, out_max.unsqueeze(1).to_broadcast([P, E, NT]), ALU.is_equal))
    ch.link(vec.scalar_tensor_tensor(out=equal, in0=equal, scalar=-float(E), in1=keep["expert8"][:, :, :],
                                     op0=ALU.mult, op1=ALU.add))
    ch.link(vec.tensor_reduce(first, equal.rearrange("p e t -> p t e"), X, ALU.min))
    ch.link(vec.tensor_tensor(onehot, keep["expert"][:, :, :], first.unsqueeze(1).to_broadcast([P, E, NT]), ALU.is_equal))


def places(vec, ch, keep, running, tile_before, tile_total, total, scanned, place):
    flat = "p e t -> p (e t)"
    ch.link(vec.tensor_copy(total, tile_total.rearrange("p (e t) -> p e t", e=E)))
    ch.link(vec.tensor_tensor_scan(scanned.rearrange(flat), keep[running][:, :, :].rearrange(flat), total.rearrange(flat),
                                   0.0, ALU.mult, ALU.add))
    ch.link(vec.tensor_tensor(scanned, scanned, total, ALU.subtract))
    ch.link(vec.tensor_tensor(place, scanned, tile_before.rearrange("p (e t) -> p e t", e=E), ALU.add))


def ago(c):
    return c - 1


def chunks_skewed(eng, front, back):
    front(0, 0, 0)
    for i in rounds(eng, NC // 2 - 1):
        front(2 * i + 1, i, 1)
        back(2 * i, i, 0)
        front(2 * i + 2, i + 1, 0)
        back(2 * i + 1, i, 1)
    last = NC // 2 - 1
    front(NC - 1, last, 1)
    back(NC - 2, last, 0)
    back(NC - 1, last, 1)


def low_part(eng, low, src, high):
    return eng.tensor_tensor(low, src, high.bitcast(F32), ALU.subtract)


def inverse_root(vec, ch, out, value, half):
    ch.link(vec.tensor_scalar(value, value, EPS, None, ALU.add))
    ch.link(vec.tensor_scalar(half.bitcast(I32), value.bitcast(I32), 1, None, ALU.logical_shift_right))
    ch.link(vec.tensor_scalar(out.bitcast(I32), half.bitcast(I32), -1.0, float(0x5F3759DF), ALU.mult, ALU.add))
    for _ in range(3):
        ch.link(vec.scalar_tensor_tensor(out=half, in0=out, scalar=-0.5, in1=out, op0=ALU.mult, op1=ALU.mult))
        ch.link(vec.tensor_tensor(half, half, value, ALU.mult))
        ch.link(vec.scalar_tensor_tensor(out=out, in0=half, scalar=1.5, in1=out, op0=ALU.add, op1=ALU.mult))


ROOT_STEPS = 12
NORM_STEPS = ROOT_STEPS + 3


def layer_norm(vec, ch, src, dst, stats, mv, var, half, rstd, spare, before_write):
    for t in range(TC):
        ins = vec.bn_stats(stats[:, t, :], src[:, t, :])
    ch.link(ins)
    vec.memset(spare, 0.0)
    for t in range(TC):
        ins = vec.bn_aggr(mv[:, t, :], stats[:, t, :])
    ch.link(ins)
    ch.link(vec.tensor_copy(var, mv[:, :, 1]))
    inverse_root(vec, ch, rstd, var, half)
    before_write()
    for t in range(TC):
        ins = vec.tensor_scalar(dst[:, t, :], src[:, t, :], mv[:, t, 0:1], rstd[:, t:t + 1], ALU.subtract, ALU.mult)
    return ins


def stage_project(nc, io, keep, dram):
    with ExitStack() as ctx:
        st = Stage(nc, ctx, "p_")
        wqk = st.sb("wqk", [P, 2, KD, D])
        wvr = st.sb("wvr", [P, KD, D + E])
        wqk_r = [st.sb(f"wqk_r{r}", [P, 2, KD, D], F32R) for r in range(2)]
        wvr_r = [st.sb(f"wvr_r{r}", [P, KD, D + E], F32R) for r in range(2)]
        xin = st.sb("xin", [P, 2, TC, D])
        stats = st.sb("stats", [P, 2, TC, 6])
        mv = st.sb("mv", [P, 2, TC, 2])
        var = st.sb("var", [P, 2, TC])
        half = st.sb("half", [P, 2, TC])
        rstd = st.sb("rstd", [P, 2, TC])
        xn = st.sb("xn", [P, 2, TC, D])
        xnt = [[st.sb(f"xnt{r}_{u}", [P, KD, CH], F32R) for r in range(2)] for u in range(2)]
        rest = st.sb("rest", [P, 4, CH])
        parts = st.sb("parts", [P, 4, 3, CH], BF16)
        vout = st.sb("vout", [P, 2, TC, D])
        spare = st.sb("spare", [P, 1])
        logits = st.sb("logits", [P, E, NT])
        top = st.sb("top", [P, NT])
        equal = st.sb("equal", [P, E, NT])
        first = st.sb("first", [P, NT])
        onehot = st.sb("onehot", [P, E, NT])
        onehot16 = st.sb("onehot16", [P, E, NT], BF16)
        shifted = st.sb("shifted", [P, E, NT])
        expd = st.sb("expd", [P, E, NT])
        total = st.sb("total", [P, E, NT])
        scanned = st.sb("scanned", [P, E, NT])
        place = st.sb("place", [P, E, NT])
        small = st.sb("small", [P, 6, NT])
        pst = [st.ps(f"pst{k}", [P, CH]) for k in range(KD)]
        psq = [st.ps(f"psq{k}", [P, CH]) for k in range(4)]
        psv = [st.ps(f"psv{k}", [P, CH]) for k in range(2)]

        weights_landed = st.sem("weights_landed")
        x_landed = [st.sem(f"x_landed{u}") for u in range(2)]
        weights_high = st.sem("weights_high")
        weights_split, xn_ready = st.sem("weights_split"), st.sem("xn_ready")
        turned, high_ready, xnt_ready, xn_kept = (st.sem("turned"), st.sem("high_ready"), st.sem("xnt_ready"),
                                                  st.sem("xn_kept"))
        qk_ready, first_part, rest_ready = st.sem("qk_ready"), st.sem("first_part"), st.sem("rest_ready")
        second_part, parts_ready = st.sem("second_part"), st.sem("parts_ready")
        parts_stored = [st.sem(f"parts_stored{k}") for k in range(4)]
        v_ready, v_copied = st.sem("v_ready"), st.sem("v_copied")
        v_stored = [st.sem(f"v_stored{u}") for u in range(2)]
        dve_step = st.sem("dve_step")
        onehot_ready, counted, shifted_ready, exp_ready = (st.sem("onehot_ready"), st.sem("counted"),
                                                           st.sem("shifted_ready"), st.sem("exp_ready"))
        block = ctx.enter_context(nc.Block())
        x_rows = io["x"].rearrange("b s d -> (b s) d")

        @block.gpsimd
        def _(pool):
            def keep_copy(c, n, u):
                pool.wait_ge(xn_ready, c + 1)
                pool.tensor_copy(keep["xn_all"][:, bass.ds(c * TC, TC), :], xn[:, u, :, :]).then_inc(xn_kept, 1)

            chunks_skewed(pool, keep_copy, lambda c, n, u: None)

        @block.sync
        def _(sp):
            def load(u, c):
                sp.dma_start(xin[:, u, :, :], x_rows[bass.ds(c * CH, CH), :].rearrange("(t p) d -> p t d", p=P)
                             ).then_inc(x_landed[u], 16)

            load(0, 0)
            load(1, 1)
            for n, name in enumerate(("wq", "wk")):
                sp.dma_start(wqk[:, n, :, :], io[name].rearrange("(k p) n -> p k n", p=P)).then_inc(weights_landed, 16)
            sp.dma_start(wvr[:, :, 0:D], io["wv"].rearrange("(k p) n -> p k n", p=P)).then_inc(weights_landed, 16)
            sp.dma_start(wvr[:, :, D:D + E], io["router0"].rearrange("(k p) n -> p k n", p=P)).then_inc(weights_landed, 16)

            def load_again(c, u):
                at = snap(sp, c * CH)
                sp.wait_ge(xn_ready, c - 1)
                sp.dma_start(xin[:, u, :, :], x_rows[bass.ds(at, CH), :].rearrange("(t p) d -> p t d", p=P)
                             ).then_inc(x_landed[u], 16)

            def store(c, u):
                at = snap(sp, c * CH)
                for m in range(4):
                    rows = dram["qk_parts"][m // 2, :, (m % 2) * P:(m % 2 + 1) * P, bass.ds(at, CH)]
                    sp.wait_ge(parts_ready, 4 * c + m + 1)
                    sp.dma_start(rows.rearrange("r p n -> p r n"), parts[:, m, :, :]).then_inc(parts_stored[m], 16)
                sp.wait_ge(v_copied, TC * (c + 1))
                sp.dma_start(dram["v"][bass.ds(at, CH), :].rearrange("(t p) d -> p t d", p=P), vout[:, u, :, :]
                             ).then_inc(v_stored[u], 16)

            load_again(2, 0)
            for i in rounds(sp, NC // 2 - 2):
                for u in range(2):
                    load_again(2 * i + u + 3, 1 - u)
                    store(2 * i + u, u)
            for c in range(NC - 4, NC):
                if c + 3 < NC:
                    load_again(c + 3, 1 - c % 2)
                store(c, c % 2)
            for m in range(4):
                sp.wait_ge(parts_stored[m], 16 * NC)
            for u in range(2):
                sp.wait_ge(v_stored[u], 16 * (NC // 2))

        @block.vector
        def _(vec):
            vec.memset(keep["zero"][:, :], 0.0)
            ch = Chain(vec, dve_step)

            def split_weights():
                vec.wait_ge(weights_landed, 64)
                for n, (hi, lo, src) in enumerate(((wqk_r[0][:, :, :, :], wqk_r[1][:, :, :, :], wqk[:, :, :, :]),
                                                   (wvr_r[0][:, :, :], wvr_r[1][:, :, :], wvr[:, :, :]))):
                    vec.tensor_copy(hi, src).then_inc(weights_high, 1)
                    vec.wait_ge(weights_high, n + 1)
                    low_part(vec, lo, src, hi).then_inc(weights_split, 1)

            def normalise(c, n, u):
                vec.wait_ge(x_landed[u], 16 * (n + 1))

                def before_write():
                    wait(vec, turned, ago(c))
                    wait(vec, xn_kept, ago(c))

                ch.base, ch.k = NORM_STEPS * c, 0
                layer_norm(vec, ch, xin[:, u, :, :], xn[:, u, :, :], stats[:, u, :, :], mv[:, u, :, :], var[:, u, :],
                           half[:, u, :], rstd[:, u, :], spare[:, :], before_write).then_inc(xn_ready, 1)

            def front(c, n, u):
                vec.wait_ge(high_ready, c + 1)
                wait(vec, v_ready, TC * ago(c))
                for k in range(KD):
                    ins = vec.tensor_tensor(xnt[u][1][:, k, :], pst[k][:, :], xnt[u][0][:, k, :].bitcast(F32), ALU.subtract)
                ins.then_inc(xnt_ready, 1)
                if not (isinstance(c, int) and c == NC - 1):
                    normalise(c + 1, n + u, 1 - u)

            def back(c, n, u):
                def rest_of(m):
                    vec.wait_ge(first_part, 4 * c + m + 1)
                    vec.scalar_tensor_tensor(out=rest[:, m, :], in0=psq[m][:, :], scalar=HD ** -0.5 if m < 2 else 1.0,
                                             in1=parts[:, m, 0, :], op0=ALU.mult, op1=ALU.subtract).then_inc(rest_ready, 1)

                def third(m):
                    vec.wait_ge(second_part, 4 * c + m + 1)
                    vec.tensor_tensor(parts[:, m, 2, :], rest[:, m, :], parts[:, m, 1, :], ALU.subtract
                                      ).then_inc(parts_ready, 1)

                for m in range(4):
                    rest_of(m)
                for m in range(4):
                    third(m)

            normalise(0, 0, 0)
            split_weights()
            chunks_skewed(vec, front, back)
            ch.base, ch.k = NORM_STEPS * NC, 0

            vec.wait_ge(v_copied, NT)
            L = logits[:, :, :]
            first_max(vec, ch, keep, L, top[:, :], equal[:, :, :], first[:, :], onehot[:, :, :])
            vec.tensor_copy(onehot16[:, :, :], onehot[:, :, :]).then_inc(onehot_ready, 1)
            vec.tensor_tensor(shifted[:, :, :], L, top[:, :].unsqueeze(1).to_broadcast([P, E, NT]), ALU.subtract
                              ).then_inc(shifted_ready, 1)
            vec.wait_ge(exp_ready, 1)
            den, kept, chosen, clipped, slot = (small[:, k, :] for k in range(5))
            ch.link(vec.tensor_reduce(den, expd[:, :, :].rearrange("p e t -> p t e"), X, ALU.add))
            ch.link(vec.reciprocal(keep["gate"][:, :], den))
            vec.wait_ge(counted, 1)
            places(vec, ch, keep, "running0", psq[0][:, 0:E * NT], psq[1][:, 0:E * NT], total[:, :, :], scanned[:, :, :],
                   place[:, :, :])
            ch.link(vec.tensor_tensor(place[:, :, :], place[:, :, :], onehot[:, :, :], ALU.mult))
            ch.link(vec.tensor_reduce(chosen, place[:, :, :].rearrange("p e t -> p t e"), X, ALU.add))
            ch.link(vec.tensor_scalar(kept, chosen, float(CAP0), None, ALU.is_lt))
            ch.link(vec.tensor_tensor(keep["gate"][:, :], keep["gate"][:, :], kept, ALU.mult))
            ch.link(vec.tensor_scalar(clipped, chosen, float(CAP0 - 1), None, ALU.min))
            ch.link(vec.scalar_tensor_tensor(out=slot, in0=first[:, :], scalar=float(CAP0), in1=clipped,
                                             op0=ALU.mult, op1=ALU.add))
            ch.link(vec.tensor_copy(keep["slot_get"][:, :], slot))
            ch.link(vec.scalar_tensor_tensor(out=clipped, in0=kept, scalar=-SKIP, in1=slot, op0=ALU.mult, op1=ALU.add))
            ch.link(vec.tensor_scalar(keep["slot_put"][:, :], clipped, SKIP, None, ALU.add))

        @block.scalar
        def _(act):
            def front(c, n, u):
                act.wait_ge(turned, c + 1)
                wait(act, v_ready, TC * ago(c))
                act.copy(xnt[u][0][:, 0, :], pst[0][:, :])
                act.copy(xnt[u][0][:, 1, :], pst[1][:, :]).then_inc(high_ready, 1)

            def back(c, n, u):
                def first(m):
                    act.wait_ge(qk_ready, 4 * c + m + 1)
                    wait(act, parts_stored[m], 16 * c)
                    act.activation(parts[:, m, 0, :], psq[m][:, :], ACT.Copy, scale=HD ** -0.5 if m < 2 else 1.0
                                   ).then_inc(first_part, 1)

                def second(m):
                    act.wait_ge(rest_ready, 4 * c + m + 1)
                    act.copy(parts[:, m, 1, :], rest[:, m, :]).then_inc(second_part, 1)

                def take_v(t):
                    act.wait_ge(v_ready, TC * c + t + 1)
                    if t == 0:
                        wait(act, v_stored[u], 16 * n)
                    act.copy(vout[:, u, t, :], psv[t % 2][:, 0:D])
                    act.copy(logits[:, :, bass.ds(c * TC + t, 1)].rearrange("p e t -> p (e t)"),
                             psv[t % 2][:, D:D + E]).then_inc(v_copied, 1)

                for m in range(4):
                    first(m)
                for t in range(TC):
                    take_v(t)
                for m in range(4):
                    second(m)

            chunks_skewed(act, front, back)
            act.wait_ge(shifted_ready, 1)
            act.activation(expd[:, :, :], shifted[:, :, :], ACT.Exp).then_inc(exp_ready, 1)

        @block.tensor
        def _(pe):
            def product(bank, stationary, moving):
                pairs = [(k, a, b) for k in range(KD) for a, b in ((0, 0), (1, 0), (0, 1))]
                for n, (k, a, b) in enumerate(pairs):
                    ins = pe.matmul(bank, stationary(a, k), moving(b, k), start=(n == 0), stop=(n == len(pairs) - 1))
                return ins

            def front(c, n, u):
                pe.wait_ge(xn_ready, c + 1)
                wait(pe, xnt_ready, c)
                for t in range(TC):
                    for k in range(KD):
                        ins = pe.transpose(pst[k][:, t * P:(t + 1) * P], xn[:, u, t, k * P:(k + 1) * P],
                                           keep["identity"][:, :])
                ins.then_inc(turned, 1)

            def back(c, n, u):
                if isinstance(c, int) and c == 0:
                    pe.wait_ge(weights_split, 2)
                pe.wait_ge(xnt_ready, c + 1)
                for m in range(4):
                    wait(pe, rest_ready, 4 * (c - 1) + m + 1)
                    product(psq[m][:, :], lambda r, k: wqk_r[r][:, m // 2, k, (m % 2) * P:(m % 2 + 1) * P],
                            lambda r, k: xnt[u][r][:, k, :]).then_inc(qk_ready, 1)
                for t in range(TC):
                    wait(pe, v_copied, TC * c + t - 1)
                    product(psv[t % 2][:, 0:D + E], lambda r, k: xnt[u][r][:, k, t * P:(t + 1) * P],
                            lambda r, k: wvr_r[r][:, k, :]).then_inc(v_ready, 1)

            chunks_skewed(pe, front, back)
            pe.wait_ge(onehot_ready, 1)
            pe.wait_ge(parts_ready, 4 * NC)
            oh = onehot16[:, :, :].rearrange("p e t -> p (e t)")
            pe.matmul(psq[0][:, 0:E * NT], keep["before16"][:, :], oh, start=True, stop=True)
            pe.matmul(psq[1][:, 0:E * NT], keep["ones16"][:, :], oh, start=True, stop=True).then_inc(counted, 1)


def attention_steps():
    maxima, ends = [], []
    for c in range(QC):
        for h in range(GH):
            for i in range(TC * c, TC * c + TC):
                for k in range(c + 1):
                    maxima.append((h, i, k))
        ends.append(len(maxima))

    def cost(u):
        return 90 + min(CH, (u[1] + 1) * P - u[2] * CH)

    def width(c, j):
        return CH - max(0, j - TC * c) * P

    whole = sum(cost(u) for u in maxima)
    lead, at = 0, 0
    while at < LEAD * whole:
        at += cost(maxima[lead])
        lead += 1

    def flow(lo, hi, dg):
        for n in range(lo, hi):
            yield ("A", dg, *maxima[n])
            if n + 1 in ends:
                c = ends.index(n + 1)
                yield ("M", dg, c)
                yield ("MT", dg, c)

    def weave(ahead):
        pairs = [(c, j) for c in range(QC) for j in range(TC * (c + 1))]
        total = sum(width(*p) for p in pairs) * GH
        ahead, steps, done, ahead_done, late = list(ahead), [], 0, 0, []

        def advance():
            nonlocal ahead_done
            while ahead and ahead_done * total < done * whole:
                u = ahead.pop(0)
                if u[0] == "A":
                    ahead_done += cost(u[2:])
                if u[0] == "MT":
                    late.append([u, 6])
                else:
                    steps.append(u)

        for n, (c, j) in enumerate(pairs):
            for h in range(GH):
                steps.append(("S", c, j, h))
                done += width(c, j)
                advance()
                for item in late:
                    item[1] -= 1
                while late and late[0][1] <= 0:
                    steps.append(late.pop(0)[0])
            if n:
                pc, pj = pairs[n - 1]
                steps.append(("PV", pc, pj))
                if pj == TC * (pc + 1) - 1:
                    steps.append(("COPY", pc))
                    late.append([("O", pc), 6])
        c, j = pairs[-1]
        steps += ahead + [u for u, _ in late] + [("PV", c, j), ("COPY", c), ("O", c)]
        return steps

    head = list(flow(0, lead, 0))
    stream = list(flow(lead, len(maxima), 0)) + list(flow(0, lead, 1))
    return head, weave(stream), weave(flow(lead, len(maxima), 0))


RING = 3


LEAD = 0.5


def stage_attention(nc, io, keep, dram):
    head, steps, last_steps = attention_steps()
    in_ring = ("A", "MT", "O")
    r_head, n_ring = (sum(u[0] in in_ring for u in order) for order in (head, steps))
    m_head = sum(u[0] == "M" for u in head)
    n_s = sum(u[0] == "S" for u in steps) // 2
    n_pv = sum(u[0] == "PV" for u in steps)
    parts_q, parts_k = (0, 0, 1, 1, 0, 2), (0, 1, 0, 1, 2, 0)
    n_loads = len(parts_q) * QC + len(parts_k)
    with ExitStack() as ctx:
        st = Stage(nc, ctx, "a_")
        qa = [st.sb(f"qa{u}", [MR, QC, GH, CH], BF16) for u in range(2)]
        kb = [st.sb(f"kb{u}", [MR, GH, S], BF16) for u in range(2)]
        vg = [st.sb(f"vg{u}", [P, KT, GH, 32]) for u in range(2)]
        probs = st.sb("probs", [P, 4, 2, CH])
        best = st.sb("best", [P, QC, GH * TC, QC])
        neg = st.sb("neg", [P, GH * TC])
        neg_rest = st.sb("neg_rest", [P, GH * TC])
        neg_parts = st.sb("neg_parts", [P, P // (GH * TC), GH * TC], BF16)
        neg_rows = st.sb("neg_rows", [3 * GH * TC, 2, P], BF16)
        sums = st.sb("sums", [P, CH])
        inv = st.sb("inv", [P, TC, GH])
        oout = st.sb("oout", [P, 2, TC, GH, HD])
        ring = [st.ps(f"ring{k}", [P, CH]) for k in range(RING)]
        pss = [st.ps(f"pss{k}", [P, 2, CH]) for k in range(2)]
        acc = st.ps("acc", [P, CH])

        loaded = [st.sem(f"loaded{u}") for u in range(2)]
        first_k, first_q = st.sem("first_k"), [st.sem(f"first_q{c}") for c in range(QC)]
        v_loaded = [st.sem(f"v_loaded{u}") for u in range(2)]
        set_up, ones_set = st.sem("set_up"), st.sem("ones_set")
        ring_full, ring_taken = st.sem("ring_full"), st.sem("ring_taken")
        s_ready, exp_done, pv_done = st.sem("s_ready"), st.sem("exp_done"), st.sem("pv_done")
        sums_copied = st.sem("sums_copied")
        m_split = st.sem("m_split")
        m_landed = [st.sem(f"m_landed{c}") for c in range(QC)]
        o_stored = [st.sem(f"o_stored{c}") for c in range(2)]
        dve_step = st.sem("dve_step")
        cleared, scattered = st.sem("cleared"), st.sem("scattered")
        block = ctx.enter_context(nc.Block())

        def bank_of(u, r):
            assert 2 * n_ring % RING == 0
            return ring[(r_head + u * n_ring + r) % RING]

        primed = 1

        def groups(eng):
            with eng.Fori(0, HG - 1) as i:
                for u in range(2):
                    yield 2 * i + u, i, u, steps
            for u in range(2):
                yield 2 * (HG - 1) + u, HG - 1, u, (steps, last_steps)[u]

        def load_q(eng, first, u, signals):
            for c in range(QC):
                for r, part in enumerate(parts_q):
                    eng.dma_start(qa[u][r * HD:(r + 1) * HD, c, :, :],
                                  dram["qk_parts"][0, part, bass.ds(first, GH * HD), u * S + c * CH:u * S + (c + 1) * CH]
                                  .rearrange("(h d) n -> d h n", d=HD)).then_inc(signals[c], 16)

        def load_k(eng, first, u, signal):
            for r, part in enumerate(parts_k):
                eng.dma_start(kb[u][r * HD:(r + 1) * HD, :, :],
                              dram["qk_parts"][1, part, bass.ds(first, GH * HD), u * S:(u + 1) * S]
                              .rearrange("(h d) n -> d h n", d=HD)).then_inc(signal, 16)

        @block.gpsimd
        def _(pool):
            ch = Chain(pool, set_up)
            for u in range(2):
                ch.link(pool.memset(vg[u][:, :, :, :], 0.0))
                ch.link(pool.memset(vg[u][:, :, :, HD:HD + 1], 1.0))
            for u in range(2):
                pool.memset(kb[u][QR:MR, :, :], 1.0).then_inc(ones_set, 1)
            table = dram["expert_in"].rearrange("(p a) d -> p (a d)", p=P)
            n = table.shape[1] // CH
            for k in range(n):
                pool.dma_start(table[:, k * CH:(k + 1) * CH], keep["zero"][:, :]).then_inc(cleared, 16)
            pool.wait_ge(cleared, 16 * n)
            for t in range(NT):
                pool.indirect_dma_start(dram["expert_in"], bass.IndirectOffsetOnAxis(ap=keep["slot_put"][:, t:t + 1], axis=0),
                                        keep["xn_all"][:, t, :], None, bounds_check=E * CAP0 - 1, oob_is_err=False
                                        ).then_inc(scattered, 16)
            pool.wait_ge(scattered, 16 * NT)

        @block.sync
        def _(sp):
            def load(first, u):
                load_q(sp, first, u, [loaded[u]] * QC)
                load_k(sp, first, u, loaded[u])
                load_v(first, u)

            def load_v(first, u):
                for h in range(GH):
                    sp.dma_start(vg[u][:, :, h, 0:HD],
                                 dram["v"][u * S:(u + 1) * S, bass.ds(first + h * HD, HD)]
                                 .rearrange("(j p) d -> p j d", p=P)).then_inc(v_loaded[u], 16)

            def store_rows(u, c, r):
                sp.wait_ge(ring_taken, r + 1)
                for part in range(3):
                    sp.dma_start(qa[u][QR + part:QR + part + 1, c, :, :].rearrange("o h (i q) -> o (h i) q", q=P),
                                 neg_rows[part * GH * TC:(part + 1) * GH * TC, c % 2, :]
                                 ).then_inc(m_landed[c], 16)

            load_q(sp, 0, 0, first_q)
            sp.wait_ge(set_up, 4)
            load_v(0, 0)
            for r, s in enumerate(s for s in head if s[0] in in_ring):
                if s[0] == "MT":
                    store_rows(0, s[2], r)
            for g, i, u, order in groups(sp):
                if not (isinstance(g, int) and g == 2 * HG - 1):
                    first = snap(sp, (i + u) * GH * HD)
                    sp.wait_ge(pv_done, primed + g * n_pv)
                    load(first, 1 - u)
                for r, s in enumerate(s for s in order if s[0] in in_ring):
                    if s[0] == "MT":
                        store_rows((u + s[1]) % 2, s[2], r_head + g * n_ring + r)
            for c in range(2):
                sp.wait_ge(o_stored[c], 16 * (primed + QC * HG))

        @block.tensor
        def _(pe):
            def a_step(u, s, r, bank):
                _, dg, h, i, k = s
                keys = min(CH, (i + 1) * P - k * CH)
                diagonal = k == i // TC
                wait(pe, ring_taken, r + 1 - RING)
                ins = pe.matmul(bank[:, 0:keys], qa[u][0:QR, i // TC, h, (i % TC) * P:(i % TC + 1) * P],
                                kb[u][0:QR, h, k * CH:k * CH + keys], start=True, stop=not diagonal)
                if diagonal:
                    ins = pe.matmul(bank[:, keys - P:keys], keep["identity16"][:, :], keep["mask_qk"][:, :],
                                    start=False, stop=True)
                ins.then_inc(ring_full, 1)

            def m_turn(n, r, bank):
                pe.wait_ge(m_split, n + 1)
                wait(pe, ring_taken, r + 1 - RING)
                pe.transpose(bank[:, 0:P // 2].bitcast(BF16), neg_parts[:, :, :].rearrange("p r n -> p (r n)"),
                             keep["identity16"][:, :]).then_inc(ring_full, 1)

            pe.nop().then_inc(pv_done, primed)
            pe.wait_ge(first_k, 16 * len(parts_k))
            m, chunk = 0, -1
            for r, s in enumerate(s for s in head if s[0] in in_ring):
                if s[0] == "A":
                    if s[3] // TC != chunk:
                        chunk = s[3] // TC
                        pe.wait_ge(first_q[chunk], 16 * len(parts_q))
                    a_step(0, s, r, ring[r % RING])
                if s[0] == "MT":
                    m_turn(m, r, ring[r % RING])
                    m += 1
            pe.wait_ge(set_up, 4)
            pe.wait_ge(ones_set, 2)
            for g, i, u, order in groups(pe):
                idx = pv = m = r = 0
                next_seen = False
                for s in order:
                    if s[0] == "A":
                        if s[1] == 1 and not next_seen:
                            next_seen = True
                            pe.wait_ge(loaded[1 - u], 16 * n_loads * (i + 1))
                        a_step((u + s[1]) % 2, s, r_head + g * n_ring + r, bank_of(u, r))
                        r += 1
                    elif s[0] == "MT":
                        m_turn(m_head + g * QC + m, r_head + g * n_ring + r, bank_of(u, r))
                        m += 1
                        r += 1
                    elif s[0] == "S":
                        _, c, j, h = s
                        e = h % 2
                        lo = max(0, j - TC * c) * P
                        if j == 0 and h == 0:
                            pe.wait_ge(m_landed[c], 48 * (g + 1))
                        if e == 0:
                            pe.wait_ge(exp_done, primed + g * n_s + max(idx - 1, 0))
                        ins = pe.matmul(pss[idx % 2][:, e, lo:CH], kb[u][0:MR, h, j * P:(j + 1) * P],
                                        qa[u][0:MR, c, h, lo:CH], start=True, stop=(j < TC * c))
                        if j >= TC * c:
                            ins = pe.matmul(pss[idx % 2][:, e, lo:lo + P], keep["identity16"][:, :],
                                            keep["mask_kq"][:, :], start=False, stop=True)
                        if e == 1:
                            ins.then_inc(s_ready, 1)
                            idx += 1
                    elif s[0] == "PV":
                        _, c, j = s
                        lo = max(0, j - TC * c) * P
                        pe.wait_ge(exp_done, primed + g * n_s + 2 * pv + 2)
                        if c == 0 and j == 0:
                            pe.wait_ge(v_loaded[u], 16 * GH * (i + 1))
                        if j == 0:
                            pe.wait_ge(sums_copied, primed + g * QC + c)
                        for h in range(GH):
                            ins = pe.matmul(acc[32 * h:32 * h + 32, lo:CH], vg[u][:, j, h, :],
                                            probs[:, 2 * (pv % 2) + h // 2, h % 2, lo:CH],
                                            start=(j == 0), stop=(j == TC * (c + 1) - 1))
                        ins.then_inc(pv_done, 1)
                        pv += 1
                    elif s[0] == "O":
                        c = s[1]
                        pe.wait_ge(sums_copied, primed + g * QC + c + 1)
                        pe.wait_ge(ring_taken, r_head + g * n_ring + r + 1 - RING)
                        for t in range(TC):
                            ins = pe.transpose(bank_of(u, r)[:, t * P:(t + 1) * P], sums[:, t * P:(t + 1) * P],
                                               keep["identity"][:, :])
                        ins.then_inc(ring_full, 1)
                        r += 1

        @block.scalar
        def _(act):
            def store(g, i, u, c, r):
                act.wait_ge(ring_taken, r_head + g * n_ring + r + 1)
                act.dma_start(dram["attn0"][u * S + c * CH:u * S + (c + 1) * CH, bass.ds(i * GH * HD, GH * HD)]
                              .rearrange("(t p) d -> p t d", p=P),
                              oout[:, c % 2, :, :, :].rearrange("p t h d -> p t (h d)")).then_inc(o_stored[c % 2], 16)

            load_k(act, 0, 0, first_k)
            act.nop().then_inc(exp_done, primed)
            act.nop().then_inc(sums_copied, primed)
            for c in range(2):
                act.nop().then_inc(o_stored[c], 16 * primed)
            for g, i, u, order in groups(act):
                idx = r = pv = r_turn = 0
                turned_at = None
                for s in order:
                    if turned_at and idx >= turned_at[0] + 3:
                        store(g, i, u, *turned_at[1:])
                        turned_at = None
                    if s[0] == "O":
                        turned_at, r_turn = (idx, s[1], r), r + 1
                    if s[0] == "S" and s[3] % 2 == 1:
                        _, c, j, h = s
                        lo = max(0, j - TC * c) * P
                        act.wait_ge(s_ready, g * n_s + idx + 1)
                        act.wait_ge(pv_done, primed + g * n_pv + max(idx // 2 - 1, 0))
                        act.activation(probs[:, idx % 4, :, lo:CH], pss[idx % 2][:, :, lo:CH], ACT.Exp).then_inc(exp_done, 1)
                        idx += 1
                    elif s[0] == "PV":
                        pv += 1
                    elif s[0] == "COPY":
                        act.wait_ge(pv_done, primed + g * n_pv + pv)
                        act.wait_ge(ring_full, r_head + g * n_ring + r_turn)
                        act.copy(sums[:, :], acc[:, :]).then_inc(sums_copied, 1)
                    elif s[0] in in_ring:
                        r += 1
                store(g, i, u, *turned_at[1:])

        @block.vector
        def _(vec):
            ch = Chain(vec, dve_step)
            per_group = 4 * QC + QC
            ch_head = 4 * m_head + 1

            def take(s, r, bank):
                _, _, h, i, k = s
                keys = min(CH, (i + 1) * P - k * CH)
                vec.wait_ge(ring_full, r + 1)
                vec.tensor_reduce(best[:, i // TC, h * TC + i % TC, k:k + 1], bank[:, 0:keys], X, ALU.max
                                  ).then_inc(ring_taken, 1)

            def split(c, r):
                vec.wait_ge(ring_taken, r)
                ch.link(vec.tensor_reduce(neg[:, :], best[:, c, :, 0:c + 1], X, ALU.max, negate=True))
                ch.link(vec.tensor_copy(neg_parts[:, 0, :], neg[:, :]))
                ch.link(vec.tensor_tensor(neg_rest[:, :], neg[:, :], neg_parts[:, 0, :], ALU.subtract))
                ch.link(vec.tensor_copy(neg_parts[:, 1, :], neg_rest[:, :]))
                vec.tensor_tensor(neg_parts[:, 2, :], neg_rest[:, :], neg_parts[:, 1, :], ALU.subtract).then_inc(m_split, 1)

            def take_rows(c, r, bank, landed):
                vec.wait_ge(ring_full, r + 1)
                wait(vec, m_landed[(c - 2) % QC], landed)
                vec.tensor_copy(neg_rows[:, c % 2, :], bank[0:3 * GH * TC, 0:P // 2].bitcast(BF16)).then_inc(ring_taken, 1)

            ch.link(vec.memset(neg_parts[:, :, :], 0.0))
            r = 0
            for s in head:
                if s[0] == "A":
                    take(s, r, ring[r % RING])
                elif s[0] == "M":
                    split(s[2], r)
                elif s[0] == "MT":
                    take_rows(s[2], r, ring[r % RING], 0)
                r += s[0] in in_ring
            for g, i, u, order in groups(vec):
                ch.base, ch.k = ch_head + g * per_group, 0
                r = 0
                for s in order:
                    at, bank = r_head + g * n_ring + r, bank_of(u, r)
                    if s[0] == "A":
                        take(s, at, bank)
                    elif s[0] == "M":
                        split(s[2], at)
                    elif s[0] == "MT":
                        _, dg, c = s
                        take_rows(c, at, bank, 48 * (g + dg + (c >= 2)))
                    elif s[0] == "O":
                        c = s[1]
                        vec.wait_ge(ring_full, at + 1)
                        t4 = bank[:, :].rearrange("p (t h x) -> p t h x", t=TC, h=GH)
                        ch.link(vec.reciprocal(inv[:, :, :], t4[:, :, :, HD:HD + 1].rearrange("p t h x -> p t (h x)")))
                        vec.wait_ge(o_stored[c % 2], 16 * (primed + 2 * g + c // 2))
                        vec.tensor_tensor(oout[:, c % 2, :, :, :], t4[:, :, :, 0:HD],
                                          inv[:, :, :].unsqueeze(3).to_broadcast([P, TC, GH, HD]), ALU.mult
                                          ).then_inc(ring_taken, 1)
                    r += s[0] in in_ring


def stage_experts(nc, io, keep, dram):
    ST = CAP0 // P
    PIECES = 2 * KD
    with ExitStack() as ctx:
        st = Stage(nc, ctx, "e_")
        w1 = [st.sb(f"w1_{u}", [P, KD, F]) for u in range(2)]
        w2 = [st.sb(f"w2_{u}", [P, FT, D]) for u in range(2)]
        w1_r = [[st.sb(f"w1_r{u}_{r}", [P, KD, F], F32R) for r in range(2)] for u in range(2)]
        w2_r = [[st.sb(f"w2_r{u}_{r}", [P, FT, D], F32R) for r in range(2)] for u in range(2)]
        rows = st.sb("rows", [P, 2, ST, D])
        rows_r = [[st.sb(f"rows_r{u}_{r}", [P, KD, CAP0], F32R) for r in range(2)] for u in range(2)]
        gelu = st.sb("gelu", [P, 4, CAP0])
        hidden = [[st.sb(f"hidden{u}_{r}", [P, FT, CAP0], F32R) for r in range(2)] for u in range(2)]
        yout = st.sb("yout", [P, ST, D])
        pst = [st.ps(f"pst{k}", [P, CAP0]) for k in range(KD)]
        psh = [st.ps(f"psh{k}", [P, CAP0]) for k in range(4)]
        psy = [st.ps(f"psy{k}", [P, D]) for k in range(2)]
        landed = [st.sem(f"landed{u}") for u in range(2)]
        w_high, w_ready, first_w_ready = st.sem("w_high"), st.sem("w_ready"), st.sem("first_w_ready")
        turned, turn_high, rows_ready = st.sem("turned"), st.sem("turn_high"), st.sem("rows_ready")
        h_ready, gelu_ready = st.sem("h_ready"), st.sem("gelu_ready")
        h_high, hidden_ready = st.sem("h_high"), st.sem("hidden_ready")
        y_ready, y_taken, stored = st.sem("y_ready"), st.sem("y_taken"), st.sem("stored")
        block = ctx.enter_context(nc.Block())
        w1_rows = io["w1"].rearrange("e d f -> (e d) f")
        w2_rows = io["w2"].rearrange("e f d -> (e f) d")

        def experts(eng):
            for i in rounds(eng, E // 2 - 1):
                for u in range(2):
                    yield 2 * i + u, u, i, False
            for u in range(2):
                yield E - 2 + u, u, E // 2 - 1, u == 1

        def weight_piece(u, m):
            if m < KD:
                return w1[u][:, m, :], w1_r[u][0][:, m, :], w1_r[u][1][:, m, :]
            some = slice((m - KD) * FT // KD, (m - KD + 1) * FT // KD)
            return w2[u][:, some, :], w2_r[u][0][:, some, :], w2_r[u][1][:, some, :]

        def low_piece(eng, e, u, m, ready):
            src, high, low = weight_piece(u, m)
            eng.wait_ge(w_high, PIECES * e + m + 1)
            eng.tensor_tensor(low, src, high.bitcast(F32), ALU.subtract).then_inc(ready, 1)

        @block.sync
        def _(sp):
            for i in rounds(sp, E // 2):
                for u in range(2):
                    e = 2 * i + u
                    slots, ins, outs = snap(sp, e * CAP0), snap(sp, e * D), snap(sp, e * F)
                    wait(sp, h_ready, FT * (e - 1))
                    sp.dma_start(rows[:, u, :, :], dram["expert_in"][bass.ds(slots, CAP0), :]
                                 .rearrange("(t p) d -> p t d", p=P)).then_inc(landed[u], 16)
                    sp.dma_start(w1[u][:, :, :], w1_rows[bass.ds(ins, D), :].rearrange("(k p) f -> p k f", p=P)
                                 ).then_inc(landed[u], 16)
                    sp.dma_start(w2[u][:, :, :], w2_rows[bass.ds(outs, F), :].rearrange("(k p) d -> p k d", p=P)
                                 ).then_inc(landed[u], 16)

        @block.gpsimd
        def _(pool):
            for e, u, i, last in experts(pool):
                if not last:
                    for m in range(PIECES):
                        low_piece(pool, e + 1, 1 - u, m, w_ready)
                pool.wait_ge(y_taken, ST * (e + 1))
                pool.dma_start(dram["expert_out"][bass.ds(e * CAP0, CAP0), :].rearrange("(t p) d -> p t d", p=P),
                               yout[:, :, :]).then_inc(stored, 16)
            pool.wait_ge(stored, 16 * E)

        @block.tensor
        def _(pe):
            def turn(e, u, landed_count):
                pe.wait_ge(landed[u], landed_count)
                wait(pe, rows_ready, e)
                for t in range(ST):
                    for k in range(KD):
                        ins = pe.transpose(pst[k][:, t * P:(t + 1) * P], rows[:, u, t, k * P:(k + 1) * P],
                                           keep["identity"][:, :])
                ins.then_inc(turned, 1)

            turn(0, 0, 48)
            for e, u, i, last in experts(pe):
                pe.wait_ge(rows_ready, e + 1)
                if isinstance(e, int) and e == 0:
                    pe.wait_ge(first_w_ready, PIECES)
                else:
                    pe.wait_ge(w_ready, PIECES * e)
                for f in range(FT):
                    wait(pe, gelu_ready, FT * e + f - 3)
                    pairs = [(k, a, b) for k in range(KD) for a, b in PARTS]
                    for n, (k, a, b) in enumerate(pairs):
                        ins = pe.matmul(psh[f % 4][:, :], w1_r[u][a][:, k, f * P:(f + 1) * P], rows_r[u][b][:, k, :],
                                        start=(n == 0), stop=(n == len(pairs) - 1))
                    ins.then_inc(h_ready, 1)
                if not last:
                    turn(e + 1, 1 - u, 48 * (i + 1 + u))
                for t in range(ST):
                    wait(pe, y_taken, ST * e + t - 1)
                    for f in range(FT):
                        if t == 0:
                            pe.wait_ge(hidden_ready, FT * e + f + 1)
                        for a, b in PARTS:
                            ins = pe.matmul(psy[t % 2][:, :], hidden[u][a][:, f, t * P:(t + 1) * P], w2_r[u][b][:, f, :],
                                            start=(f == 0 and (a, b) == PARTS[0]),
                                            stop=(f == FT - 1 and (a, b) == PARTS[-1]))
                    ins.then_inc(y_ready, 1)

        @block.scalar
        def _(act):
            def high_piece(u, m):
                src, high, _ = weight_piece(u, m)
                act.copy(high, src).then_inc(w_high, 1)

            def high_rows(e, u):
                act.wait_ge(turned, e + 1)
                wait(act, h_ready, FT * (e - 1))
                act.copy(rows_r[u][0][:, 0, :], pst[0][:, :])
                act.copy(rows_r[u][0][:, 1, :], pst[1][:, :]).then_inc(turn_high, 1)

            high_rows(0, 0)
            for m in range(PIECES):
                high_piece(0, m)
            for e, u, i, last in experts(act):
                for f in range(FT):
                    act.wait_ge(h_ready, FT * e + f + 1)
                    wait(act, hidden_ready, FT * e + f - 3)
                    act.activation(gelu[:, f % 4, :], psh[f % 4][:, :], ACT.Gelu_apprx_tanh).then_inc(gelu_ready, 1)
                    if f == 0:
                        wait(act, y_ready, ST * (e - 1))
                    act.wait_ge(gelu_ready, FT * e + f + 1)
                    act.copy(hidden[u][0][:, f, :], gelu[:, f % 4, :]).then_inc(h_high, 1)
                    if f in (3, 6) and not last:
                        if f == 3:
                            act.wait_ge(landed[1 - u], 48 * (i + 1 + u))
                            wait(act, y_ready, ST * e)
                        high_piece(1 - u, f // 4)
                if not last:
                    high_rows(e + 1, 1 - u)
                    for m in range(2, PIECES):
                        high_piece(1 - u, m)

        @block.vector
        def _(vec):
            def low_rows(e, u):
                vec.wait_ge(turn_high, e + 1)
                for k in range(KD):
                    ins = vec.tensor_tensor(rows_r[u][1][:, k, :], pst[k][:, :], rows_r[u][0][:, k, :].bitcast(F32),
                                            ALU.subtract)
                ins.then_inc(rows_ready, 1)

            low_rows(0, 0)
            for m in range(PIECES):
                low_piece(vec, 0, 0, m, first_w_ready)
            for e, u, i, last in experts(vec):
                for f in range(FT):
                    vec.wait_ge(h_high, FT * e + f + 1)
                    vec.tensor_tensor(hidden[u][1][:, f, :], gelu[:, f % 4, :], hidden[u][0][:, f, :].bitcast(F32),
                                      ALU.subtract).then_inc(hidden_ready, 1)
                if not last:
                    low_rows(e + 1, 1 - u)
                for t in range(ST):
                    vec.wait_ge(y_ready, ST * e + t + 1)
                    if t == 0:
                        wait(vec, stored, 16 * e)
                    vec.tensor_copy(yout[:, t, :], psy[t % 2][:, :]).then_inc(y_taken, 1)


def stage_join(nc, io, keep, dram):
    with ExitStack() as ctx:
        st = Stage(nc, ctx, "j_")
        wo = st.sb("wo", [P, KD, D])
        wr = st.sb("wr", [P, KD, E])
        oin = st.sb("oin", [P, 2, TC, D])
        xin = st.sb("xin", [P, 2, TC, D])
        yin = st.sb("yin", [P, 2, TC, D])
        ot = st.sb("ot", [P, 2, KD, CH])
        silu = st.sb("silu", [P, 2, TC, D])
        x1 = st.sb("x1", [P, 2, TC, D])
        xn = st.sb("xn", [P, 2, TC, D])
        xnt = st.sb("xnt", [P, 2, KD, CH])
        stats = st.sb("stats", [P, 2, TC, 6])
        mv = st.sb("mv", [P, 2, TC, 2])
        var = st.sb("var", [P, 2, TC])
        half = st.sb("half", [P, 2, TC])
        rstd = st.sb("rstd", [P, 2, TC])
        spare = st.sb("spare", [P, 1])
        logits = st.sb("logits", [P, E, NT])
        names3 = ("equal", "onehot0", "onehot1", "both", "masked", "total", "scanned", "place", "fits")
        big = {n: st.sb("r_" + n, [P, E, NT]) for n in names3}
        both16 = st.sb("both16", [P, E, NT], BF16)
        small = {n: st.sb("s_" + n, [P, NT]) for n in ("top0", "top1", "first0", "first1", "gap", "ratio", "den", "w0", "w1")}
        pst = [st.ps(f"pst{k}", [P, CH]) for k in range(KD)]
        psx = [st.ps(f"psx{k}", [P, CH]) for k in range(KD)]
        pss = [st.ps(f"pss{k}", [P, 2, D]) for k in range(2)]
        psl = st.ps("psl", [P, TC, E])
        psc = st.ps("psc", [P, 2, E * NT])
        EARLY = 6
        piece = st.sb("piece", [P, EARLY, J])
        pieces = []
        for k in range(KD):
            for n in range(3):
                at = slice(n * J, (n + 1) * J)
                pieces.append((io["w_qkv"][k * P:(k + 1) * P, at], *(keep["wqkv"][r][:, k, at] for r in range(2))))
            for n in range(E * D // J):
                es = slice(n * J // D, (n + 1) * J // D)
                pieces.append((io["we"][es, k * P:(k + 1) * P, :].rearrange("e p d -> p e d"),
                               *(keep["we"][r][:, k, es, :].rearrange("p e d -> p (e d)") for r in range(2))))
        piece_turns = {0: (0, 1, 2), 1: (3, 4, 5), NC - 2: (6, 7), NC - 1: (8, 9)}
        piece_landed = [st.sem(f"piece_landed{m}") for m in range(EARLY)]
        piece_high, piece_ready, wout_landed = st.sem("piece_high"), st.sem("piece_ready"), st.sem("wout_landed")

        weights_landed = st.sem("weights_landed")
        in_landed = [st.sem(f"in_landed{u}") for u in range(2)]
        y_landed = [st.sem(f"y_landed{u}") for u in range(2)]
        o_turned, ot_ready, s_ready, silu_ready = (st.sem("o_turned"), st.sem("ot_ready"), st.sem("s_ready"),
                                                   st.sem("silu_ready"))
        s_taken = st.sem("s_taken")
        x1_ready = st.sem("x1_ready")
        xn_ready = st.sem("xn_ready")
        x_turned, xnt_ready, l_ready, l_taken = st.sem("x_turned"), st.sem("xnt_ready"), st.sem("l_ready"), st.sem("l_taken")
        x1_stored = [st.sem(f"x1_stored{u}") for u in range(2)]
        xnt_stored = [st.sem(f"xnt_stored{u}") for u in range(2)]
        dve_step = st.sem("dve_step")
        onehot_ready, counted, gap_ready, ratio_ready = (st.sem("onehot_ready"), st.sem("counted"), st.sem("gap_ready"),
                                                         st.sem("ratio_ready"))
        block = ctx.enter_context(nc.Block())
        x_rows = io["x"].rearrange("b s d -> (b s) d")

        def tiles(rows, c):
            return rows[bass.ds(c * CH, CH), :].rearrange("(t p) d -> p t d", p=P)

        @block.sync
        def _(sp):
            sp.dma_start(wo[:, :, :], io["wo"].rearrange("(k p) n -> p k n", p=P)).then_inc(weights_landed, 16)
            sp.dma_start(wr[:, :, :], io["router1"].rearrange("(k p) n -> p k n", p=P)).then_inc(weights_landed, 16)

            def load(c, u):
                sp.dma_start(oin[:, u, :, :], tiles(dram["attn0"], c)).then_inc(in_landed[u], 16)
                sp.dma_start(xin[:, u, :, :], tiles(x_rows, c)).then_inc(in_landed[u], 16)

            def store(c, u):
                sp.wait_ge(x1_ready, c + 1)
                sp.dma_start(tiles(dram["x1"], c), x1[:, u, :, :]).then_inc(x1_stored[u], 16)

            load(0, 0)
            load(1, 1)

            def load_piece(m):
                into = piece[:, m % EARLY, :]
                if len(pieces[m][0].shape) == 3:
                    into = into.rearrange("p (e d) -> p e d", d=D)
                if m >= EARLY:
                    sp.wait_ge(piece_ready, m - EARLY + 1)
                sp.dma_start(into, pieces[m][0]).then_inc(piece_landed[m % EARLY], 16)

            for m in range(EARLY):
                load_piece(m)
            sp.dma_start(keep["wout"][:, :, :], io["w_out"].rearrange("(k p) n -> p k n", p=P)).then_inc(wout_landed, 16)
            with sp.Fori(0, NC // 2 - 1) as i:
                for u in range(2):
                    store(2 * i + u, u)
                    load(2 * i + u + 2, u)
            for m in range(EARLY, len(pieces)):
                load_piece(m)
            store(NC - 2, 0)
            store(NC - 1, 1)
            for u in range(2):
                sp.wait_ge(x1_stored[u], 16 * (NC // 2))
                sp.wait_ge(xnt_stored[u], 16 * (NC // 2))
            sp.wait_ge(wout_landed, 16)

        @block.gpsimd
        def _(pool):
            def low_piece(m):
                pool.wait_ge(piece_high, m + 1)
                low_part(pool, pieces[m][2], piece[:, m % EARLY, :], pieces[m][1]).then_inc(piece_ready, 1)

            for c in range(NC):
                u = c % 2
                if c >= 2:
                    pool.wait_ge(y_landed[u], 16 * TC * (c // 2))
                    pool.wait_ge(silu_ready, c - 1)
                for t in range(TC):
                    n = c * TC + t
                    pool.indirect_dma_start(yin[:, u, t, :], None, dram["expert_out"],
                                            bass.IndirectOffsetOnAxis(ap=keep["slot_get"][:, n:n + 1], axis=0)
                                            ).then_inc(y_landed[u], 16)
                if 1 <= c <= EARLY:
                    low_piece(c - 1)
            for m in range(EARLY, len(pieces)):
                low_piece(m)

        @block.tensor
        def _(pe):
            pe.wait_ge(weights_landed, 32)

            def logits_of(c, u):
                pe.wait_ge(xnt_ready, c + 1)
                wait(pe, l_taken, c)
                for t in range(TC):
                    for k in range(KD):
                        ins = pe.matmul(psl[:, t, :], xnt[:, u, k, t * P:(t + 1) * P], wr[:, k, :],
                                        start=(k == 0), stop=(k == KD - 1))
                ins.then_inc(l_ready, 1)

            def front(c, n, u):
                pe.wait_ge(in_landed[u], 32 * (n + 1))
                wait(pe, ot_ready, c)
                for t in range(TC):
                    for k in range(KD):
                        ins = pe.transpose(pst[k][:, t * P:(t + 1) * P], oin[:, u, t, k * P:(k + 1) * P],
                                           keep["identity"][:, :])
                ins.then_inc(o_turned, 1)
                if not (isinstance(c, int) and c < 2):
                    logits_of(c - 2, u)
                pe.wait_ge(ot_ready, c + 1)
                wait(pe, s_taken, c)
                for t in range(TC):
                    for k in range(KD):
                        ins = pe.matmul(pss[t // 2][:, t % 2, :], ot[:, u, k, t * P:(t + 1) * P], wo[:, k, :],
                                        start=(k == 0), stop=(k == KD - 1))
                ins.then_inc(s_ready, 1)

            def back(c, n, u):
                pe.wait_ge(xn_ready, c + 1)
                wait(pe, xnt_ready, c)
                for t in range(TC):
                    for k in range(KD):
                        ins = pe.transpose(psx[k][:, t * P:(t + 1) * P], xn[:, u, t, k * P:(k + 1) * P],
                                           keep["identity"][:, :])
                ins.then_inc(x_turned, 1)

            chunks_skewed(pe, front, back)
            logits_of(NC - 2, 0)
            logits_of(NC - 1, 1)
            pe.wait_ge(onehot_ready, 1)
            oh = both16[:, :, :].rearrange("p e t -> p (e t)")
            pe.matmul(psc[:, 0, :], keep["before16"][:, :], oh, start=True, stop=True)
            pe.matmul(psc[:, 1, :], keep["ones16"][:, :], oh, start=True, stop=True).then_inc(counted, 1)

        @block.scalar
        def _(act):
            def high_piece(m):
                act.wait_ge(piece_landed[m % EARLY], 16 * (m // EARLY + 1))
                act.copy(pieces[m][1], piece[:, m % EARLY, :]).then_inc(piece_high, 1)

            def take_logits(c):
                act.wait_ge(l_ready, c + 1)
                act.copy(logits[:, :, bass.ds(c * TC, TC)].rearrange("p e t -> p t e"), psl[:, :, :]).then_inc(l_taken, 1)

            def front(c, n, u):
                act.wait_ge(o_turned, c + 1)
                wait(act, s_ready, ago(c))
                act.copy(ot[:, u, 0, :], pst[0][:, :])
                act.copy(ot[:, u, 1, :], pst[1][:, :]).then_inc(ot_ready, 1)
                if not (isinstance(c, int) and c < 2):
                    take_logits(c - 2)
                act.wait_ge(y_landed[u], 16 * TC * (n + 1))
                wait(act, x1_ready, ago(c))
                for t in range(TC):
                    ins = act.activation(silu[:, u, t, :], yin[:, u, t, :], ACT.Silu,
                                         scale=keep["gate"][:, bass.ds(c * TC + t, 1)])
                ins.then_inc(silu_ready, 1)

            def back(c, n, u):
                act.wait_ge(x_turned, c + 1)
                wait(act, xnt_stored[u], 16 * n)
                act.copy(xnt[:, u, 0, :], psx[0][:, :])
                act.copy(xnt[:, u, 1, :], psx[1][:, :]).then_inc(xnt_ready, 1)
                act.wait_ge(xnt_ready, c + 1)
                act.dma_start(dram["xnt1"][:, :, bass.ds(c * CH, CH)].rearrange("k p n -> p k n"), xnt[:, u, :, :]
                              ).then_inc(xnt_stored[u], 16)
                if isinstance(c, int):
                    for m in piece_turns[c]:
                        high_piece(m)

            chunks_skewed(act, front, back)
            take_logits(NC - 2)
            take_logits(NC - 1)
            act.wait_ge(gap_ready, 1)
            act.activation(small["ratio"][:, :], small["gap"][:, :], ACT.Exp).then_inc(ratio_ready, 1)

        @block.vector
        def _(vec):
            ch = Chain(vec, dve_step)

            def front(c, n, u):
                ch.base, ch.k = NORM_STEPS * c, 0
                vec.wait_ge(s_ready, c + 1)
                vec.wait_ge(silu_ready, c + 1)
                vec.wait_ge(in_landed[u], 32 * (n + 1))
                for k in range(2):
                    ins = vec.tensor_tensor(silu[:, u, 2 * k:2 * k + 2, :], pss[k][:, :, :], silu[:, u, 2 * k:2 * k + 2, :],
                                            ALU.mult)
                ins.then_inc(s_taken, 1)
                vec.wait_ge(s_taken, c + 1)
                wait(vec, x1_stored[u], 16 * n)
                vec.tensor_tensor(x1[:, u, :, :], xin[:, u, :, :], silu[:, u, :, :], ALU.add).then_inc(x1_ready, 1)
                vec.wait_ge(x1_ready, c + 1)
                layer_norm(vec, ch, x1[:, u, :, :], xn[:, u, :, :], stats[:, u, :, :], mv[:, u, :, :], var[:, u, :],
                           half[:, u, :], rstd[:, u, :], spare[:, :], lambda: wait(vec, x_turned, ago(c))
                           ).then_inc(xn_ready, 1)

            chunks_skewed(vec, front, lambda c, n, u: None)
            ch.base, ch.k = NORM_STEPS * NC, 0

            vec.wait_ge(l_taken, NC)
            L, s = logits[:, :, :], {n: v[:, :] for n, v in small.items()}
            b = {n: v[:, :, :] for n, v in big.items()}
            first_max(vec, ch, keep, L, s["top0"], b["equal"], s["first0"], b["onehot0"])
            ch.link(vec.scalar_tensor_tensor(out=b["masked"], in0=b["onehot0"], scalar=-3.0e38, in1=L, op0=ALU.mult, op1=ALU.add))
            first_max(vec, ch, keep, b["masked"], s["top1"], b["equal"], s["first1"], b["onehot1"])
            ch.link(vec.tensor_tensor(b["both"], b["onehot0"], b["onehot1"], ALU.add))
            vec.tensor_copy(both16[:, :, :], b["both"]).then_inc(onehot_ready, 1)
            vec.tensor_tensor(s["gap"], s["top1"], s["top0"], ALU.subtract).then_inc(gap_ready, 1)
            vec.wait_ge(ratio_ready, 1)
            ch.link(vec.tensor_scalar(s["den"], s["ratio"], 1.0, None, ALU.add))
            ch.link(vec.reciprocal(s["w0"], s["den"]))
            ch.link(vec.tensor_tensor(s["w1"], s["ratio"], s["w0"], ALU.mult))
            vec.wait_ge(counted, 1)
            places(vec, ch, keep, "running1", psc[:, 0, :], psc[:, 1, :], b["total"], b["scanned"], b["place"])
            ch.link(vec.tensor_scalar(b["fits"], b["place"], float(CAP1), None, ALU.is_lt))
            for w, oh in (("w0", "onehot0"), ("w1", "onehot1")):
                ch.link(vec.tensor_tensor(b[oh], b[oh], s[w].unsqueeze(1).to_broadcast([P, E, NT]), ALU.mult))
            ch.link(vec.tensor_tensor(b["both"], b["onehot0"], b["onehot1"], ALU.add))
            ch.link(vec.tensor_tensor(keep["coef"][:, :, :].rearrange("p t e -> p e t"), b["both"], b["fits"], ALU.mult))


PAIRS = H // 2


def window_steps():
    fillers = {0: [("W", 0)], 1: [("W", 1)], 2: [("W", 2)], 3: [("W", 3), ("QR", 0)],
               4: [("W", 4), ("QR", 1), ("QR", 2), ("KR", 0)], 5: [("W", 5), ("QR", 3), ("QR", 4), ("KR", 1), ("KR", 2)],
               6: [("E", 0), ("QR", 5), ("KR", 3)], 7: [("E", 1), ("KR", 4), ("KR", 5)]}
    steps = []
    for p in range(PAIRS):
        steps.append(("S", p))
        if p >= 1:
            steps.append(("N", p - 1))
        steps += fillers[p]
        if p >= 3:
            steps.append(("T", p - 3))
        if p >= 4:
            steps.append(("PV", p - 4))
    steps += [("N", 7), ("R", 0), ("E", 2), ("T", 5), ("PV", 4), ("R", 1), ("T", 6), ("E", 3), ("PV", 5), ("T", 7), ("R", 2),
              ("PV", 6), ("X",), ("R", 3), ("PV", 7), ("G",), ("OUT",)]
    return steps


def emptier(s):
    if s[0] == "W":
        return "act"
    if s[0] == "E":
        return "dve"
    if s[0] == "T":
        return ("dve", "act")[s[1] % 2]
    return "dve"


class Uses:

    def __init__(self, kinds, ahead, steps):
        self.kinds = kinds
        self.ahead = ahead
        self.every = [s for s in steps if s[0] in kinds]
        assert len(ahead) % 2 == 0 and len(self.every) % 2 == 0

    def emptied(self, who, t):
        return sum(emptier(s) == who for s in self.ahead) + t * sum(emptier(s) == who for s in self.every)

    def filled(self, t):
        return len(self.ahead) + t * len(self.every)

    def within(self, order, n, who=None):
        mine = [s for s in order if s[0] in self.kinds][:n]
        return len([s for s in mine if who is None or emptier(s) == who])

    def index(self, order, step):
        return [s for s in order if s[0] in self.kinds].index(step)


def stage_windows(nc, io, keep, dram, out):
    steps = window_steps()
    ending_steps = [s for s in steps if s[0] != "X"]
    last_steps = [s for s in ending_steps if s[0] not in ("W", "QR", "KR", "R")]
    work = Uses(("W", "E"), [("W", n) for n in range(6)], steps)
    turns = Uses(("T", "R"), [("R", n) for n in range(4)], steps)
    with ExitStack() as ctx:
        st = Stage(nc, ctx, "w_")
        wqkv, we, wout = keep["wqkv"], keep["we"], keep["wout"]
        rope = st.sb("rope", [P, 2, 3, DH // 2])
        own_mask = st.sb("own_mask", [P, P], BF16)
        before_mask = st.sb("before_mask", [P, P], BF16)
        even_masks = st.sb("even_masks", [P, NT // 2, P], BF16)
        xnt = st.sb("xnt", [P, 2, KD, P])
        xr = [st.sb(f"xr{r}", [P, 2, KD, P], F32R) for r in range(2)]
        x1 = st.sb("x1", [P, 2, D])
        raw = st.sb("raw", [P, 3, J])
        rot = st.sb("rot", [P, 2, J])
        crossed = st.sb("crossed", [P, 2, J])
        v = [st.sb(f"v{u}", [P, J]) for u in range(2)]
        kd = [[st.sb(f"kd{u}_{r}", [P, PAIRS, 2, P], F32R) for r in range(2)] for u in range(2)]
        qt = [st.sb(f"qt{r}", [P, PAIRS, P], F32R) for r in range(2)]
        top = st.sb("top", [P, 2, PAIRS])
        rows = st.sb("rows", [P, 2, PAIRS])
        inv = st.sb("inv", [P, 2, PAIRS])
        probs = st.sb("probs", [P, 4, 2, 2 * P])
        pt = st.sb("pt", [P, 2, 4, P])
        ot = st.sb("ot", [P, PAIRS, P])
        y = st.sb("y", [P, D])
        sig = st.sb("sig", [P, D])
        res = st.sb("res", [P, 2, D])
        psw = [st.ps(f"psw{k}", [P, CH]) for k in range(2)]
        pss = [st.ps(f"pss{k}", [P, 2, 2 * P]) for k in range(2)]
        pst = [st.ps(f"pst{k}", [P, 4, P]) for k in range(2)]
        pso = st.ps("pso", [P, 4, P])
        psy = st.ps("psy", [P, D])

        pool_set = st.sem("pool_set")
        x_high, x_ready, turn_high = st.sem("x_high"), st.sem("x_ready"), st.sem("turn_high")
        rope_landed = [st.sem(f"rope_landed{u}") for u in range(2)]
        xt_landed = [st.sem(f"xt_landed{u}") for u in range(2)]
        x1_landed = [st.sem(f"x1_landed{u}") for u in range(2)]
        work_ready, s_ready, t_ready = st.sem("work_ready"), st.sem("s_ready"), st.sem("t_ready")
        work_taken = {w: st.sem("work_taken_" + w) for w in ("act", "dve")}
        turn_taken = {w: st.sem("turn_taken_" + w) for w in ("act", "dve")}
        top_ready, exp_ready, inv_ready, p_ready = (st.sem("top_ready"), st.sem("exp_ready"), st.sem("inv_ready"),
                                                    st.sem("p_ready"))
        pv_done, ot_ready, y_ready, out_ready = st.sem("pv_done"), st.sem("ot_ready"), st.sem("y_ready"), st.sem("out_ready")
        q_rotated, k_rotated, v_moved = st.sem("q_rotated"), st.sem("k_rotated"), st.sem("v_moved")
        sig_ready, res_step = st.sem("sig_ready"), st.sem("res_step")
        stored = [st.sem(f"stored{u}") for u in range(2)]
        dve_step, pool_step = st.sem("dve_step"), st.sem("pool_step")
        keys_cleared = st.sem("keys_cleared")
        block = ctx.enter_context(nc.Block())
        out_rows = out.rearrange("b s d -> (b s) d")

        def tiles(eng):
            for i in rounds(eng, NT // 2 - 1):
                for u in range(2):
                    yield 2 * i + u, u, i, steps
            yield NT - 2, 0, NT // 2 - 1, ending_steps
            yield NT - 1, 1, NT // 2 - 1, last_steps

        def heads(ap):
            return ap.rearrange("p (h s x) -> p h s x", s=2, x=DH // 2)

        wide = [P, H, DH // 2]

        def rotary(eng, r, n, table):
            src = raw[:, r, :]
            cos, sin, minus_sin = (rope[:, table, k, :] for k in range(3))
            if n < 2:
                return eng.tensor_tensor(heads(crossed[:, r, :])[:, :, n, :], heads(src)[:, :, 1 - n, :],
                                         (minus_sin, sin)[n].unsqueeze(1).to_broadcast(wide), ALU.mult)
            half = slice((n % 2) * J // 2, (n % 2 + 1) * J // 2)
            if n < 4:
                return eng.tensor_tensor(rot[:, r, half].rearrange("p (h x) -> p h x", x=DH // 2),
                                         src[:, half].rearrange("p (h x) -> p h x", x=DH // 2),
                                         cos.unsqueeze(1).to_broadcast([P, H, DH // 2]), ALU.mult)
            return eng.tensor_tensor(rot[:, r, half], rot[:, r, half], crossed[:, r, half], ALU.add)

        @block.sync
        def _(sp):
            def load_x(at, u):
                sp.dma_start(xnt[:, u, :, :], dram["xnt1"][:, :, bass.ds(at, P)].rearrange("k p n -> p k n")
                             ).then_inc(xt_landed[u], 16)

            def load_rope(at, u):
                sp.dma_start(rope[:, u, :, :], io["rope"][bass.ds(at, P), :, :]).then_inc(rope_landed[u], 16)

            for u in range(2):
                load_x(u * P, u)
                load_rope(u * P, u)
            for t, u, i, order in tiles(sp):
                at = snap(sp, t * P)
                if not (isinstance(t, int) and t >= NT - 2):
                    ahead = snap(sp, (t + 2) * P)
                    sp.wait_ge(x_ready, t + 1)
                    load_x(ahead, u)
                    sp.wait_ge(q_rotated, t + 1)
                    sp.wait_ge(k_rotated, t + 1)
                    load_rope(ahead, u)
                sp.wait_ge(out_ready, t + 1)
                sp.dma_start(out_rows[bass.ds(at, P), :], res[:, u, :]).then_inc(stored[u], 16)
            for u in range(2):
                sp.wait_ge(stored[u], 16 * (NT // 2))

        @block.gpsimd
        def _(pool):
            ch = Chain(pool, pool_step)
            def low_rows(tile, u):
                pool.wait_ge(x_high, tile + 1)
                pool.tensor_tensor(xr[1][:, u, :, :], xnt[:, u, :, :], xr[0][:, u, :, :].bitcast(F32), ALU.subtract
                                   ).then_inc(x_ready, 1)

            def rotate(n, t, taken, table, landed):
                if n == 0:
                    pool.wait_ge(rope_landed[table], landed)
                    wait(pool, work_taken["act"], taken)
                    wait(pool, t_ready, turns.filled(t))
                    wait(pool, k_rotated, t + 1)
                ins = rotary(pool, 1, n, table)
                if n < 5:
                    ch.link(ins)
                else:
                    ins.then_inc(k_rotated, 1)

            low_rows(0, 0)
            ch.link(pool.memset(own_mask[:, :], 0.0))
            ch.link(pool.affine_select(out=own_mask[:, :], in_=own_mask[:, :], compare_op=ALU.is_ge, fill=NEG, base=0,
                                       pattern=[[-1, P]], channel_multiplier=1))
            for mask in (before_mask[:, :].unsqueeze(1), even_masks[:, :, :]):
                ch.link(pool.memset(mask, 0.0))
                ch.link(pool.affine_select(out=mask, in_=mask, compare_op=ALU.is_ge, fill=NEG, base=0,
                                           pattern=[[0, mask.shape[1]], [1, P]], channel_multiplier=-1))
            for b in range(B):
                ch.link(pool.memset(even_masks[:, b * NT // B // 2, :], NEG))
            pool.memset(v[1][:, :], 0.0).then_inc(pool_set, 1)

            low_rows(1, 1)
            pool.wait_ge(pool_set, 1)
            for n in range(6):
                rotate(n, -1, 4, 0, 16)
            start = ch.k
            for t, u, i, order in tiles(pool):
                ch.base, ch.k = start + t * 5, 0
                for s in order:
                    if s[0] == "N":
                        p = s[1]
                        wait(pool, inv_ready, PAIRS * t + p + 1)
                        pool.tensor_tensor(probs[:, p % 4, :, :], probs[:, p % 4, :, :],
                                           inv[:, :, p:p + 1].to_broadcast([P, 2, 2 * P]), ALU.mult).then_inc(p_ready, 1)
                    elif s[0] == "KR":
                        rotate(s[1], t, work.emptied("act", t) + 4, 1 - u, 16 * (i + 1 + u))
                    elif s[0] == "X":
                        low_rows(t + 2, u)

        @block.tensor
        def _(pe):
            def bank_free(use, taken, order, t, n):
                if n < 2:
                    for who in ("act", "dve"):
                        wait(pe, taken[who], use.emptied(who, t))
                else:
                    before = [s for s in order if s[0] in use.kinds][n - 2]
                    who = emptier(before)
                    wait(pe, taken[who], use.emptied(who, t) + use.within(order, n - 1, who))

            def widths(bank, src, moving):
                pairs = [(k, a, b) for k in range(KD) for a, b in PARTS]
                for m, (k, a, b) in enumerate(pairs):
                    ins = pe.matmul(psw[bank][:, :], xr[a][:, src, k, :], moving(b, k),
                                    start=(m == 0), stop=(m == len(pairs) - 1))
                return ins

            def project(n, bank, src):
                widths(bank, src, lambda r, k: wqkv[r][:, k, n * CH:(n + 1) * CH]).then_inc(work_ready, 1)

            def turn(n, bank, tile):
                pe.wait_ge(q_rotated if n < 2 else k_rotated, tile + 1)
                for j in range(4):
                    pair = 4 * (n % 2) + j
                    ins = pe.transpose(pst[bank][:, j, :], rot[:, n // 2, pair * P:(pair + 1) * P], keep["identity"][:, :])
                ins.then_inc(t_ready, 1)

            pe.wait_ge(x_ready, 1)
            for n in range(6):
                wait(pe, work_taken["act"], n - 1)
                project(n, n % 2, 0)
            for n in range(4):
                if n >= 2:
                    pe.wait_ge(turn_taken["dve"], n - 1)
                turn(n, n % 2, 0)
            pe.wait_ge(pool_set, 1)
            for t, u, i, order in tiles(pe):
                w = r = 0
                for s in order:
                    if s[0] == "S":
                        p = s[1]
                        if p == 0:
                            for who in ("act", "dve"):
                                wait(pe, turn_taken[who], turns.emptied(who, t))
                        wait(pe, exp_ready, PAIRS * t + max(p - 1, 0))
                        mask = (even_masks[:, bass.ds(i, 1), :], before_mask[:, :].unsqueeze(1))[u]
                        for role, (mask, keys) in enumerate(((mask, kd[1 - u]), (own_mask[:, :].unsqueeze(1), kd[u]))):
                            scores = pss[p % 2][:, :, role * P:(role + 1) * P]
                            pe.matmul(scores, keep["identity16"][:, :], mask.to_broadcast([P, 2, P]), start=True, stop=False)
                            for a, b in PARTS:
                                ins = pe.matmul(scores, qt[a][:, p, :], keys[b][:, p, :, :], start=False,
                                                stop=(a, b) == PARTS[-1])
                        ins.then_inc(s_ready, 1)
                    elif s[0] == "W":
                        bank_free(work, work_taken, order, t, w)
                        if s[1] == 0:
                            pe.wait_ge(x_ready, t + 2)
                        project(s[1], w % 2, 1 - u)
                        w += 1
                    elif s[0] == "E":
                        bank_free(work, work_taken, order, t, w)
                        widths(w % 2, u, lambda r, k: we[r][:, k, 2 * s[1]:2 * s[1] + 2, :]).then_inc(work_ready, 1)
                        w += 1
                    elif s[0] == "T":
                        p = s[1]
                        wait(pe, p_ready, PAIRS * t + p + 1)
                        bank_free(turns, turn_taken, order, t, r)
                        for e in range(2):
                            for role in range(2):
                                ins = pe.transpose(pst[r % 2][:, 2 * e + role, :], probs[:, p % 4, e, role * P:(role + 1) * P],
                                                   keep["identity"][:, :])
                        ins.then_inc(t_ready, 1)
                        r += 1
                    elif s[0] == "R":
                        bank_free(turns, turn_taken, order, t, r)
                        turn(s[1], r % 2, t + 1)
                        r += 1
                    elif s[0] == "PV":
                        p = s[1]
                        n = turns.index(order, ("T", p))
                        who = emptier(("T", p))
                        wait(pe, turn_taken[who], turns.emptied(who, t) + turns.within(order, n + 1, who))
                        if p == 0:
                            pe.wait_ge(v_moved, t + 1)
                            wait(pe, ot_ready, 2 * t)
                        if p == 4:
                            wait(pe, ot_ready, 2 * t + 1)
                        for role in range(2):
                            for e in range(2):
                                h = 2 * p + e
                                ins = pe.matmul(pso[e * DH:(e + 1) * DH, p % 4, :], v[(u + 1 + role) % 2][:, h * DH:(h + 1) * DH],
                                                pt[:, p % 2, 2 * e + role, :], start=(role == 0), stop=(role == 1))
                        ins.then_inc(pv_done, 1)
                    elif s[0] == "OUT":
                        wait(pe, out_ready, t)
                        for p in range(PAIRS):
                            if p % 4 == 0:
                                wait(pe, ot_ready, 2 * t + p // 4 + 1)
                            ins = pe.matmul(psy[:, :], ot[:, p, :], wout[:, p, :], start=(p == 0), stop=(p == PAIRS - 1))
                        ins.then_inc(y_ready, 1)

        @block.scalar
        def _(act):
            def take_work(n, t, filled, bank):
                act.wait_ge(work_ready, filled)
                wait(act, (q_rotated, k_rotated, v_moved)[n // 2], t + 1)
                act.activation(raw[:, n // 2, (n % 2) * CH:(n % 2 + 1) * CH], psw[bank][:, :], ACT.Copy,
                               scale=DH ** -0.5 if n < 2 else 1.0).then_inc(work_taken["act"], 1)

            def high_turned(n, t, filled, bank, into):
                wait(act, t_ready, filled)
                wait(act, s_ready, PAIRS * (t + 1))
                four = slice(4 * (n % 2), 4 * (n % 2) + 4)
                if n < 2:
                    ins = act.copy(qt[0][:, four, :], pst[bank][:, :, :])
                else:
                    for e in range(2):
                        head = slice(e * DH, (e + 1) * DH)
                        ins = act.copy(kd[into][0][head, four, e, :], pst[bank][head, :, :])
                ins.then_inc(turn_high, 1)

            def high_rows(tile, u, landed):
                act.wait_ge(xt_landed[u], landed)
                act.copy(xr[0][:, u, :, :], xnt[:, u, :, :]).then_inc(x_high, 1)

            for u in range(2):
                high_rows(u, u, 16)
            for n in range(6):
                take_work(n, -1, n + 1, n % 2)
            act.wait_ge(keys_cleared, 1)
            for n in range(4):
                high_turned(n, -1, n + 1, n % 2, 0)
            act.wait_ge(pool_set, 1)
            for t, u, i, order in tiles(act):
                wait(act, out_ready, t - 1)
                act.dma_start(x1[:, u, :], dram["x1"][bass.ds(t * P, P), :]).then_inc(x1_landed[u], 16)
                w = r = 0
                for s in order:
                    if s[0] == "S":
                        p = s[1]
                        if p == 0:
                            wait(act, inv_ready, PAIRS * t)
                        act.wait_ge(top_ready, PAIRS * t + p + 1)
                        wait(act, t_ready, turns.filled(t) + (turns.index(order, ("T", p - 4)) + 1 if p >= 4 else 0))
                        for e in range(2):
                            ins = act.activation(probs[:, p % 4, e, :], pss[p % 2][:, e, :], ACT.Exp, bias=top[:, e, p:p + 1],
                                                 accum_out=rows[:, e, p:p + 1])
                        ins.then_inc(exp_ready, 1)
                        if p == 1:
                            wait(act, pv_done, PAIRS * t)
                            wait(act, work_taken["act"], work.emptied("act", t))
                            act.copy(v[u][:, :], raw[:, 2, :]).then_inc(v_moved, 1)
                    elif s[0] == "W":
                        take_work(s[1], t, work.filled(t) + w + 1, w % 2)
                        w += 1
                    elif s[0] == "E":
                        w += 1
                    elif s[0] in ("T", "R"):
                        if s[0] == "T" and emptier(s) == "act":
                            wait(act, t_ready, turns.filled(t) + r + 1)
                            wait(act, pv_done, PAIRS * t + max(s[1] - 1, 0))
                            act.copy(pt[:, s[1] % 2, :, :], pst[r % 2][:, :, :]).then_inc(turn_taken["act"], 1)
                        elif s[0] == "R":
                            high_turned(s[1], t, turns.filled(t) + r + 1, r % 2, 1 - u)
                        r += 1
                    elif s[0] == "X":
                        act.wait_ge(work_ready, work.filled(t + 1))
                        high_rows(t + 2, u, 16 * (i + 2))
                    elif s[0] == "PV" and s[1] % 4 == 3:
                        half = s[1] // 4
                        wait(act, pv_done, PAIRS * t + s[1] + 1)
                        if half == 0:
                            wait(act, y_ready, t)
                        act.copy(ot[:, 4 * half:4 * half + 4, :], pso[:, :, :]).then_inc(ot_ready, 1)
                    elif s[0] == "G":
                        act.wait_ge(work_taken["dve"], work.emptied("dve", t + 1))
                        wait(act, out_ready, t)
                        act.activation(sig[:, :], y[:, :], ACT.Exp, scale=-1.0).then_inc(sig_ready, 1)

        @block.vector
        def _(vec):
            ch = Chain(vec, dve_step)
            for u in range(2):
                for r in range(2):
                    for two in range(0, PAIRS, 2):
                        ins = vec.tensor_copy(kd[u][r][:, two:two + 2, :, :], keep["zero"][:, :])
            ins.then_inc(keys_cleared, 1)
            vec.wait_ge(keys_cleared, 1)

            def rotate(n, t, taken, table, landed):
                if n == 0:
                    vec.wait_ge(rope_landed[table], landed)
                    wait(vec, work_taken["act"], taken)
                    wait(vec, t_ready, turns.filled(t))
                    wait(vec, q_rotated, t + 1)
                ins = rotary(vec, 0, n, table)
                if n < 5:
                    ch.link(ins)
                else:
                    ins.then_inc(q_rotated, 1)

            def low_turned(n, t, count, bank, into):
                wait(vec, turn_high, count)
                four = slice(4 * (n % 2), 4 * (n % 2) + 4)
                if n < 2:
                    ins = vec.tensor_tensor(qt[1][:, four, :], pst[bank][:, :, :], qt[0][:, four, :].bitcast(F32), ALU.subtract)
                else:
                    for e in range(2):
                        head = slice(e * DH, (e + 1) * DH)
                        ins = vec.tensor_tensor(kd[into][1][head, four, e, :], pst[bank][head, :, :],
                                                kd[into][0][head, four, e, :].bitcast(F32), ALU.subtract)
                ins.then_inc(turn_taken["dve"], 1)

            for n in range(6):
                rotate(n, -1, 2, 0, 16)
            for n in range(4):
                low_turned(n, -1, n + 1, n % 2, 0)
            start = ch.k
            per_tile = 5 + 4 + 3
            for t, u, i, order in tiles(vec):
                ch.base, ch.k = start + t * per_tile, 0
                w = r = 0
                for s in order:
                    if s[0] == "S":
                        p = s[1]
                        vec.wait_ge(s_ready, PAIRS * t + p + 1)
                        vec.tensor_reduce(top[:, :, p], pss[p % 2][:, :, :], X, ALU.max, negate=True).then_inc(top_ready, 1)
                    elif s[0] == "N":
                        p = s[1]
                        if p == 0:
                            wait(vec, p_ready, PAIRS * t)
                        wait(vec, exp_ready, PAIRS * t + p + 1)
                        vec.reciprocal(inv[:, :, p], rows[:, :, p]).then_inc(inv_ready, 1)
                    elif s[0] == "QR":
                        rotate(s[1], t, work.emptied("act", t) + 2, 1 - u, 16 * (i + 1 + u))
                    elif s[0] == "W":
                        w += 1
                    elif s[0] == "E":
                        n = s[1]
                        vec.wait_ge(work_ready, work.filled(t) + w + 1)
                        if n == 0:
                            wait(vec, out_ready, t)
                        for e in range(2):
                            weight = keep["coef"][:, bass.ds(t, 1), 2 * n + e:2 * n + e + 1].rearrange("p t e -> p (t e)")
                            part = psw[w % 2][:, e * D:(e + 1) * D]
                            if n == 0 and e == 0:
                                ins = vec.tensor_scalar(y[:, :], part, weight, None, ALU.mult)
                            else:
                                ins = vec.scalar_tensor_tensor(out=y[:, :], in0=part, scalar=weight, in1=y[:, :],
                                                               op0=ALU.mult, op1=ALU.add)
                            if e == 0:
                                ch.link(ins)
                        ins.then_inc(work_taken["dve"], 1)
                        w += 1
                        vec.wait_ge(work_taken["dve"], work.emptied("dve", t) + n + 1)
                    elif s[0] in ("T", "R"):
                        if s[0] == "T" and emptier(s) == "dve":
                            wait(vec, t_ready, turns.filled(t) + r + 1)
                            wait(vec, pv_done, PAIRS * t + max(s[1] - 1, 0))
                            vec.tensor_copy(pt[:, s[1] % 2, :, :], pst[r % 2][:, :, :]).then_inc(turn_taken["dve"], 1)
                        elif s[0] == "R":
                            low_turned(s[1], t, 4 * (t + 1) + s[1] + 1, r % 2, 1 - u)
                        r += 1
                    elif s[0] == "G":
                        vec.wait_ge(sig_ready, t + 1)
                        ch.link(vec.tensor_scalar(sig[:, :], sig[:, :], 1.0, None, ALU.add))
                        ch.link(vec.reciprocal(sig[:, :], sig[:, :]))
                        ch.link(vec.tensor_tensor(sig[:, :], sig[:, :], y[:, :], ALU.mult))
                    elif s[0] == "OUT":
                        wait(vec, y_ready, t + 1)
                        wait(vec, stored[u], 16 * i)
                        ins = vec.tensor_tensor(res[:, u, :], psy[:, :], sig[:, :], ALU.mult)
                        ins.then_inc(res_step, 1)
                        vec.wait_ge(res_step, t + 1)
                        vec.wait_ge(x1_landed[u], 16 * (i + 1))
                        vec.tensor_tensor(res[:, u, :], res[:, u, :], x1[:, u, :], ALU.add).then_inc(out_ready, 1)


def make_program(nc, io, out, upto=7):
    dram = {
        "qk_parts": nc.dram_tensor("qk_parts", [2, 3, D, T], BF16).ap(),
        "v": nc.dram_tensor("v_rows", [T, D], F32).ap(),
        "expert_in": nc.dram_tensor("expert_in", [E * CAP0, D], F32).ap(),
        "expert_out": nc.dram_tensor("expert_out", [E * CAP0, D], F32).ap(),
        "attn0": nc.dram_tensor("attn0", [T, D], F32).ap(),
        "xnt1": nc.dram_tensor("xnt1", [KD, P, T], F32).ap(),
        "x1": nc.dram_tensor("x1", [T, D], F32).ap(),
    }
    with ExitStack() as ctx:
        st = Stage(nc, ctx)
        keep = {
            "identity": st.sb("identity", [P, P]),
            "identity16": st.sb("identity16", [P, P], BF16),
            "ones16": st.sb("ones16", [P, P], BF16),
            "zero16": st.sb("zero16", [P, P], BF16),
            "before16": st.sb("before16", [P, P], BF16),
            "mask_qk": st.sb("mask_qk", [P, P], BF16),
            "mask_kq": st.sb("mask_kq", [P, P], BF16),
            "expert": st.sb("expert", [P, E, NT]),
            "expert8": st.sb("expert8", [P, E, NT]),
            "running0": st.sb("running0", [P, E, NT]),
            "running1": st.sb("running1", [P, E, NT]),
            "gate": st.sb("gate", [P, NT]),
            "slot_get": st.sb("slot_get", [P, NT], U32),
            "slot_put": st.sb("slot_put", [P, NT], U32),
            "zero": st.sb("zero", [P, CH]),
            "coef": st.sb("coef", [P, NT, E]),
        }
        build_constants(nc, keep)
        with ExitStack() as front:
            keep["xn_all"] = Stage(nc, front).sb("xn_all", [P, NT, D])
            stage_project(nc, io, keep, dram)
            if upto >= 3:
                stage_attention(nc, io, keep, dram)
        if upto >= 4:
            stage_experts(nc, io, keep, dram)
        keep["wqkv"] = [st.sb(f"wqkv{r}", [P, KD, 3 * J], F32R) for r in range(2)]
        keep["we"] = [st.sb(f"we{r}", [P, KD, E, D], F32R) for r in range(2)]
        keep["wout"] = st.sb("wout", [P, PAIRS, D])
        if upto >= 5:
            stage_join(nc, io, keep, dram)
        if upto >= 7:
            stage_windows(nc, io, keep, dram, out)
    return dram


def declare(nc, inputs):
    import numpy as np

    def turned(a):
        return np.ascontiguousarray(np.asarray(a).T)

    arrays = {
        "x": np.ascontiguousarray(inputs["L0_attn_x"]),
        "wq": turned(inputs["L0_attn_Wq"]), "wk": turned(inputs["L0_attn_Wk"]), "wv": turned(inputs["L0_attn_Wv"]),
        "wo": turned(inputs["L0_attn_Wo"]), "router0": np.ascontiguousarray(inputs["L0_ffn_router_w"]),
        "w1": np.ascontiguousarray(inputs["L0_ffn_w1"]), "w2": np.ascontiguousarray(inputs["L0_ffn_w2"]),
        "w_qkv": np.ascontiguousarray(inputs["L1_attn_W_qkv"]), "w_out": np.ascontiguousarray(inputs["L1_attn_W_out"]),
        "router1": turned(inputs["L1_ffn_Wr"]), "we": np.ascontiguousarray(inputs["L1_ffn_We"]),
    }
    arrays.update(tables())
    named = {f"in_{k}": v for k, v in arrays.items()}
    io = {k: nc.dram_tensor(f"in_{k}", list(v.shape), mybir.dt.from_np(v.dtype), kind="ExternalInput").ap()
          for k, v in arrays.items()}
    out = nc.dram_tensor("out_0", [B, S, D], F32, kind="ExternalOutput").ap()
    return named, io, out


def tables():
    import numpy as np

    inv_freq = (1.0 / np.power(np.float32(10000.0), np.arange(0, DH, 2, dtype=np.float32) / np.float32(DH))).astype(np.float32)
    angles = (np.arange(T) % S)[:, None] * inv_freq.astype(np.float64)[None, :]
    cos, sin = np.cos(angles), np.sin(angles)
    return {"rope": np.stack([cos, sin, -sin], 1).astype(np.float32)}


def kernel(**inputs):
    import concourse.bacc as bacc
    from concourse.bass_utils import run_bass_kernel_spmd

    nc = bacc.Bacc("TRN2", target_bir_lowering=False, num_devices=1)
    arrays, io, out = declare(nc, inputs)
    make_program(nc, io, out)
    r = run_bass_kernel_spmd(nc, [arrays], core_ids=[0])
    return r.results[0]["out_0"]
```
